# Optimizing a Trainium2 kernel written in Bass

```python
import numpy as np
import jax
import jax.numpy as jnp

def _softmax(x, axis=-1):
    return jax.nn.softmax(x, axis=axis)

def _gelu(x):
    return jax.nn.gelu(x, approximate=True)

def _silu(x):
    return jax.nn.silu(x)

def _sigmoid(x):
    return jax.nn.sigmoid(x)

def _layernorm(x, axis=-1, eps=1e-05):
    m = jnp.mean(x, axis=axis, keepdims=True)
    v = jnp.var(x, axis=axis, keepdims=True)
    return (x - m) / jnp.sqrt(v + eps)

def _scatter_add(tgt, idx, src, axis=0):
    return tgt.at[idx].add(src)

def _segment_sum(src, seg, n):
    return jax.ops.segment_sum(src, seg, n)
kernel_name = 'mk_hybrid_d2_jaxref_r8_f27fef'

def setup_inputs(seed: int=0):
    np.random.seed(seed)
    _w = jnp.asarray

    def _L0_attn_a_setup():
        import jax, jax.numpy as jnp
        import numpy as np
        HIDDEN = 128
        N_HEADS = 16
        HEAD_DIM = HIDDEN // N_HEADS
        WINDOW = 32
        HALF_W = WINDOW // 2
        GLOBAL_TOKENS = (0,)

        def _longformer_mask(seq_len: int) -> jnp.ndarray:
            idx = jnp.arange(seq_len)
            mask = jnp.abs(idx[:, None] - idx[None, :]) <= HALF_W
            for g in GLOBAL_TOKENS:
                if 0 <= g < seq_len:
                    mask = mask.at[g, :].set(True)
                    mask = mask.at[:, g].set(True)
            return mask
        key = jax.random.key(seed)
        ks = jax.random.split(key, 5)
        B, S = (1, 512)
        scale = 0.02
        return {'x': jax.random.normal(ks[0], (B, S, HIDDEN), dtype=jnp.float32), 'Wq': jax.random.normal(ks[1], (HIDDEN, HIDDEN), dtype=jnp.float32) * scale, 'Wk': jax.random.normal(ks[2], (HIDDEN, HIDDEN), dtype=jnp.float32) * scale, 'Wv': jax.random.normal(ks[3], (HIDDEN, HIDDEN), dtype=jnp.float32) * scale, 'Wo': jax.random.normal(ks[4], (HIDDEN, HIDDEN), dtype=jnp.float32) * scale}
    _L0_attn_a_in = _L0_attn_a_setup()

    def _L0_attn_b_setup():
        import jax, jax.numpy as jnp
        import numpy as np
        B, S, D, Hd = (4, 512, 128, 128)

        def _linear_scan(a, x, reverse):

            def comb(l, r):
                al, bl = l
                ar, br = r
                return (al * ar, bl * ar + br)
            _, h = jax.lax.associative_scan(comb, (a, x), axis=1, reverse=reverse)
            return h

        def _rglru(x, a_logit, Wx, bx, Wgx, bgx, Wga, bga, Wo, bo, reverse):
            a_expit = jax.nn.sigmoid(a_logit)
            x = x @ Wx + bx
            gate_x = jax.nn.sigmoid(x @ Wgx + bgx)
            gate_a = jax.nn.sigmoid(x @ Wga + bga)
            a = gate_a * a_expit
            xin = jnp.sqrt(1.0 - a * a) * (gate_x * x)
            h = _linear_scan(a, xin, reverse)
            return h @ Wo + bo
        key = jax.random.key(seed)
        ks = jax.random.split(key, 24)
        f32 = jnp.float32

        def w(k, fan_in, shape):
            return (jax.random.normal(k, shape) / np.sqrt(fan_in)).astype(f32)

        def a_init(k):
            u = jax.random.uniform(k, (Hd,), minval=0.9, maxval=0.999)
            return (jnp.log(u) - jnp.log1p(-u)).astype(f32)
        inp = {'x': jax.random.normal(ks[0], (B, S, D), dtype=f32)}
        for i, pfx in enumerate(['fwd', 'bwd']):
            o = 1 + i * 10
            inp[f'{pfx}_a_logit'] = a_init(ks[o])
            inp[f'{pfx}_Wx'] = w(ks[o + 1], D, (D, Hd))
            inp[f'{pfx}_bx'] = jnp.zeros((Hd,), f32)
            inp[f'{pfx}_Wgx'] = w(ks[o + 2], Hd, (Hd, Hd))
            inp[f'{pfx}_bgx'] = jnp.zeros((Hd,), f32)
            inp[f'{pfx}_Wga'] = w(ks[o + 3], Hd, (Hd, Hd))
            inp[f'{pfx}_bga'] = jnp.zeros((Hd,), f32)
            inp[f'{pfx}_Wo'] = w(ks[o + 4], Hd, (Hd, D))
            inp[f'{pfx}_bo'] = jnp.zeros((D,), f32)
        inp['ld_W'] = w(ks[22], D, (D, D))
        inp['ld_b'] = jnp.zeros((D,), f32)
        return inp
    _L0_attn_b_in = _L0_attn_b_setup()

    def _L0_ffn_setup():
        import jax, jax.numpy as jnp
        import numpy as np
        THRESH_FACTOR = 0.7

        def ternary_quantize(w):
            delta = THRESH_FACTOR * jnp.mean(jnp.abs(w))
            return jnp.where(w > delta, 1.0, jnp.where(w < -delta, -1.0, 0.0)).astype(w.dtype)
        key = jax.random.key(seed)
        k1, k2, k3 = jax.random.split(key, 3)
        B, S, D_IN, D_OUT = (8, 512, 128, 128)
        inp = {'input': jax.random.normal(k1, (B, S, D_IN), dtype=jnp.float32), 'weight': jax.random.normal(k2, (D_OUT, D_IN), dtype=jnp.float32) * (1.0 / np.sqrt(D_IN)), 'alpha': jnp.ones((1,), dtype=jnp.float32), 'bias': jax.random.normal(k3, (D_OUT,), dtype=jnp.float32) * (1.0 / np.sqrt(D_IN))}
        return inp
    _L0_ffn_in = _L0_ffn_setup()

    def _L1_attn_a_setup():
        import jax, jax.numpy as jnp
        import numpy as np
        D_MODEL = 128
        NUM_HEADS = 16
        HEAD_DIM = D_MODEL // NUM_HEADS
        EPS = 1e-08
        key = jax.random.key(seed)
        ks = jax.random.split(key, 6)
        B, T = (4, 256)
        s = 0.02
        return {'x': jax.random.normal(ks[0], (B, T, D_MODEL), dtype=jnp.float32), 'Wq': jax.random.normal(ks[1], (D_MODEL, D_MODEL), dtype=jnp.float32) * s, 'Wk': jax.random.normal(ks[2], (D_MODEL, D_MODEL), dtype=jnp.float32) * s, 'Wv': jax.random.normal(ks[3], (D_MODEL, D_MODEL), dtype=jnp.float32) * s, 'Wo': jax.random.normal(ks[4], (D_MODEL, D_MODEL), dtype=jnp.float32) * s, 'bo': jnp.zeros((D_MODEL,), dtype=jnp.float32)}
    _L1_attn_a_in = _L1_attn_a_setup()

    def _L1_attn_b_setup():
        import jax, jax.numpy as jnp
        import numpy as np
        N_HEADS = 16
        INPUT_DIM = 128
        EMBED_DIM = 128
        KEY_DIM = EMBED_DIM // N_HEADS
        BATCH = 4
        SEQ = 256

        def _uniform(key, shape, bound):
            return jax.random.uniform(key, shape, jnp.float32, -bound, bound)
        key = jax.random.key(seed)
        kq, k1, k2, k3, k4 = jax.random.split(key, 5)
        stdv_k = 1.0 / np.sqrt(KEY_DIM)
        stdv_e = 1.0 / np.sqrt(EMBED_DIM)
        return {'q': jax.random.normal(kq, (BATCH, SEQ, INPUT_DIM), jnp.float32), 'W_query': _uniform(k1, (N_HEADS, INPUT_DIM, KEY_DIM), stdv_k), 'W_key': _uniform(k2, (N_HEADS, INPUT_DIM, KEY_DIM), stdv_k), 'W_val': _uniform(k3, (N_HEADS, INPUT_DIM, KEY_DIM), stdv_k), 'W_out': _uniform(k4, (N_HEADS, KEY_DIM, EMBED_DIM), stdv_e)}
    _L1_attn_b_in = _L1_attn_b_setup()

    def _L1_ffn_setup():
        import jax, jax.numpy as jnp
        import numpy as np
        B, S, D = (4, 256, 128)
        E = 8
        CF = 1
        key = jax.random.key(seed)
        k_x, k_g, k_w, k_b = jax.random.split(key, 4)
        x = jax.random.normal(k_x, (B, S, D), dtype=jnp.float32)
        Wg = jax.random.normal(k_g, (D, E), dtype=jnp.float32) * (1.0 / np.sqrt(D))
        We = jax.random.normal(k_w, (D, D), dtype=jnp.float32) * (1.0 / np.sqrt(D))
        be = jax.random.normal(k_b, (D,), dtype=jnp.float32) * 0.01
        return {'x': x, 'Wg': Wg, 'We': We, 'be': be}
    _L1_ffn_in = _L1_ffn_setup()
    _d = {'L0_attn_a_x': _L0_attn_a_in['x'], 'L0_attn_a_Wq': _L0_attn_a_in['Wq'], 'L0_attn_a_Wk': _L0_attn_a_in['Wk'], 'L0_attn_a_Wv': _L0_attn_a_in['Wv'], 'L0_attn_a_Wo': _L0_attn_a_in['Wo'], 'L0_attn_b_fwd_a_logit': _L0_attn_b_in['fwd_a_logit'], 'L0_attn_b_fwd_Wx': _L0_attn_b_in['fwd_Wx'], 'L0_attn_b_fwd_bx': _L0_attn_b_in['fwd_bx'], 'L0_attn_b_fwd_Wgx': _L0_attn_b_in['fwd_Wgx'], 'L0_attn_b_fwd_bgx': _L0_attn_b_in['fwd_bgx'], 'L0_attn_b_fwd_Wga': _L0_attn_b_in['fwd_Wga'], 'L0_attn_b_fwd_bga': _L0_attn_b_in['fwd_bga'], 'L0_attn_b_fwd_Wo': _L0_attn_b_in['fwd_Wo'], 'L0_attn_b_fwd_bo': _L0_attn_b_in['fwd_bo'], 'L0_attn_b_bwd_a_logit': _L0_attn_b_in['bwd_a_logit'], 'L0_attn_b_bwd_Wx': _L0_attn_b_in['bwd_Wx'], 'L0_attn_b_bwd_bx': _L0_attn_b_in['bwd_bx'], 'L0_attn_b_bwd_Wgx': _L0_attn_b_in['bwd_Wgx'], 'L0_attn_b_bwd_bgx': _L0_attn_b_in['bwd_bgx'], 'L0_attn_b_bwd_Wga': _L0_attn_b_in['bwd_Wga'], 'L0_attn_b_bwd_bga': _L0_attn_b_in['bwd_bga'], 'L0_attn_b_bwd_Wo': _L0_attn_b_in['bwd_Wo'], 'L0_attn_b_bwd_bo': _L0_attn_b_in['bwd_bo'], 'L0_attn_b_ld_W': _L0_attn_b_in['ld_W'], 'L0_attn_b_ld_b': _L0_attn_b_in['ld_b'], 'L0_ffn_weight': _L0_ffn_in['weight'], 'L0_ffn_alpha': _L0_ffn_in['alpha'], 'L0_ffn_bias': _L0_ffn_in['bias'], 'L1_attn_a_Wq': _L1_attn_a_in['Wq'], 'L1_attn_a_Wk': _L1_attn_a_in['Wk'], 'L1_attn_a_Wv': _L1_attn_a_in['Wv'], 'L1_attn_a_Wo': _L1_attn_a_in['Wo'], 'L1_attn_a_bo': _L1_attn_a_in['bo'], 'L1_attn_b_W_query': _L1_attn_b_in['W_query'], 'L1_attn_b_W_key': _L1_attn_b_in['W_key'], 'L1_attn_b_W_val': _L1_attn_b_in['W_val'], 'L1_attn_b_W_out': _L1_attn_b_in['W_out'], 'L1_ffn_Wg': _L1_ffn_in['Wg'], 'L1_ffn_We': _L1_ffn_in['We'], 'L1_ffn_be': _L1_ffn_in['be']}
    _x0 = _d['L0_attn_a_x']
    _d['L0_attn_a_x'] = jax.random.normal(jax.random.fold_in(jax.random.key(seed), 1), (2, 1024, 128), dtype=_x0.dtype)
    del _x0
    return _d

def reference(L0_attn_a_x, L0_attn_a_Wq, L0_attn_a_Wk, L0_attn_a_Wv, L0_attn_a_Wo, L0_attn_b_fwd_a_logit, L0_attn_b_fwd_Wx, L0_attn_b_fwd_bx, L0_attn_b_fwd_Wgx, L0_attn_b_fwd_bgx, L0_attn_b_fwd_Wga, L0_attn_b_fwd_bga, L0_attn_b_fwd_Wo, L0_attn_b_fwd_bo, L0_attn_b_bwd_a_logit, L0_attn_b_bwd_Wx, L0_attn_b_bwd_bx, L0_attn_b_bwd_Wgx, L0_attn_b_bwd_bgx, L0_attn_b_bwd_Wga, L0_attn_b_bwd_bga, L0_attn_b_bwd_Wo, L0_attn_b_bwd_bo, L0_attn_b_ld_W, L0_attn_b_ld_b, L0_ffn_weight, L0_ffn_alpha, L0_ffn_bias, L1_attn_a_Wq, L1_attn_a_Wk, L1_attn_a_Wv, L1_attn_a_Wo, L1_attn_a_bo, L1_attn_b_W_query, L1_attn_b_W_key, L1_attn_b_W_val, L1_attn_b_W_out, L1_ffn_Wg, L1_ffn_We, L1_ffn_be):

    def _L0_attn_a_ref(x, Wq, Wk, Wv, Wo):
        import jax, jax.numpy as jnp
        import numpy as np
        HIDDEN = 128
        N_HEADS = 16
        HEAD_DIM = HIDDEN // N_HEADS
        WINDOW = 32
        HALF_W = WINDOW // 2
        GLOBAL_TOKENS = (0,)

        def _longformer_mask(seq_len: int) -> jnp.ndarray:
            idx = jnp.arange(seq_len)
            mask = jnp.abs(idx[:, None] - idx[None, :]) <= HALF_W
            for g in GLOBAL_TOKENS:
                if 0 <= g < seq_len:
                    mask = mask.at[g, :].set(True)
                    mask = mask.at[:, g].set(True)
            return mask
        B, S, H = x.shape
        scale = HEAD_DIM ** (-0.5)

        def proj(W):
            return jnp.einsum('bsh,oh->bso', x, W).reshape(B, S, N_HEADS, HEAD_DIM).transpose(0, 2, 1, 3)
        q, k, v = (proj(Wq), proj(Wk), proj(Wv))
        scores = jnp.einsum('bnsd,bntd->bnst', q, k) * scale
        mask = _longformer_mask(S)
        scores = jnp.where(mask[None, None], scores, jnp.float32(-jnp.inf))
        attn = jax.nn.softmax(scores, axis=-1)
        out = jnp.einsum('bnst,bntd->bnsd', attn, v)
        out = out.transpose(0, 2, 1, 3).reshape(B, S, H)
        return jnp.einsum('bsh,oh->bso', out, Wo)

    def _L0_attn_b_ref(x, fwd_a_logit, fwd_Wx, fwd_bx, fwd_Wgx, fwd_bgx, fwd_Wga, fwd_bga, fwd_Wo, fwd_bo, bwd_a_logit, bwd_Wx, bwd_bx, bwd_Wgx, bwd_bgx, bwd_Wga, bwd_bga, bwd_Wo, bwd_bo, ld_W, ld_b):
        import jax, jax.numpy as jnp
        import numpy as np
        B, S, D, Hd = (4, 512, 128, 128)

        def _linear_scan(a, x, reverse):

            def comb(l, r):
                al, bl = l
                ar, br = r
                return (al * ar, bl * ar + br)
            _, h = jax.lax.associative_scan(comb, (a, x), axis=1, reverse=reverse)
            return h

        def _rglru(x, a_logit, Wx, bx, Wgx, bgx, Wga, bga, Wo, bo, reverse):
            a_expit = jax.nn.sigmoid(a_logit)
            x = x @ Wx + bx
            gate_x = jax.nn.sigmoid(x @ Wgx + bgx)
            gate_a = jax.nn.sigmoid(x @ Wga + bga)
            a = gate_a * a_expit
            xin = jnp.sqrt(1.0 - a * a) * (gate_x * x)
            h = _linear_scan(a, xin, reverse)
            return h @ Wo + bo
        last_scale = 1.0
        identity = x
        xg = jax.nn.gelu(x)
        x_fwd = _rglru(xg, fwd_a_logit, fwd_Wx, fwd_bx, fwd_Wgx, fwd_bgx, fwd_Wga, fwd_bga, fwd_Wo, fwd_bo, reverse=False)
        x_bwd = _rglru(xg, bwd_a_logit, bwd_Wx, bwd_bx, bwd_Wgx, bwd_bgx, bwd_Wga, bwd_bga, bwd_Wo, bwd_bo, reverse=True)
        x = (x_fwd + x_bwd) / 2 + identity
        x = jax.nn.gelu(x) @ ld_W + ld_b + identity
        return last_scale * x

    def _L0_ffn_ref(input, weight, alpha, bias):
        import jax, jax.numpy as jnp
        import numpy as np
        THRESH_FACTOR = 0.7

        def ternary_quantize(w):
            delta = THRESH_FACTOR * jnp.mean(jnp.abs(w))
            return jnp.where(w > delta, 1.0, jnp.where(w < -delta, -1.0, 0.0)).astype(w.dtype)
        w_ternary = ternary_quantize(weight)
        w_eff = w_ternary * alpha
        out = jnp.einsum('bsd,od->bso', input, w_eff) + bias
        return out

    def _L1_attn_a_ref(x, Wq, Wk, Wv, Wo, bo):
        import jax, jax.numpy as jnp
        import numpy as np
        D_MODEL = 128
        NUM_HEADS = 16
        HEAD_DIM = D_MODEL // NUM_HEADS
        EPS = 1e-08
        B, T, _ = x.shape
        H, D = (NUM_HEADS, HEAD_DIM)
        scale = jnp.sqrt(jnp.asarray(D, dtype=x.dtype))
        q = (x @ Wq.T).reshape(B, T, H, D).transpose(0, 2, 1, 3)
        k = (x @ Wk.T).reshape(B, T, H, D).transpose(0, 2, 1, 3)
        v = (x @ Wv.T).reshape(B, T, H, D).transpose(0, 2, 1, 3)
        s = jnp.einsum('bhtd,bhsd->bhts', q, k) / scale
        m = jnp.max(s, axis=-1, keepdims=True)
        e = jnp.exp(s - m)
        num = jnp.einsum('bhts,bhsd->bhtd', e, v)
        den = jnp.sum(e, axis=-1, keepdims=True) + EPS
        out = (num / den).transpose(0, 2, 1, 3).reshape(B, T, H * D)
        return out @ Wo.T + bo

    def _L1_attn_b_ref(q, W_query, W_key, W_val, W_out):
        import jax, jax.numpy as jnp
        import numpy as np
        N_HEADS = 16
        INPUT_DIM = 128
        EMBED_DIM = 128
        KEY_DIM = EMBED_DIM // N_HEADS
        BATCH = 4
        SEQ = 256

        def _uniform(key, shape, bound):
            return jax.random.uniform(key, shape, jnp.float32, -bound, bound)
        norm = 1.0 / np.sqrt(KEY_DIM)
        Q = jnp.einsum('bsd,hdk->hbsk', q, W_query)
        K = jnp.einsum('bsd,hdk->hbsk', q, W_key)
        V = jnp.einsum('bsd,hdv->hbsv', q, W_val)
        scores = norm * jnp.einsum('hbqk,hbnk->hbqn', Q, K)
        attn = jax.nn.softmax(scores, axis=-1)
        heads = jnp.einsum('hbqn,hbnv->hbqv', attn, V)
        out = jnp.einsum('hbqv,hve->bqe', heads, W_out)
        return out

    def _L1_ffn_ref(x, Wg, We, be):
        import jax, jax.numpy as jnp
        import numpy as np
        B, S, D = (4, 256, 128)
        E = 8
        CF = 1
        b, s, d = x.shape
        n = b * s
        cap = n // E * CF
        h = x.reshape(n, d)
        router_logits = h @ Wg
        probs = jax.nn.softmax(router_logits, axis=1)
        best = jnp.argmax(probs, axis=1)
        mask = jax.nn.one_hot(best, E, dtype=probs.dtype)
        gate = jnp.sum(probs * mask, axis=1)
        locations = jnp.cumsum(mask, axis=0) - 1.0
        mask = mask * (locations < cap).astype(mask.dtype)
        loc_idx = jnp.sum(locations * mask, axis=1).astype(jnp.int32)
        new_gate = gate[:, None] * mask
        loc_oh = jax.nn.one_hot(loc_idx, cap, dtype=new_gate.dtype)
        combine = new_gate[:, :, None] * loc_oh[:, None, :]
        dispatch = (combine != 0).astype(h.dtype)
        dispatched = jnp.einsum('nec,nd->ecd', dispatch, h).reshape(E * cap, d)
        expert_out = dispatched @ We + be
        out = combine.reshape(n, E * cap) @ expert_out
        return out.reshape(b, s, d)
    x = L0_attn_a_x
    x = x + _L0_attn_a_ref(_layernorm(x, axis=-1), L0_attn_a_Wq, L0_attn_a_Wk, L0_attn_a_Wv, L0_attn_a_Wo)
    x = x + _L0_ffn_ref(_layernorm(x, axis=-1), L0_ffn_weight, L0_ffn_alpha, L0_ffn_bias)
    x = x + _L0_attn_b_ref(_layernorm(x, axis=-1), L0_attn_b_fwd_a_logit, L0_attn_b_fwd_Wx, L0_attn_b_fwd_bx, L0_attn_b_fwd_Wgx, L0_attn_b_fwd_bgx, L0_attn_b_fwd_Wga, L0_attn_b_fwd_bga, L0_attn_b_fwd_Wo, L0_attn_b_fwd_bo, L0_attn_b_bwd_a_logit, L0_attn_b_bwd_Wx, L0_attn_b_bwd_bx, L0_attn_b_bwd_Wgx, L0_attn_b_bwd_bgx, L0_attn_b_bwd_Wga, L0_attn_b_bwd_bga, L0_attn_b_bwd_Wo, L0_attn_b_bwd_bo, L0_attn_b_ld_W, L0_attn_b_ld_b)
    x = x + _L0_ffn_ref(_layernorm(x, axis=-1), L0_ffn_weight, L0_ffn_alpha, L0_ffn_bias)
    x = x + _L1_attn_a_ref(_layernorm(x, axis=-1), L1_attn_a_Wq, L1_attn_a_Wk, L1_attn_a_Wv, L1_attn_a_Wo, L1_attn_a_bo)
    x = x + _L1_ffn_ref(_layernorm(x, axis=-1), L1_ffn_Wg, L1_ffn_We, L1_ffn_be)
    x = x + _L1_attn_b_ref(_layernorm(x, axis=-1), L1_attn_b_W_query, L1_attn_b_W_key, L1_attn_b_W_val, L1_attn_b_W_out)
    x = x + _L1_ffn_ref(_layernorm(x, axis=-1), L1_ffn_Wg, L1_ffn_We, L1_ffn_be)
    return x

_drawn_inputs = setup_inputs


def setup_inputs(seed=0):
    import zlib

    import numpy as np

    out = dict(_drawn_inputs(seed))
    spreads = {'L0_attn_b_fwd_bx': (0.0, 0.8),
     'L0_attn_b_fwd_bgx': (0.0, 2.0),
     'L0_attn_b_fwd_bga': (0.0, 2.0),
     'L0_attn_b_fwd_bo': (0.0, 2.0),
     'L0_attn_b_bwd_bx': (0.0, 0.8),
     'L0_attn_b_bwd_bgx': (0.0, 2.0),
     'L0_attn_b_bwd_bga': (0.0, 2.0),
     'L0_attn_b_bwd_bo': (0.0, 2.0),
     'L0_attn_b_ld_b': (0.0, 0.717),
     'L1_attn_a_bo': (0.0, 0.8)}
    factors = {'L0_attn_a_Wq': 8.0,
     'L0_attn_a_Wk': 8.0,
     'L0_attn_a_Wv': 6.313,
     'L0_attn_a_Wo': 6.409,
     'L0_attn_b_fwd_a_logit': 8.0,
     'L0_attn_b_fwd_Wx': 4.432,
     'L0_attn_b_fwd_Wgx': 8.0,
     'L0_attn_b_fwd_Wga': 8.0,
     'L0_attn_b_fwd_Wo': 4.05,
     'L0_attn_b_bwd_a_logit': 8.0,
     'L0_attn_b_bwd_Wx': 4.589,
     'L0_attn_b_bwd_Wgx': 8.0,
     'L0_attn_b_bwd_Wga': 8.0,
     'L0_attn_b_bwd_Wo': 4.128,
     'L0_ffn_bias': 3.855,
     'L1_attn_a_Wq': 8.0,
     'L1_attn_a_Wk': 8.0,
     'L1_attn_a_Wv': 8.0,
     'L1_attn_a_Wo': 8.0,
     'L1_ffn_Wg': 2.779,
     'L1_ffn_be': 61.12}
    for name, (base, spread) in spreads.items():
        noise = np.random.default_rng([zlib.crc32(name.encode()), seed]).standard_normal(out[name].shape)
        drawn = base * np.exp(spread * noise) if base else spread * noise
        out[name] = jnp.asarray(drawn.astype(out[name].dtype))
    for name, factor in factors.items():
        out[name] = (out[name] * factor).astype(out[name].dtype)
    return out
```

```python
from contextlib import ExitStack

import numpy as np

import concourse.bass as bass
from concourse import mybir

ALU = mybir.AluOpType
ACT = mybir.ActivationFunctionType
AX = mybir.AxisListType
F32 = mybir.dt.float32
BF16 = mybir.dt.bfloat16
F16 = mybir.dt.float16

P = 128
B, S = 2, 1024
N = B * S
NC = N // 512
NT = N // P
H, D = 16, 8
NP = 9
R = NP * D
RM = R + 3
SCALE = float(D) ** -0.5
LN_EPS = 1e-5
DEN_EPS = 1e-8
HALF = 16
QT = P - 1 - 2 * HALF
WT = -(-S // QT)
QW = WT * QT
KW = WT * P
PADW = HALF + QW + HALF + 3
E = 8
CAP = N // E
NEG = -1.0e30
UNITS = B * H
KT = S // P
VC = 3 * D + 1
LO_F = 5 * P
LO_W = 6 * QT
RING_W, RING_F = 8, 4

W_NAMES = ["wq0", "wk0", "wv0", "wo0", "f_x", "f_gx", "f_ga", "f_o", "b_x", "b_gx", "b_ga", "b_o", "ld",
           "tern", "wq1", "wk1", "wv1", "wo1", "wq2", "wk2", "wv2", "wo2", "we"]
B_NAMES = ["f_a", "f_bx", "f_bgx", "f_bga", "f_bo", "b_a", "b_bx", "b_bgx", "b_bga", "b_bo", "ld_b",
           "ffn_b", "bo", "be", "alpha"]
C_STEPS = 43
WI = {n: i for i, n in enumerate(W_NAMES)}
BI = {n: i for i, n in enumerate(B_NAMES)}


def build(nc, xT, weights, biases, wg, out, stages=8):
    with ExitStack() as ctx:
        def sb(name, shape, dt=F32):
            return ctx.enter_context(nc.sbuf_tensor(name, shape, dt))

        def sem(name):
            return ctx.enter_context(nc.semaphore(name))

        parts_dram = nc.dram_tensor("parts_dram", (2, 3, P, B * KW), BF16).ap()

        bank = [ctx.enter_context(nc.psum_tensor(f"bank{i}", [P, 512], F32)) for i in range(2)]
        wide = ctx.enter_context(nc.psum_tensor("wide", [P, 6, 512], F32))

        def bk(i):
            return wide[:, i, :] if i < 6 else bank[i - 6][:, :]

        x = sb("x", [P, N])
        xcsq = sb("xcsq", [P, 2 * N])
        xc, sq = xcsq[:, 0:N], xcsq[:, N:2 * N]
        xp = sb("xp", [P, B, PADW])
        W = sb("W", [P, len(W_NAMES), P])
        bias = sb("bias", [P, len(B_NAMES)])
        wgs = sb("wgs", [P, E])
        ident = sb("ident", [P, P])
        identb = sb("identb", [P, P], BF16)
        ones = sb("ones", [P, P])
        meanw = sb("meanw", [P, P])
        tri = sb("tri", [P, P])
        sel = sb("sel", [NT, NT, P])
        epsc = sb("epsc", [P, 1])
        keep = sb("keep", [P, E, NT])
        rank = sb("rank", [P, NT, E])
        maskq = sb("maskq", [P, WT, P], BF16)
        maskk = sb("maskk", [P, WT, QT], BF16)
        hmask = sb("hmask", [P, H])
        hmaskT = sb("hmaskT", [H, H, D + 1])
        ln_s = sb("ln_s", [P, 2, NT])
        ln_t = sb("ln_t", [NT, P])
        tern = sb("tern", [P, P])
        tg = sb("tg", [P, 2, P])
        ts_ = sb("ts_", [P, 4])
        eas = sb("eas", [P, 4])

        big = sb("big", [P, 7 * N])
        xwin = big[:, 0:B * KW].rearrange("p (b t k) -> p b t k", b=B, t=WT)
        kf = big[:, B * KW:2 * B * KW]
        V = sb("V", [P, B * WT, H, D + 1])
        o = 2 * B * KW
        A = big[:, o:o + B * WT * P].rearrange("p (t f) -> p t f", f=P)
        o += B * WT * P
        pt = big[:, o:o + 4 * 1056].rearrange("p (n c) -> p n c", n=4)
        aT = sq
        pth = big[:, o:o + 4 * 1056].bitcast(BF16).rearrange("p (n c two) -> p n c two", n=4, two=2)[:, :, :, 1]
        lo = kf.bitcast(F16)[:, 0:4 * 1056].rearrange("p (n c) -> p n c", n=4)
        Vb = sb("Vb", [P, B * WT, H, VC], BF16)
        res = sb("res", [P, 2, 512])
        parts = sb("parts", [P, 2, 3, 512], BF16)
        Ka = sb("Ka", [RM, RING_W, KW], BF16)
        Qa = sb("Qa", [RM, RING_W, QW + 1], BF16)
        mx = sb("mx", [P, KT, 2])
        nm = sb("nm", [P, RING_W, WT])
        mres = sb("mres", [WT, P])
        mp = big[0:WT, o + 4 * 1056:o + 4 * 1056 + RING_W * 3 * P // 2].bitcast(BF16).rearrange(
            "p (u n c) -> p u n c", u=RING_W, n=3)
        num = sb("num", [P, WT, D])
        den = sb("den", [P, WT])
        rden = sb("rden", [P, WT])
        q0f = sb("q0f", [P, B])
        q0m = sb("q0m", [P, B, H])
        s0 = big[0:H, o:o + B * WT * P].rearrange("p (b t k) -> p b t k", b=B, t=WT)
        s0s = sb("s0s", [H, B, 4])
        s0t = sb("s0t", [P, B, WT, H])
        o0 = sb("o0", [H, B, H, D + 1])
        o0s = sb("o0s", [H, B, D + 1])
        z0 = sb("z0", [H, B, H, D])
        q0x = sb("q0x", [H, B, 3])
        q0o = sb("q0o", [P, B])
        rg = big[:, 0:3 * N].rearrange("p (n t) -> p n t", n=3)
        rb = big[:, 3 * N:7 * N].rearrange("p (n t) -> p n t", n=2)
        rc = xcsq
        mgb = big[:, 0:N]
        me = sb("me", [P, NT, E])
        mw = sb("mw", [P, NT, E])
        moh = sb("moh", [P, NT * E])
        mloc = sb("mloc", [P, NT, E])
        mt1 = sb("mt1", [P, E, NT])
        mt2 = sb("mt2", [P, E, NT])
        mst = sb("mst", [P, 6, NT])
        mgate = sb("mgate", [P, NT])

        x_loaded, w_loaded = sem("x_loaded"), sem("w_loaded")
        c_ready = sem("c_ready")
        tw = sem("tw")
        tw_sum = sem("tw_sum")
        ea_ready = sem("ea_ready")
        x_new = sem("x_new")
        ln_mean, ln_cent, ln_sq, ln_var = sem("ln_mean"), sem("ln_cent"), sem("ln_sq"), sem("ln_var")
        ln_std, ln_rstd, ln_rT, ln_rTs = sem("ln_std"), sem("ln_rstd"), sem("ln_rT"), sem("ln_rTs")
        ln_b, xn_ready = sem("ln_b"), sem("xn_ready")
        win_ready = sem("win_ready")
        qk_mm = sem("qk_mm")
        part_act = sem("part_act")
        part_dve = sem("part_dve")
        qk_out = [sem(f"qk_out{i}") for i in range(2)]
        v_mm, v_out = sem("v_mm"), sem("v_out")
        v_dve = sem("v_dve")
        lo_pool, lo_dve = sem("lo_pool"), sem("lo_dve")
        q0_copied, kf_done, q0_max = sem("q0_copied"), sem("kf_done"), sem("q0_max")
        aug_w = [sem(f"aug_w{i}") for i in range(RING_W)]
        aug_f = [sem(f"aug_f{i}") for i in range(RING_F)]
        mrow_w = [sem(f"mrow_w{i}") for i in range(RING_W)]
        mrow_f = [sem(f"mrow_f{i}") for i in range(RING_F)]
        st_ready = sem("st_ready")
        exp_done = sem("exp_done")
        sm_ready, sm_read = sem("sm_ready"), sem("sm_read")
        nm_ready = sem("nm_ready")
        mt_ready = sem("mt_ready")
        split = sem("split")
        pv_steps = sem("pv_steps")
        evac = sem("evac")
        g0 = sem("g0")
        g0v = sem("g0v")
        g0a = sem("g0a")
        at_mm, at_out, o_mm = sem("at_mm"), sem("at_out"), sem("o_mm")
        f_mm = sem("f_mm")
        r_pe, r_act, r_dve, r_pool = sem("r_pe"), sem("r_act"), sem("r_dve"), sem("r_pool")
        m_pe, m_act, m_dve, m_y = sem("m_pe"), sem("m_act"), sem("m_dve"), sem("m_y")
        stored = sem("stored")

        def w(name):
            return W[:, WI[name], :]

        def bcol(name):
            return bias[:, BI[name]:BI[name] + 1]

        def xch(t, c):
            return t[:, 512 * c:512 * c + 512]

        def xn(c):
            b, o = c // 2, HALF + 512 * (c % 2)
            return xp[:, b, o:o + 512]

        def xnt(t):
            b, o = t // KT, HALF + P * (t % KT)
            return xp[:, b, o:o + P]

        QCH = [(b, t, min(5, WT - t)) for b in range(B) for t in range(0, WT, 5)]
        KCH = [(b, t, min(4, WT - t)) for b in range(B) for t in range(0, WT, 4)]

        def qk_chunks(layer):
            if layer == 0:
                for b, t, n in QCH:
                    yield 0, xp[:, b, HALF + t * QT:HALF + (t + n) * QT], n * QT, b * QW + t * QT
                for b, t, n in KCH:
                    yield 1, xwin[:, b, t:t + n, :], n * P, b * KW + t * P
            else:
                for i in range(2):
                    for c in range(NC):
                        yield i, xn(c), 512, 512 * c

        QK_BASE = [0] + [len(QCH) + len(KCH) + 2 * NC * i for i in range(3)]
        VCH = [[(b * WT + t, min(4, WT - t)) for b in range(B) for t in range(0, WT, 4)],
               [(4 * c, 4) for c in range(NC)], [(4 * c, 4) for c in range(NC)]]
        V_BASE = [0, len(VCH[0]), len(VCH[0]) + NC, len(VCH[0]) + 2 * NC]
        AT_BASE = [0, len(QCH), len(QCH) + NC]
        ST_BASE = [0, UNITS, UNITS + UNITS * KT]
        SM_BASE = [0, UNITS, UNITS + UNITS * KT * 2]

        nst = min(stages, 8)
        R_U, R_G = [NC, 4 * NC], [2 * NC, 5 * NC]
        R_SQ = 7 * NC
        R_OUT = R_SQ + 4 * NC
        R_GELU2 = R_OUT + NC
        R_SCAN = 6 * NC + 2 * B
        R_HB = R_SCAN + 2
        M_PE, M_ACT, M_DVE = 3 * NC, 1 + NC, 18

        block = ctx.enter_context(nc.Block())

        @block.sync
        def _(sp):
            sp.dma_start(x[:, :], xT).then_inc(x_loaded, 16)
            sp.dma_start(W[:, :, :], weights).then_inc(w_loaded, 16)
            sp.dma_start(bias[:, :], biases).then_inc(w_loaded, 16)
            sp.dma_start(wgs[:, :], wg).then_inc(w_loaded, 16)

            def store_parts(layer):
                for n, (i, _, cols, at) in enumerate(qk_chunks(layer), QK_BASE[layer]):
                    sp.wait_ge(part_dve, 2 * n + 2)
                    sp.dma_start(parts_dram[i, :, :, at:at + cols].rearrange("a p c -> p a c"),
                                 parts[:, n % 2, :, 0:cols]).then_inc(qk_out[n % 2], 16)

            def parts_stored(layer):
                n = QK_BASE[layer + 1]
                sp.wait_ge(qk_out[0], 16 * ((n + 1) // 2))
                sp.wait_ge(qk_out[1], 16 * (n // 2))

            def load_unit(layer, h, b, slot):
                qn, kn = (QW, KW) if layer == 0 else (S, S)
                loaded = aug_w[slot] if layer == 0 else aug_f[slot]
                for i in range(3):
                    q = parts_dram[0, i, bass.ds(h * D, D), b * qn:b * qn + qn]
                    sp.dma_start(Qa[i * 24:i * 24 + 24, slot, 0:qn],
                                 q.unsqueeze(1).broadcast_to((D, 3, qn))).then_inc(loaded, 16)
                    k = parts_dram[1, :, bass.ds(h * D, D), b * kn:b * kn + kn]
                    sp.dma_start(Ka[i * 24:i * 24 + 24, slot, 0:kn],
                                 k.rearrange("j d t -> d j t")).then_inc(loaded, 16)

            def place_maximum(layer, u, slot):
                qt, n = (QT, WT) if layer == 0 else (P, KT)
                rows = mrow_w[slot] if layer == 0 else mrow_f[slot]
                sp.wait_ge(split, 4 * (UNITS * layer + u) + 8)
                for i in range(3):
                    sp.dma_start(Qa[R + i:R + i + 1, slot, 0:n * qt],
                                 mp[0:n, slot, i, 0:qt]).then_inc(rows, 16)

            def attention(layer):
                per = 1 if layer == 0 else KT
                ring, ahead = (RING_W, 2) if layer == 0 else (RING_F, 1)
                for u in range(ring):
                    load_unit(layer, u // B, u % B, u)
                for u in range(ahead):
                    place_maximum(layer, u, u)

                def slot(i, j, last):
                    s = i * ring + j
                    if not last or j + ahead < ring:
                        place_maximum(layer, s + ahead, (j + ahead) % ring)
                    if not last:
                        sp.wait_ge(st_ready, ST_BASE[layer] + (s + 1) * per)
                        load_unit(layer, i * (ring // B) + (ring + j) // B, j % B, j)

                with sp.Fori(0, UNITS // ring - 1) as i:
                    for j in range(ring):
                        slot(i, j, False)
                for j in range(ring):
                    slot(UNITS // ring - 1, j, True)

            sp.wait_ge(c_ready, C_STEPS)
            for stage in range(nst):
                if stage in (0, 4, 6):
                    layer = {0: 0, 4: 1, 6: 2}[stage]
                    store_parts(layer)
                    parts_stored(layer)
                    attention(layer)
            for c in range(NC):
                sp.wait_ge(x_new, NC * (nst - 1) + c + 1)
                sp.dma_start(out[:, 512 * c:512 * c + 512], xch(x, c)).then_inc(stored, 16)
            sp.wait_ge(stored, 16 * NC)

        @block.gpsimd
        def _(pool):
            n = [0]

            def step(ins):
                n[0] += 1
                ins.then_inc(c_ready, 1)
                pool.wait_ge(c_ready, n[0])

            def select(v, op, fill, base, pattern, cm):
                step(pool.affine_select(out=v, in_=v, compare_op=op, fill=fill, base=base, pattern=pattern,
                                        channel_multiplier=cm))

            step(pool.memset(ones[:, :], 1.0))
            step(pool.memset(meanw[:, :], 1.0 / P))
            step(pool.memset(epsc[:, :], LN_EPS))
            step(pool.memset(xp[:, :, :], 0.0))
            step(pool.memset(ident[:, :], 0.0))
            select(ident[:, :], ALU.not_equal, 1.0, 0, [[-1, P]], 1)
            step(pool.memset(identb[:, :], 0.0))
            select(identb[:, :], ALU.not_equal, 1.0, 0, [[-1, P]], 1)
            step(pool.memset(sel[:, :, :], 0.0))
            select(sel[:, :, :], ALU.not_equal, 1.0, 0, [[-1, NT], [0, P]], 1)
            step(pool.memset(maskq[:, :, :], 0.0))
            select(maskq[:, :, 0:P - 1], ALU.is_ge, NEG, 0, [[0, WT], [1, P - 1]], -1)
            select(maskq[:, :, 0:P - 1], ALU.is_ge, NEG, 2 * HALF, [[0, WT], [-1, P - 1]], 1)
            select(maskq[:, :, 0:P - 1], ALU.is_gt, NEG, -HALF, [[QT, WT], [1, P - 1]], 0)
            select(maskq[:, :, 0:P - 1], ALU.is_gt, NEG, S + HALF, [[-QT, WT], [-1, P - 1]], 0)
            step(pool.memset(maskk[:, :, :], 0.0))
            select(maskk[:, :, :], ALU.is_ge, NEG, 0, [[0, WT], [-1, QT]], 1)
            select(maskk[:, :, :], ALU.is_ge, NEG, 2 * HALF, [[0, WT], [1, QT]], -1)
            select(maskk[:, :, :], ALU.is_gt, NEG, -HALF, [[QT, WT], [0, QT]], 1)
            select(maskk[:, :, :], ALU.is_gt, NEG, S + HALF, [[-QT, WT], [0, QT]], -1)
            select(maskk[:, :, :], ALU.is_gt, 0.0, P - 1, [[0, WT], [0, QT]], -1)
            step(pool.memset(Ka[:, :, :], 1.0))
            step(pool.memset(Qa[:, :, :], 0.0))
            step(pool.memset(V[:, :, :, D:D + 1], 1.0))
            step(pool.memset(Vb[:, :, :, 3 * D:VC], 1.0))
            step(pool.memset(s0[:, :, :, :], 0.0))
            step(pool.memset(tri[:, :], 1.0))
            select(tri[:, :], ALU.is_ge, 0.0, 0, [[1, P]], -1)
            step(pool.memset(keep[:, :, :], 1.0))
            step(pool.memset(keep[:, :, 0:1], 0.0))
            for e in range(E):
                step(pool.memset(rank[:, :, e:e + 1], float(E - e)))
            step(pool.memset(hmask[:, :], 1.0))
            select(hmask[:, :], ALU.is_ge, 0.0, 0, [[-D, H]], 1)
            select(hmask[:, :], ALU.is_ge, 0.0, D - 1, [[D, H]], -1)
            step(pool.memset(hmaskT[:, :, :], 1.0))
            select(hmaskT[:, :, :], ALU.is_equal, 0.0, 0, [[-1, H], [0, D + 1]], 1)
            assert n[0] == C_STEPS, n[0]

            def remainder(slot, cols):
                pool.tensor_tensor(lo[:, slot, 0:cols], pt[:, slot, 0:cols], pth[:, slot, 0:cols],
                                   ALU.subtract).then_inc(lo_pool, 1)

            if nst > 0:
                with pool.Fori(0, UNITS // RING_W) as i:
                    for j in range(RING_W):
                        pool.wait_ge(exp_done, i * RING_W + j + 2)
                        remainder(j % 2, LO_W)
            for layer in (1, 2):
                if nst > 2 * layer + 2:
                    with pool.Fori(0, UNITS) as i:
                        for j in range(KT):
                            pool.wait_ge(exp_done, ST_BASE[layer] + i * KT + j + 2)
                            remainder(j % 4, LO_F)

        @block.tensor
        def _(pe):
            def mm(o, l, r, start=True, stop=True, **kw):
                return nc.tensor.matmul(o, l, r, start=start, stop=stop, **kw)

            def layernorm(k):
                if k == 0:
                    pe.wait_ge(x_loaded, 16)
                else:
                    pe.wait_ge(x_new, NC * k)
                for c in range(NC):
                    mm(bk(c), meanw[:, :], xch(x, c)).then_inc(ln_mean, 1)
                for c in range(NC):
                    pe.wait_ge(ln_sq, NC * k + c + 1)
                    for t in range(4 * c, 4 * c + 4):
                        ins = mm(bk(4)[:, t:t + 1], sq[:, P * t:P * t + P], meanw[:, 0:1])
                ins.then_inc(ln_var, 1)
                pe.wait_ge(ln_rstd, k + 1)
                nc.tensor.transpose(bk(5)[0:NT, 0:P], ln_s[:, 1, :], ident[:, :]).then_inc(ln_rT, 1)
                pe.wait_ge(ln_rTs, k + 1)
                for t in range(NT):
                    ins = mm(bk(t // 4)[:, P * (t % 4):P * (t % 4) + P], sel[:, t, :], ln_t[:, :])
                    if t % 4 == 3:
                        ins.then_inc(ln_b, 1)

            def ternary():
                pe.wait_ge(tw, 1)
                mm(bk(6)[:, 0:1], ones[:, :], ts_[:, 0:1]).then_inc(tw_sum, 1)

            def project_qkv(layer):
                pe.wait_ge(xn_ready, NC * ({0: 0, 1: 4, 2: 6}[layer] + 1))
                if layer == 0:
                    pe.wait_ge(win_ready, 3)
                wn = ("wq%d" % layer, "wk%d" % layer)
                for n, (i, mov, cols, _) in enumerate(qk_chunks(layer), QK_BASE[layer]):
                    if n >= 2:
                        pe.wait_ge(part_dve, 2 * (n - 2) + 2)
                    mm(bk(n % 2)[:, 0:cols], w(wn[i]), mov).then_inc(qk_mm, 1)
                for g, (t0, k) in enumerate(VCH[layer], V_BASE[layer]):
                    if g >= 2:
                        pe.wait_ge(v_dve, 2 * g - 2)
                    for y in range(k):
                        t = t0 + y
                        lhs = xwin[:, t // WT, t % WT, :] if layer == 0 else xnt(t)
                        ins = mm(bk(2 + g % 2)[:, y * P:(y + 1) * P], lhs, w("wv%d" % layer))
                    ins.then_inc(v_mm, 1)

            def query_zero():
                pe.wait_ge(g0v, 1)
                pe.wait_ge(v_dve, 2 * V_BASE[1])
                pe.wait_ge(part_dve, 2 * QK_BASE[1])
                for b in range(B):
                    for t in range(0, WT, 5):
                        k = min(5, WT - t)
                        cols = kf[:, b * KW + t * P:b * KW + (t + k) * P].rearrange("p (t k) -> p t k", k=P)
                        ins = mm(bk(3 * b + t // 5)[0:H, 0:k * QT].rearrange("p (t k) -> p t k", k=QT),
                                 q0m[:, b, :], cols[:, :, HALF:HALF + QT])
                    ins.then_inc(g0, 1)
                pe.wait_ge(g0a, 2)
                for b in range(B):
                    for t in range(WT):
                        ins = nc.tensor.transpose(bk(6)[:, (b * WT + t) * H:(b * WT + t + 1) * H],
                                                  s0[:, b, t, :], ident[0:H, 0:H])
                ins.then_inc(g0, 1)
                pe.wait_ge(g0v, 4)
                for b in range(B):
                    for t in range(WT):
                        ins = mm(bk(7)[0:H, 160 * b:160 * b + H * (D + 1)], s0t[:, b, t, :],
                                 V[:, b * WT + t, :, :].rearrange("p h d -> p (h d)"),
                                 start=(t == 0), stop=(t == WT - 1))
                ins.then_inc(g0, 1)
                pe.wait_ge(g0v, 14)
                for b in range(B):
                    ins = mm(bk(6)[:, 400 + b:401 + b], z0[:, b, :, :].rearrange("p h d -> p (h d)"),
                             ones[0:H, 0:1])
                ins.then_inc(g0, 1)

            def windowed_attention():
                pe.wait_ge(g0v, 15)
                pe.drain().then_inc(pv_steps, 4)

                def maxima(u, j):
                    pe.wait_ge(sm_read, u + 1)
                    for t in range(0, WT, 4):
                        k = min(4, WT - t)
                        mm(bk(t // 4)[0:QT, 0:k * P], identb[0:QT, 0:QT],
                           maskq[0:QT, t:t + k, :].rearrange("p t k -> p (t k)"))
                        for y in range(t, t + k):
                            ins = mm(bk(t // 4)[0:QT, (y - t) * P:(y - t + 1) * P],
                                     Qa[0:R, j, y * QT:(y + 1) * QT], Ka[0:R, j, y * P:(y + 1) * P],
                                     start=False, stop=True, skip_group_check=True)
                    ins.then_inc(sm_ready, 1)

                def turn(u, j):
                    pe.wait_ge(sm_read, u + 2)
                    pe.wait_ge(split, 4 * u + 4)
                    nc.tensor.transpose(bk(7)[0:WT, 0:QT], nm[0:QT, j, :], ident[0:QT, 0:QT]).then_inc(mt_ready, 1)

                def scores(u, j, use):
                    pe.wait_ge(mrow_w[j], 48 * use)
                    pe.wait_ge(exp_done, u + 1)
                    for t in range(0, WT, 5):
                        k = min(5, WT - t)
                        mm(bk(3 + t // 5)[:, 0:k * QT], identb[:, :],
                           maskk[:, t:t + k, :].rearrange("p t k -> p (t k)"))
                        for y in range(t, t + k):
                            ins = mm(bk(3 + t // 5)[:, (y - t) * QT:(y - t + 1) * QT],
                                     Ka[0:RM, j, y * P:(y + 1) * P], Qa[0:RM, j, y * QT:(y + 1) * QT],
                                     start=False, stop=True, skip_group_check=True)
                    ins.then_inc(st_ready, 1)

                def values(u, j, h, b):
                    pe.wait_ge(lo_pool, u + 1)
                    pe.wait_ge(lo_dve, u + 1)
                    pe.wait_ge(evac, 4 * u + 4)
                    for t in range(WT):
                        v = Vb[:, b * WT + t, bass.ds(h, 1), :].rearrange("p h d -> p (h d)")
                        o = bk(6)[0:QT, t * VC:(t + 1) * VC]
                        mm(o, pth[:, j % 2, t * QT:(t + 1) * QT], v, stop=False)
                        ins = mm(o, lo[:, j % 2, t * QT:(t + 1) * QT], v, start=False)
                    ins.then_inc(pv_steps, 1)

                for u in range(3):
                    pe.wait_ge(aug_w[u], 96)
                    maxima(u, u)
                for u in range(2):
                    turn(u, u)
                scores(0, 0, 1)

                def slot(i, j, last):
                    s = i * RING_W + j
                    if not last or j + 3 < RING_W:
                        pe.wait_ge(aug_w[(j + 3) % RING_W], 96 * (i + 1 + (j + 3) // RING_W))
                        maxima(s + 3, (j + 3) % RING_W)
                    if not last or j + 2 < RING_W:
                        turn(s + 2, (j + 2) % RING_W)
                    values(s, j, i * (RING_W // B) + j // B, j % B)
                    if not last or j + 1 < RING_W:
                        scores(s + 1, (j + 1) % RING_W, i + 1 + (j + 1) // RING_W)

                with pe.Fori(0, UNITS // RING_W - 1) as i:
                    for j in range(RING_W):
                        slot(i, j, False)
                for j in range(RING_W):
                    slot(UNITS // RING_W - 1, j, True)

            def full_attention(layer):
                u0, st0, sm0 = layer * UNITS, ST_BASE[layer], SM_BASE[layer]
                use0 = (layer - 1) * (UNITS // RING_F)
                pe.wait_ge(v_dve, 2 * V_BASE[layer + 1])
                pe.wait_ge(part_dve, 2 * QK_BASE[layer + 1])

                def maxima(u, j, t):
                    for y in range(2):
                        pe.wait_ge(sm_read, sm0 + (u * KT + t) * 2 + y)
                        mm(bk(4 + y), Qa[0:R, j, t * P:(t + 1) * P],
                           Ka[0:R, j, 512 * y:512 * y + 512]).then_inc(sm_ready, 1)

                def turn(u, j):
                    pe.wait_ge(nm_ready, u0 - UNITS + u + 1)
                    pe.wait_ge(split, 4 * (u0 + u) + 4)
                    nc.tensor.transpose(bk(7)[0:KT, 0:P], nm[:, j, 0:KT], ident[:, :]).then_inc(mt_ready, 1)

                def scores(u, j, t):
                    pe.wait_ge(exp_done, st0 + u * KT + t)
                    for y in range(2):
                        ins = mm(bk(2 * (t % 2) + y), Ka[0:RM, j, t * P:(t + 1) * P],
                                 Qa[0:RM, j, 512 * y:512 * y + 512])
                    ins.then_inc(st_ready, 1)

                def values(u, j, t, h, b):
                    n = st0 + u * KT + t
                    pe.wait_ge(lo_pool, n + 1)
                    pe.wait_ge(lo_dve, n + 1)
                    if t == 0:
                        pe.wait_ge(evac, 4 * (u0 + u) + 4)
                    v = Vb[:, b * KT + t, bass.ds(h, 1), :].rearrange("p h d -> p (h d)")
                    for y in range(KT):
                        o = bk(6)[:, y * VC:(y + 1) * VC]
                        mm(o, pth[:, t % 4, y * P:(y + 1) * P], v, start=(t == 0 and y == 0), stop=False,
                           skip_group_check=True)
                        ins = mm(o, lo[:, t % 4, y * P:(y + 1) * P], v, start=False, stop=(t == KT - 1),
                                 skip_group_check=True)
                    ins.then_inc(pv_steps, 1)

                for u in range(2):
                    pe.wait_ge(aug_f[u], 96 * (use0 + 1))
                    for t in range(KT):
                        maxima(u, u, t)
                turn(0, 0)
                pe.wait_ge(mrow_f[0], 48 * (use0 + 1))
                scores(0, 0, 0)
                scores(0, 0, 1)

                def slot(i, j, last):
                    s = i * RING_F + j
                    nxt = not last or j + 1 < RING_F
                    smx = not last or j + 2 < RING_F
                    for t in range(KT):
                        if t < KT - 2:
                            scores(s, j, t + 2)
                        elif nxt:
                            if t == KT - 2:
                                pe.wait_ge(mrow_f[(j + 1) % RING_F], 48 * (use0 + i + 1 + (j + 1) // RING_F))
                            scores(s + 1, (j + 1) % RING_F, t + 2 - KT)
                        if t == 1 and nxt:
                            turn(s + 1, (j + 1) % RING_F)
                        if smx:
                            if t == 0:
                                pe.wait_ge(aug_f[(j + 2) % RING_F], 96 * (use0 + i + 1 + (j + 2) // RING_F))
                            maxima(s + 2, (j + 2) % RING_F, t)
                        values(s, j, t, i * (RING_F // B) + j // B, j % B)

                with pe.Fori(0, UNITS // RING_F - 1) as i:
                    for j in range(RING_F):
                        slot(i, j, False)
                for j in range(RING_F):
                    slot(UNITS // RING_F - 1, j, True)

            def project_out(layer):
                n0 = AT_BASE[layer]
                pe.wait_ge(evac, 4 * UNITS * (layer + 1) + 4)
                chunks = ([(b * WT + t, k, QT) for b, t, k in QCH] if layer == 0
                          else [(4 * c, 4, P) for c in range(NC)])
                for n, (t, k, q) in enumerate(chunks):
                    if n >= 2:
                        pe.wait_ge(at_out, n0 + n - 1)
                    for y in range(k):
                        ins = nc.tensor.transpose(bk(n % 2)[:, y * q:(y + 1) * q], A[0:q, t + y, :], ident[0:q, 0:q])
                    ins.then_inc(at_mm, 1)
                pe.wait_ge(at_out, n0 + len(chunks))
                if layer == 0:
                    pe.wait_ge(g0v, 16)
                for c in range(NC):
                    mm(bk(2 + c), w("wo%d" % layer), xch(aT, c)).then_inc(o_mm, 1)

            def ffn(k):
                pe.wait_ge(tw, 5)
                for c in range(NC):
                    pe.wait_ge(xn_ready, NC * (1 + 2 * k) + c + 1)
                    mm(bk(4 + c), tern[:, :], xn(c)).then_inc(f_mm, 1)

            def recurrent():
                pe.wait_ge(xn_ready, NC * 3)
                n = 0
                for d in range(2):
                    p = "fb"[d]
                    for c in range(NC):
                        if d == 0:
                            pe.wait_ge(r_act, c + 1)
                        else:
                            pe.wait_ge(r_act, R_U[0] + c + 1)
                        mm(bk(c), w(p + "_x"), rg[:, 0, 512 * c:512 * c + 512]).then_inc(r_pe, 1)
                    for c in range(NC):
                        pe.wait_ge(r_act, R_U[d] + c + 1)
                        if n >= 2:
                            pe.wait_ge(r_act, R_G[(n - 2) // NC] + 2 * ((n - 2) % NC) + 2)
                        u = rg[:, 1 + d, 512 * c:512 * c + 512]
                        mm(bk(4 + 2 * (n % 2)), w(p + "_gx"), u).then_inc(r_pe, 1)
                        mm(bk(5 + 2 * (n % 2)), w(p + "_ga"), u).then_inc(r_pe, 1)
                        n += 1
                pe.wait_ge(r_dve, R_SCAN)
                for c in range(NC):
                    mm(bk(c), w("f_o"), rg[:, 1, 512 * c:512 * c + 512], stop=False)
                    mm(bk(c), w("b_o"), rg[:, 2, 512 * c:512 * c + 512], start=False).then_inc(r_pe, 1)
                for c in range(NC):
                    pe.wait_ge(r_act, R_GELU2 + c + 1)
                    mm(bk(4 + c), w("ld"), rb[:, 0, 512 * c:512 * c + 512]).then_inc(r_pe, 1)

            def moe(k):
                pe.wait_ge(xn_ready, NC * (6 + 2 * k))
                for t in range(NT):
                    ins = mm(bk(0)[:, t * E:(t + 1) * E], xnt(t), wgs[:, :])
                ins.then_inc(m_pe, 1)
                for c in range(NC):
                    mm(bk(4 + c), w("we"), xn(c)).then_inc(m_pe, 1)
                pe.wait_ge(m_dve, M_DVE * k + 10)
                mm(bk(1)[:, 0:P], tri[:, :], moh[:, :]).then_inc(m_pe, 1)
                mm(bk(2)[:, 0:P], ones[:, :], moh[:, :]).then_inc(m_pe, 1)
                pe.wait_ge(m_dve, M_DVE * k + 17)
                nc.tensor.transpose(bk(3)[0:NT, 0:P], mgate[:, :], ident[:, :]).then_inc(m_pe, 1)
                pe.wait_ge(m_dve, M_DVE * k + 18)
                for t in range(NT):
                    ins = mm(bk(t // 4)[:, P * (t % 4):P * (t % 4) + P], sel[:, t, :], ln_t[:, :])
                    if t % 4 == 3:
                        ins.then_inc(m_pe, 1)

            pe.wait_ge(c_ready, C_STEPS)
            pe.wait_ge(w_loaded, 48)
            ternary()
            for stage in range(nst):
                layernorm(stage)
                if stage == 0:
                    project_qkv(0)
                    query_zero()
                    windowed_attention()
                    project_out(0)
                if stage in (1, 3):
                    ffn(stage // 2)
                if stage == 2:
                    recurrent()
                if stage == 4 or stage == 6:
                    project_qkv(stage // 2 - 1)
                    full_attention(stage // 2 - 1)
                    project_out(stage // 2 - 1)
                if stage == 5 or stage == 7:
                    moe(stage // 2 - 2)

        @block.scalar
        def _(act):
            def fn(o, i, f, **kw):
                return nc.scalar.activation(o, i, f, **kw)

            def layernorm(k):
                for c in range(NC):
                    act.wait_ge(ln_cent, NC * k + c + 1)
                    fn(xch(sq, c), xch(xc, c), ACT.Square).then_inc(ln_sq, 1)
                act.wait_ge(ln_var, k + 1)
                fn(ln_s[:, 0, :], bk(4)[:, 0:NT], ACT.Sqrt, bias=epsc[:, 0:1]).then_inc(ln_std, 1)

            def project_qkv(layer):
                if layer == 0:
                    act.wait_ge(xn_ready, NC)
                    for b in range(B):
                        act.copy(xwin[:, b, :, P - 1:P],
                                 xp[:, b, HALF:HALF + 1].unsqueeze(1).broadcast_to((P, WT, 1))).then_inc(win_ready, 1)
                for n, (i, _, cols, at) in enumerate(qk_chunks(layer), QK_BASE[layer]):
                    act.wait_ge(qk_mm, n + 1)
                    if n >= 2:
                        act.wait_ge(qk_out[n % 2], 16 * (n // 2))
                    o = parts[:, n % 2, :, 0:cols]
                    if layer == 0 and i == 1:
                        fn(kf[:, at:at + cols], bk(n % 2)[:, 0:cols], ACT.Copy).then_inc(kf_done, 1)
                    elif layer == 0 and at % QW == 0:
                        fn(q0f[:, at // QW:at // QW + 1], bk(n % 2)[:, 0:1], ACT.Copy).then_inc(q0_copied, 1)
                    fn(o[:, 0, :], bk(n % 2)[:, 0:cols], ACT.Copy).then_inc(part_act, 1)
                    act.wait_ge(part_dve, 2 * n + 1)
                    fn(o[:, 1, :], res[:, n % 2, 0:cols], ACT.Copy).then_inc(part_act, 1)
                for g, (t0, k) in enumerate(VCH[layer], V_BASE[layer]):
                    act.wait_ge(v_mm, g + 1)
                    src = bk(2 + g % 2)[:, 0:k * P].rearrange("p (t h d) -> p t h d", t=k, h=H)
                    if layer == 0:
                        fn(V[:, t0:t0 + k, :, 0:D], src, ACT.Copy)
                    fn(Vb[:, t0:t0 + k, :, 0:D], src, ACT.Copy).then_inc(v_out, 1)
                    act.wait_ge(v_dve, 2 * g + 1)
                    fn(Vb[:, t0:t0 + k, :, D:2 * D],
                       res[:, g % 2, 0:k * P].rearrange("p (t h d) -> p t h d", t=k, h=H), ACT.Copy).then_inc(v_out, 1)

            def query_zero():
                act.wait_ge(g0v, 3)
                for b in range(B):
                    for t in range(0, WT, 5):
                        k = min(5, WT - t)
                        n = min(k * QT, S - t * QT)
                        src = bk(3 * b + t // 5)[0:H, 0:n]
                        dst = s0[:, b, t:t + k, HALF:HALF + QT] if n == k * QT else s0[:, b, t, HALF:HALF + n]
                        if n == k * QT:
                            src = src.rearrange("p (t k) -> p t k", k=QT)
                        ins = fn(dst, src, ACT.Exp, bias=s0s[:, b, 1:2], scale=SCALE)
                    ins.then_inc(g0a, 1)

            def windowed_attention():
                act.wait_ge(g0v, 15)
                act.drain().then_inc(exp_done, 1)

                def slot(i, j):
                    u = i * RING_W + j
                    act.wait_ge(st_ready, u + 1)
                    act.wait_ge(pv_steps, u + 3)
                    fn(pt[:, j % 2, 0:5 * 2 * QT].rearrange("p (g c) -> p g c", g=2), wide[:, 3:5, 0:5 * QT],
                       ACT.Exp, scale=SCALE)
                    fn(pt[:, j % 2, 10 * QT:11 * QT], wide[:, 5, 0:QT], ACT.Exp, scale=SCALE).then_inc(exp_done, 1)

                with act.Fori(0, UNITS // RING_W) as i:
                    for j in range(RING_W):
                        slot(i, j)

            def full_attention(layer):
                st0 = ST_BASE[layer]

                def tile(n, j):
                    act.wait_ge(st_ready, st0 + n + 1)
                    act.wait_ge(pv_steps, st0 + n + 1)
                    fn(pt[:, j % 4, 0:S].rearrange("p (g c) -> p g c", g=2),
                       wide[:, 2 * (j % 2):2 * (j % 2) + 2, :], ACT.Exp, scale=SCALE).then_inc(exp_done, 1)

                with act.Fori(0, UNITS // 4) as i:
                    for j in range(4 * KT):
                        tile(i * (4 * KT) + j, j)

            def project_out(layer):
                n0 = AT_BASE[layer]
                if layer == 0:
                    for n, (b, t, k) in enumerate(QCH):
                        act.wait_ge(at_mm, n0 + n + 1)
                        c = min(k * QT, S - t * QT)
                        fn(aT[:, b * S + t * QT:b * S + t * QT + c], bk(n % 2)[:, 0:c], ACT.Copy).then_inc(at_out, 1)
                else:
                    for c in range(NC):
                        act.wait_ge(at_mm, n0 + c + 1)
                        fn(xch(aT, c), bk(c % 2), ACT.Copy).then_inc(at_out, 1)

            def recurrent():
                def r(ins):
                    ins.then_inc(r_act, 1)

                for c in range(NC):
                    act.wait_ge(xn_ready, NC * 2 + c + 1)
                    r(fn(rg[:, 0, 512 * c:512 * c + 512], xn(c), ACT.Gelu_apprx_tanh))
                for d in range(2):
                    p = "fb"[d]
                    for c in range(NC):
                        act.wait_ge(r_pe, 3 * NC * d + c + 1)
                        r(fn(rg[:, 1 + d, 512 * c:512 * c + 512], bk(c), ACT.Identity, bias=bcol(p + "_bx")))
                    for c in range(NC):
                        k = 2 * ((NC * d + c) % 2)
                        act.wait_ge(r_pe, 3 * NC * d + NC + 2 * c + 2)
                        r(fn(rb[:, 0, 512 * (NC * d + c):512 * (NC * d + c) + 512], bk(4 + k), ACT.Sigmoid, bias=bcol(p + "_bgx")))
                        r(fn(rb[:, 1, 512 * (NC * d + c):512 * (NC * d + c) + 512], bk(5 + k), ACT.Sigmoid, bias=bcol(p + "_bga")))
                for d in range(2):
                    for c in range(NC):
                        at = 512 * (NC * d + c)
                        act.wait_ge(r_dve, 2 * (NC * d + c) + 1)
                        r(fn(rc[:, at:at + 512], rb[:, 1, at:at + 512], ACT.Square))
                        act.wait_ge(r_act, R_SQ + 2 * (NC * d + c) + 1)
                        r(fn(rc[:, at:at + 512], rc[:, at:at + 512], ACT.Sqrt, scale=-1.0, bias=ones[:, 0:1]))
                for c in range(NC):
                    act.wait_ge(r_pe, 6 * NC + c + 1)
                    act.wait_ge(r_dve, R_HB)
                    r(fn(rg[:, 0, 512 * c:512 * c + 512], bk(c), ACT.Identity, scale=0.5, bias=eas[:, 3:4]))
                for c in range(NC):
                    act.wait_ge(r_dve, R_HB + c + 1)
                    r(fn(rb[:, 0, 512 * c:512 * c + 512], rg[:, 0, 512 * c:512 * c + 512], ACT.Gelu_apprx_tanh))

            def moe(k):
                act.wait_ge(m_dve, M_DVE * k + 2)
                fn(me[:, :, :], me[:, :, :], ACT.Exp).then_inc(m_act, 1)
                for c in range(NC):
                    act.wait_ge(m_pe, M_PE * k + 8 + c + 1)
                    fn(xch(mgb, c), bk(c), ACT.Copy).then_inc(m_act, 1)

            act.wait_ge(w_loaded, 48)
            act.wait_ge(c_ready, C_STEPS)
            fn(eas[:, 0:1], bcol("f_a"), ACT.Sigmoid).then_inc(ea_ready, 1)
            fn(eas[:, 1:2], bcol("b_a"), ACT.Sigmoid).then_inc(ea_ready, 1)
            for stage in range(nst):
                layernorm(stage)
                if stage == 0:
                    project_qkv(0)
                    query_zero()
                    windowed_attention()
                    project_out(0)
                if stage == 2:
                    recurrent()
                if stage == 4 or stage == 6:
                    project_qkv(stage // 2 - 1)
                    full_attention(stage // 2 - 1)
                    project_out(stage // 2 - 1)
                if stage == 5 or stage == 7:
                    moe(stage // 2 - 2)

        @block.vector
        def _(dve):
            def tt(o, a, b, op):
                return nc.vector.tensor_tensor(o, a, b, op)

            def layernorm(k):
                for c in range(NC):
                    dve.wait_ge(ln_mean, NC * k + c + 1)
                    tt(xch(xc, c), xch(x, c), bk(c), ALU.subtract).then_inc(ln_cent, 1)
                dve.wait_ge(ln_std, k + 1)
                nc.vector.reciprocal(ln_s[:, 1, :], ln_s[:, 0, :]).then_inc(ln_rstd, 1)
                dve.wait_ge(ln_rT, k + 1)
                nc.vector.tensor_copy(ln_t[:, :], bk(5)[0:NT, 0:P]).then_inc(ln_rTs, 1)
                for c in range(NC):
                    dve.wait_ge(ln_b, NC * k + c + 1)
                    dve.wait_ge(ln_cent, NC * k + c + 1)
                    tt(xn(c), xch(xc, c), bk(c), ALU.mult).then_inc(xn_ready, 1)

            def ternary():
                nc.vector.tensor_reduce(ts_[:, 0:1], w("tern"), AX.X, ALU.add,
                                        apply_absolute_value=True).then_inc(tw, 1)
                dve.wait_ge(tw_sum, 1)
                nc.vector.tensor_scalar(ts_[:, 1:2], bk(6)[:, 0:1], 1.0 / (P * P), 0.7,
                                        ALU.mult, ALU.mult).then_inc(tw, 1)
                dve.wait_ge(tw, 2)
                nc.vector.tensor_scalar(ts_[:, 2:3], ts_[:, 1:2], -1.0, None, ALU.mult).then_inc(tw, 1)
                dve.wait_ge(tw, 3)
                nc.vector.tensor_scalar(tg[:, 0, :], w("tern"), ts_[:, 1:2], bcol("alpha"), ALU.is_gt, ALU.mult)
                nc.vector.tensor_scalar(tg[:, 1, :], w("tern"), ts_[:, 2:3], bcol("alpha"), ALU.is_lt,
                                        ALU.mult).then_inc(tw, 1)
                dve.wait_ge(tw, 4)
                tt(tern[:, :], tg[:, 0, :], tg[:, 1, :], ALU.subtract).then_inc(tw, 1)

            def project_qkv(layer):
                if layer == 0:
                    for b in range(B):
                        dve.wait_ge(xn_ready, NC)
                        for t in range(WT):
                            ins = nc.vector.tensor_copy(xwin[:, b, t, 0:P - 1], xp[:, b, QT * t:QT * t + P - 1])
                    ins.then_inc(win_ready, 1)
                for n, (i, _, cols, _) in enumerate(qk_chunks(layer), QK_BASE[layer]):
                    src, o, r = bk(n % 2)[:, 0:cols], parts[:, n % 2, :, 0:cols], res[:, n % 2, 0:cols]
                    dve.wait_ge(part_act, 2 * n + 1)
                    tt(r, src, o[:, 0, :], ALU.subtract).then_inc(part_dve, 1)
                    dve.wait_ge(part_act, 2 * n + 2)
                    tt(o[:, 2, :], r, o[:, 1, :], ALU.subtract).then_inc(part_dve, 1)
                for g, (t0, k) in enumerate(VCH[layer], V_BASE[layer]):
                    v = Vb[:, t0:t0 + k, :, :]
                    src = bk(2 + g % 2)[:, 0:k * P].rearrange("p (t h d) -> p t h d", t=k, h=H)
                    r = res[:, g % 2, 0:k * P].rearrange("p (t h d) -> p t h d", t=k, h=H)
                    dve.wait_ge(v_out, 2 * g + 1)
                    tt(r, src, v[:, :, :, 0:D], ALU.subtract).then_inc(v_dve, 1)
                    dve.wait_ge(v_out, 2 * g + 2)
                    tt(v[:, :, :, 2 * D:3 * D], r, v[:, :, :, D:2 * D], ALU.subtract).then_inc(v_dve, 1)

            def query_zero():
                dve.wait_ge(q0_copied, B)
                for b in range(B):
                    ins = nc.vector.tensor_scalar(q0m[:, b, :], hmask[:, :], q0f[:, b:b + 1], None, ALU.mult)
                ins.then_inc(g0v, 1)
                for b in range(B):
                    dve.wait_ge(g0, b + 1)
                    for t in range(0, WT, 5):
                        c = min(5 * QT, S - t * QT)
                        ins = nc.vector.tensor_reduce(q0x[:, b, t // 5:t // 5 + 1],
                                                      bk(3 * b + t // 5)[0:H, 0:c], AX.X, ALU.max)
                    ins.then_inc(q0_max, 1)
                    dve.wait_ge(q0_max, 1 + 2 * b)
                    nc.vector.tensor_reduce(s0s[:, b, 0:1], q0x[:, b, :], AX.X, ALU.max).then_inc(q0_max, 1)
                    dve.wait_ge(q0_max, 2 + 2 * b)
                    nc.vector.tensor_scalar(s0s[:, b, 1:2], s0s[:, b, 0:1], -SCALE, None, ALU.mult).then_inc(g0v, 1)
                dve.wait_ge(g0, 3)
                nc.vector.tensor_copy(s0t[:, :, :, :].rearrange("p b t h -> p (b t h)"),
                                      bk(6)[:, 0:B * WT * H]).then_inc(g0v, 1)
                dve.wait_ge(g0, 4)
                k = 4
                for b in range(B):
                    tt(o0[:, b, :, :], bk(7)[0:H, 160 * b:160 * b + H * (D + 1)].rearrange("p (h d) -> p h d", h=H),
                       hmaskT[:, :, :], ALU.mult).then_inc(g0v, 1)
                    dve.wait_ge(g0v, k + 1)
                    nc.vector.tensor_reduce(o0s[:, b, :], o0[:, b, :, :].rearrange("p h d -> p d h"), AX.X,
                                            ALU.add).then_inc(g0v, 1)
                    dve.wait_ge(g0v, k + 2)
                    nc.vector.reciprocal(s0s[:, b, 2:3], o0s[:, b, D:D + 1]).then_inc(g0v, 1)
                    dve.wait_ge(g0v, k + 3)
                    nc.vector.tensor_scalar(o0s[:, b, 0:D], o0s[:, b, 0:D], s0s[:, b, 2:3], None,
                                            ALU.mult).then_inc(g0v, 1)
                    dve.wait_ge(g0v, k + 4)
                    tt(z0[:, b, :, :], hmaskT[:, :, 0:D], o0s[:, b, 0:D].unsqueeze(1).broadcast_to((H, H, D)),
                       ALU.mult).then_inc(g0v, 1)
                    k += 5
                dve.wait_ge(g0, 5)
                nc.vector.tensor_copy(q0o[:, :], bk(6)[:, 400:400 + B]).then_inc(g0v, 1)

            def split_maximum(g, rows, cols, j):
                dve.wait_ge(mt_ready, g + 1)
                src, o, r = bk(7)[0:rows, 0:cols], mp[0:rows, j, :, 0:cols], mres[0:rows, 0:cols]
                nc.vector.tensor_copy(o[:, 0, :], src).then_inc(split, 1)
                dve.wait_ge(split, 4 * g + 5)
                tt(r, src, o[:, 0, :], ALU.subtract).then_inc(split, 1)
                dve.wait_ge(split, 4 * g + 6)
                nc.vector.tensor_copy(o[:, 1, :], r).then_inc(split, 1)
                dve.wait_ge(split, 4 * g + 7)
                tt(o[:, 2, :], r, o[:, 1, :], ALU.subtract).then_inc(split, 1)

            def remainder(slot, a, b):
                tt(lo[:, slot, a:b], pt[:, slot, a:b], pth[:, slot, a:b], ALU.subtract).then_inc(lo_dve, 1)

            def divide(g, q, tiles, t0, h, eps):
                src = bk(6)[0:q, 0:tiles * VC].rearrange("p (t d) -> p t d", d=VC)
                nc.vector.tensor_scalar(den[0:q, 0:tiles], src[:, :, 3 * D], eps, None, ALU.add).then_inc(evac, 1)
                nc.vector.tensor_reduce(num[0:q, 0:tiles, :], src[:, :, 0:3 * D].rearrange("p t (n d) -> p t d n", d=D),
                                        AX.X, ALU.add).then_inc(evac, 1)
                dve.wait_ge(evac, 4 * g + 5)
                nc.vector.reciprocal(rden[0:q, 0:tiles], den[0:q, 0:tiles]).then_inc(evac, 1)
                dve.wait_ge(evac, 4 * g + 7)
                tt(A[0:q, t0:t0 + tiles, bass.ds(h * D, D)], num[0:q, 0:tiles, :],
                   rden[0:q, 0:tiles].unsqueeze(2).broadcast_to((q, tiles, D)), ALU.mult).then_inc(evac, 1)

            def windowed_attention():
                dve.wait_ge(g0v, 15)
                dve.drain().then_inc(sm_read, 1)
                dve.drain().then_inc(split, 4)
                dve.drain().then_inc(evac, 4)

                def maxima(u, j):
                    dve.wait_ge(sm_ready, u + 1)
                    nc.vector.tensor_reduce(nm[0:QT, j, 0:WT],
                                            wide[0:QT, 0:3, :].rearrange("p g (t k) -> p (g t) k", k=P)[:, 0:WT, :],
                                            AX.X, ALU.max, negate=True).then_inc(sm_read, 1)

                for u in range(3):
                    maxima(u, u)
                for u in range(2):
                    split_maximum(u, WT, QT, u)

                def slot(i, j, last):
                    s = i * RING_W + j
                    if not last or j + 3 < RING_W:
                        maxima(s + 3, (j + 3) % RING_W)
                    if not last or j + 2 < RING_W:
                        k = (j + 2) % RING_W
                        split_maximum(s + 2, WT, QT, k)
                    dve.wait_ge(exp_done, s + 2)
                    remainder(j % 2, LO_W, QW)
                    dve.wait_ge(pv_steps, s + 5)
                    divide(s, QT, WT, (j % B) * WT, i * (RING_W // B) + j // B, 0.0)

                with dve.Fori(0, UNITS // RING_W - 1) as i:
                    for j in range(RING_W):
                        slot(i, j, False)
                for j in range(RING_W):
                    slot(UNITS // RING_W - 1, j, True)

            def full_attention(layer):
                u0, st0, sm0 = layer * UNITS, ST_BASE[layer], SM_BASE[layer]
                use0 = (layer - 1) * (UNITS // RING_F)
                eps = DEN_EPS if layer == 1 else 0.0

                def maxima(u, t):
                    for y in range(2):
                        n = sm0 + (u * KT + t) * 2 + y
                        dve.wait_ge(sm_ready, n + 1)
                        nc.vector.tensor_reduce(mx[:, t, y:y + 1], bk(4 + y), AX.X, ALU.max).then_inc(sm_read, 1)

                def collect(u, j):
                    dve.wait_ge(sm_read, sm0 + (u + 1) * KT * 2 + 1)
                    nc.vector.tensor_reduce(nm[:, j, 0:KT], mx[:, :, :], AX.X, ALU.max,
                                            negate=True).then_inc(nm_ready, 1)
                    dve.wait_ge(nm_ready, u0 - UNITS + u + 1)

                for t in range(KT):
                    maxima(0, t)
                collect(0, 0)
                for t in range(KT):
                    maxima(1, t)
                collect(1, 1)
                split_maximum(u0, KT, P, 0)

                def slot(i, j, last):
                    s = i * RING_F + j
                    for t in range(KT):
                        dve.wait_ge(exp_done, st0 + s * KT + t + 2)
                        remainder(t % 4, LO_F, S)
                        if not last or j + 2 < RING_F:
                            maxima(s + 2, t)
                        if t == 1 and (not last or j + 1 < RING_F):
                            k = (j + 1) % RING_F
                            split_maximum(u0 + s + 1, KT, P, k)
                    if not last or j + 2 < RING_F:
                        collect(s + 2, (j + 2) % RING_F)
                    dve.wait_ge(pv_steps, st0 + (s + 1) * KT + 4)
                    divide(u0 + s, P, KT, (j % B) * KT, i * (RING_F // B) + j // B, eps)

                with dve.Fori(0, UNITS // RING_F - 1) as i:
                    for j in range(RING_F):
                        slot(i, j, False)
                for j in range(RING_F):
                    slot(UNITS // RING_F - 1, j, True)

            def add_projection(layer, stage):
                if layer == 0:
                    dve.wait_ge(at_out, AT_BASE[1])
                    nc.vector.tensor_copy(aT[:, 0:N].rearrange("p (b s) -> p b s", b=B)[:, :, 0:1],
                                          q0o[:, :].unsqueeze(2)).then_inc(g0v, 1)
                for c in range(NC):
                    dve.wait_ge(o_mm, NC * layer + c + 1)
                    if layer == 1:
                        nc.vector.scalar_tensor_tensor(xch(x, c), bk(2 + c), bcol("bo"), xch(x, c), ALU.add,
                                                       ALU.add).then_inc(x_new, 1)
                    else:
                        tt(xch(x, c), bk(2 + c), xch(x, c), ALU.add).then_inc(x_new, 1)

            def ffn(k):
                for c in range(NC):
                    dve.wait_ge(f_mm, NC * k + c + 1)
                    nc.vector.scalar_tensor_tensor(xch(x, c), bk(4 + c), bcol("ffn_b"), xch(x, c), ALU.add,
                                                   ALU.add).then_inc(x_new, 1)

            def recurrent():
                n = [0]

                def r(ins):
                    n[0] += 1
                    ins.then_inc(r_dve, 1)

                dve.wait_ge(ea_ready, 2)
                for d in range(2):
                    for c in range(NC):
                        at = 512 * (NC * d + c)
                        dve.wait_ge(r_act, R_G[d] + 2 * c + 2)
                        a = rb[:, 1, at:at + 512]
                        r(nc.vector.tensor_scalar(a, a, eas[:, d:d + 1], None, ALU.mult))
                        g = rb[:, 0, at:at + 512]
                        r(tt(g, g, rg[:, 1 + d, 512 * c:512 * c + 512], ALU.mult))
                for d in range(2):
                    for c in range(NC):
                        at = 512 * (NC * d + c)
                        dve.wait_ge(r_act, R_SQ + 2 * (NC * d + c) + 2)
                        dve.wait_ge(r_dve, 2 * (NC * d + c) + 2)
                        g = rb[:, 0, at:at + 512]
                        r(tt(g, g, rc[:, at:at + 512], ALU.mult))
                for d in range(2):
                    for b in range(B):
                        at = N * d + S * b
                        dve.wait_ge(r_dve, 2 * 2 * NC + 2 * NC)
                        a, g, h = rb[:, 1, at:at + S], rb[:, 0, at:at + S], rg[:, 1 + d, S * b:S * b + S]
                        if d:
                            a, g, h = a[:, ::-1], g[:, ::-1], h[:, ::-1]
                        r(nc.vector.tensor_tensor_scan(h, a, g, 0.0, ALU.mult, ALU.add))
                assert n[0] == R_SCAN, n[0]
                r(tt(eas[:, 2:3], bcol("f_bo"), bcol("b_bo"), ALU.add))
                dve.wait_ge(r_dve, n[0])
                r(nc.vector.tensor_scalar(eas[:, 3:4], eas[:, 2:3], 0.5, None, ALU.mult))
                assert n[0] == R_HB
                for c in range(NC):
                    dve.wait_ge(r_act, R_OUT + c + 1)
                    y = rg[:, 0, 512 * c:512 * c + 512]
                    r(tt(y, y, xn(c), ALU.add))
                for c in range(NC):
                    dve.wait_ge(r_pe, 7 * NC + c + 1)
                    y = rb[:, 1, 512 * c:512 * c + 512]
                    r(nc.vector.scalar_tensor_tensor(y, bk(4 + c), bcol("ld_b"), xn(c), ALU.add, ALU.add))
                    dve.wait_ge(r_dve, n[0])
                    tt(xch(x, c), y, xch(x, c), ALU.add).then_inc(x_new, 1)

            def moe(k):
                n = [0]

                def m(ins):
                    n[0] += 1
                    ins.then_inc(m_dve, 1)
                    dve.wait_ge(m_dve, M_DVE * k + n[0])

                logits = bk(0)[:, 0:NT * E].rearrange("p (t e) -> p t e", e=E)

                def wide8(t):
                    return t.unsqueeze(2).broadcast_to((P, NT, E))

                dve.wait_ge(m_pe, M_PE * k + 1)
                m(nc.vector.tensor_reduce(mst[:, 0, :], logits, AX.X, ALU.max))
                m(tt(me[:, :, :], logits, wide8(mst[:, 0, :]), ALU.subtract))
                dve.wait_ge(m_act, M_ACT * k + 1)
                m(nc.vector.tensor_reduce(mst[:, 1, :], me[:, :, :], AX.X, ALU.add))
                m(nc.vector.reciprocal(mst[:, 2, :], mst[:, 1, :]))
                m(tt(me[:, :, :], me[:, :, :], wide8(mst[:, 2, :]), ALU.mult))
                m(nc.vector.tensor_reduce(mst[:, 3, :], me[:, :, :], AX.X, ALU.max))
                m(tt(mw[:, :, :], me[:, :, :], wide8(mst[:, 3, :]), ALU.is_equal))
                m(tt(mw[:, :, :], mw[:, :, :], rank[:, :, :], ALU.mult))
                m(nc.vector.tensor_reduce(mst[:, 4, :], mw[:, :, :], AX.X, ALU.max))
                onehot = moh[:, :].rearrange("p (t e) -> p t e", e=E)
                m(tt(onehot, mw[:, :, :], wide8(mst[:, 4, :]), ALU.is_equal))
                dve.wait_ge(m_pe, M_PE * k + 7)
                m(nc.vector.tensor_copy(mt1[:, :, :], bk(2)[:, 0:P].rearrange("p (t e) -> p e t", e=E)))
                m(nc.vector.tensor_tensor_scan(mt2[:, :, :].rearrange("p e t -> p (e t)"),
                                               keep[:, :, :].rearrange("p e t -> p (e t)"),
                                               mt1[:, :, :].rearrange("p e t -> p (e t)"), 0.0, ALU.mult, ALU.add))
                m(tt(mt2[:, :, :], mt2[:, :, :], mt1[:, :, :], ALU.subtract))
                m(tt(mloc[:, :, :], bk(1)[:, 0:P].rearrange("p (t e) -> p t e", e=E),
                     mt2[:, :, :].rearrange("p e t -> p t e"), ALU.add))
                m(nc.vector.scalar_tensor_tensor(mloc[:, :, :], mloc[:, :, :], float(CAP), onehot, ALU.is_le, ALU.mult))
                m(nc.vector.tensor_reduce(mst[:, 5, :], mloc[:, :, :], AX.X, ALU.add))
                m(tt(mgate[:, :], mst[:, 5, :], mst[:, 3, :], ALU.mult))
                dve.wait_ge(m_pe, M_PE * k + 8)
                m(nc.vector.tensor_copy(ln_t[:, :], bk(3)[0:NT, 0:P]))
                assert n[0] == M_DVE, n[0]
                for c in range(NC):
                    dve.wait_ge(m_act, M_ACT * k + 2 + c)
                    y = xch(xc, c)
                    nc.vector.scalar_tensor_tensor(y, bk(4 + c), bcol("be"), xch(mgb, c), ALU.add,
                                                   ALU.mult).then_inc(m_y, 1)
                    dve.wait_ge(m_y, NC * k + c + 1)
                    tt(xch(x, c), y, xch(x, c), ALU.add).then_inc(x_new, 1)

            dve.wait_ge(w_loaded, 48)
            dve.wait_ge(c_ready, C_STEPS)
            ternary()
            for stage in range(nst):
                layernorm(stage)
                if stage == 0:
                    project_qkv(0)
                    query_zero()
                    windowed_attention()
                    add_projection(0, 0)
                if stage in (1, 3):
                    ffn(stage // 2)
                if stage == 2:
                    recurrent()
                if stage == 4 or stage == 6:
                    full = stage // 2 - 1
                    project_qkv(full)
                    full_attention(full)
                    add_projection(full, stage)
                if stage == 5 or stage == 7:
                    moe(stage // 2 - 2)


def kernel(**inputs):
    import concourse.bacc as bacc
    from concourse.bass_utils import run_bass_kernel_spmd

    a = {k: np.asarray(v) for k, v in inputs.items()}

    def rows(name):
        return a[name].transpose(1, 0, 2).reshape(P, P)

    rec = {f"{p}_{n}": a[f"L0_attn_b_{q}_W{m}"] for p, q in (("f", "fwd"), ("b", "bwd"))
           for n, m in (("x", "x"), ("gx", "gx"), ("ga", "ga"), ("o", "o"))}
    ws = {"wq0": a["L0_attn_a_Wq"].T, "wk0": a["L0_attn_a_Wk"].T, "wv0": a["L0_attn_a_Wv"].T,
          "wo0": a["L0_attn_a_Wo"].T, "ld": a["L0_attn_b_ld_W"], "tern": a["L0_ffn_weight"].T,
          "wq1": a["L1_attn_a_Wq"].T, "wk1": a["L1_attn_a_Wk"].T, "wv1": a["L1_attn_a_Wv"].T,
          "wo1": a["L1_attn_a_Wo"].T, "wq2": rows("L1_attn_b_W_query"), "wk2": rows("L1_attn_b_W_key"),
          "wv2": rows("L1_attn_b_W_val"), "wo2": a["L1_attn_b_W_out"].reshape(P, P), "we": a["L1_ffn_We"], **rec}
    bs = {f"{p}_{n}": a[f"L0_attn_b_{q}_{m}"] for p, q in (("f", "fwd"), ("b", "bwd"))
          for n, m in (("a", "a_logit"), ("bx", "bx"), ("bgx", "bgx"), ("bga", "bga"), ("bo", "bo"))}
    bs.update(ld_b=a["L0_attn_b_ld_b"], ffn_b=a["L0_ffn_bias"], bo=a["L1_attn_a_bo"], be=a["L1_ffn_be"],
              alpha=np.repeat(a["L0_ffn_alpha"], P))
    arrays = {
        "xT": np.ascontiguousarray(a["L0_attn_a_x"].reshape(N, P).T),
        "weights": np.ascontiguousarray(np.stack([ws[n] for n in W_NAMES], 1)),
        "biases": np.ascontiguousarray(np.stack([bs[n] for n in B_NAMES], 1)),
        "wg": np.ascontiguousarray(a["L1_ffn_Wg"]),
    }
    nc = bacc.Bacc("TRN2", target_bir_lowering=False, num_devices=1)
    aps = [nc.dram_tensor(n, v.shape, F32, kind="ExternalInput").ap() for n, v in arrays.items()]
    out = nc.dram_tensor("outT", (P, N), F32, kind="ExternalOutput").ap()
    build(nc, *aps, out)
    r = run_bass_kernel_spmd(nc, [arrays], core_ids=[0])
    return np.ascontiguousarray(r.results[0]["outT"].T).reshape(B, S, P)
```

```python
from contextlib import ExitStack

import numpy as np

import concourse.bass as bass
from concourse import mybir

ALU = mybir.AluOpType
ACT = mybir.ActivationFunctionType
AX = mybir.AxisListType
F32 = mybir.dt.float32
BF16 = mybir.dt.bfloat16
F16 = mybir.dt.float16

P = 128
B, S = 2, 1024
N = B * S
NC = N // 512
NT = N // P
H, D = 16, 8
NP = 9
R = NP * D
M0 = P - 3
SCALE = float(D) ** -0.5
LN_EPS = 1e-5
DEN_EPS = 1e-8
HALF = 16
QT = P - 1 - 2 * HALF
WT = -(-S // QT)
QW = WT * QT
KW = WT * P
PADW = HALF + QW + HALF + 3
E = 8
CAP = N // E
NEG = -1.0e30
UNITS = B * H
KT = S // P
VC = 3 * (D + 1)
LO_F = 11 * P // 2
RING_W, RING_F = 4, 4
LEAD = 5
BODY_W = B * RING_W

W_NAMES = ["wq0", "wk0", "wv0", "wo0", "f_x", "f_gx", "f_ga", "f_o", "b_x", "b_gx", "b_ga", "b_o", "ld",
           "tern", "wq1", "wk1", "wv1", "wo1", "wq2", "wk2", "wv2", "wo2", "we"]
B_NAMES = ["f_a", "f_bx", "f_bgx", "f_bga", "f_bo", "b_a", "b_bx", "b_bgx", "b_bga", "b_bo", "ld_b",
           "ffn_b", "bo", "be", "alpha"]
WI = {n: i for i, n in enumerate(W_NAMES)}
BI = {n: i for i, n in enumerate(B_NAMES)}


def build(nc, xT, weights, biases, wg, out, stages=8):
    with ExitStack() as ctx:
        def sb(name, shape, dt=F32):
            return ctx.enter_context(nc.sbuf_tensor(name, shape, dt))

        def sem(name):
            return ctx.enter_context(nc.semaphore(name))

        q_dram = nc.dram_tensor("q_dram", (P, 3, B * QW), BF16).ap()
        k_dram = nc.dram_tensor("k_dram", (3, P, B * KW), BF16).ap()

        bank = [ctx.enter_context(nc.psum_tensor(f"bank{i}", [P, 512], F32)) for i in range(2)]
        wide = ctx.enter_context(nc.psum_tensor("wide", [P, 6, 512], F32))

        def bk(i):
            return wide[:, i, :] if i < 6 else bank[i - 6][:, :]

        x = sb("x", [P, N])
        xcsq = sb("xcsq", [P, 2 * N])
        xc, sq = xcsq[:, 0:N], xcsq[:, N:2 * N]
        xp = sb("xp", [P, B, PADW])
        W = sb("W", [P, len(W_NAMES), P])
        bias = sb("bias", [P, len(B_NAMES)])
        wgs = sb("wgs", [P, E])
        ident = sb("ident", [P, P])
        identb = sb("identb", [P, P], BF16)
        ones = sb("ones", [P, P])
        meanw = sb("meanw", [P, P])
        tri = sb("tri", [P, P])
        epsc = sb("epsc", [P, 1])
        keep = sb("keep", [P, E, NT])
        rank = sb("rank", [P, NT, E])
        maskq = sb("maskq", [P, WT, P], BF16)
        maskk = sb("maskk", [P, WT, QT], BF16)
        hmask = sb("hmask", [P, H])
        hmaskT = sb("hmaskT", [H, H, D + 1])
        ln_s = sb("ln_s", [P, 2, NT])
        tern = sb("tern", [P, P])
        tg = sb("tg", [P, 2, P])
        ts_ = sb("ts_", [P, 4])
        eas = sb("eas", [P, 4])

        big = sb("big", [P, 7 * N])
        xwin = big[:, 0:B * KW].rearrange("p (b t k) -> p b t k", b=B, t=WT)
        kf = big[:, B * KW:2 * B * KW]
        V = sb("V", [P, B * WT, H, D + 1])
        o = 2 * B * KW
        A = big[:, o:o + B * WT * P].rearrange("p (t f) -> p t f", f=P)
        o += B * WT * P
        pt = big[:, o:o + 4 * 1056].rearrange("p (n c) -> p n c", n=4)
        aT = sq
        pth = big[:, o:o + 4 * 1056].bitcast(BF16).rearrange("p (n c two) -> p n c two", n=4, two=2)[:, :, :, 1]
        lo = kf.bitcast(F16)[:, 0:4 * 1056].rearrange("p (n c) -> p n c", n=4)
        Vb = sb("Vb", [P, B * WT, H, 3, D + 1], BF16)
        res = sb("res", [P, 2, 512])
        diag = res[:, :, :].rearrange("p n (t c) -> p n t c", c=P)
        parts = sb("parts", [P, 2, 3, 512], BF16)
        Ks = sb("Ks", [P, RING_W * B * KW], BF16)
        Qs = sb("Qs", [P, RING_W * B * QW], BF16)
        Kw, Qw = (a[:, :].rearrange("p (n c) -> p n c", n=RING_W) for a in (Ks, Qs))
        Kf, Qf = (a[:, 0:RING_F * S].rearrange("p (n c) -> p n c", n=RING_F) for a in (Ks, Qs))
        mx = sb("mx", [P, 2, KT, 2])
        nm = sb("nm", [P, RING_W, B * WT])
        mres = sb("mres", [B * WT, 2, P])
        mp = big[0:B * WT, o + 4 * 1056:o + 4 * 1056 + RING_W * 3 * P // 2].bitcast(BF16).rearrange(
            "p (u n c) -> p u n c", u=RING_W, n=3)
        num = sb("num", [P, 2, WT, D + 1])
        den = sb("den", [P, 2, WT])
        rden = sb("rden", [P, 2, WT])
        q0f = sb("q0f", [P, B])
        q0m = sb("q0m", [P, B, H])
        s0 = big[0:H, o:o + B * WT * P].rearrange("p (b t k) -> p b t k", b=B, t=WT)
        s0s = sb("s0s", [H, B, 4])
        s0t = sb("s0t", [P, B, WT, H])
        o0 = sb("o0", [H, B, H, D + 1])
        o0s = sb("o0s", [H, B, D + 1])
        z0 = sb("z0", [H, B, H, D])
        q0x = sb("q0x", [H, B, 3])
        q0o = sb("q0o", [P, B])
        rg = big[:, 0:3 * N].rearrange("p (n t) -> p n t", n=3)
        rb = big[:, 3 * N:7 * N].rearrange("p (n t) -> p n t", n=2)
        rc = xcsq
        mgb = big[:, 0:N]
        me = sb("me", [P, NT, E])
        mw = sb("mw", [P, NT, E])
        moh = sb("moh", [P, NT * E])
        mloc = sb("mloc", [P, NT, E])
        mt1 = sb("mt1", [P, E, NT])
        mt2 = sb("mt2", [P, E, NT])
        mst = sb("mst", [P, 6, NT])
        mgate = sb("mgate", [P, NT])

        x_loaded, w_loaded = sem("x_loaded"), sem("w_loaded")
        c_steps = sem("c_steps")
        ln_const, win_const, moe_const = sem("ln_const"), sem("win_const"), sem("moe_const")
        q0_const = sem("q0_const")
        tw = sem("tw")
        tw_sum = sem("tw_sum")
        ea_ready = sem("ea_ready")
        x_new = sem("x_new")
        ln_mean, ln_cent, ln_sq, ln_var = sem("ln_mean"), sem("ln_cent"), sem("ln_sq"), sem("ln_var")
        ln_std, ln_rstd, ln_diag = sem("ln_std"), sem("ln_rstd"), sem("ln_diag")
        ln_b, xn_ready = sem("ln_b"), sem("xn_ready")
        win_ready = sem("win_ready")
        qk_mm = sem("qk_mm")
        part_act = sem("part_act")
        part_dve = sem("part_dve")
        qk_out = [sem(f"qk_out{i}") for i in range(2)]
        v_mm, v_out = sem("v_mm"), sem("v_out")
        v_dve = sem("v_dve")
        lo_pool, lo_dve = sem("lo_pool"), sem("lo_dve")
        q0_copied, kf_done, q0_max = sem("q0_copied"), sem("kf_done"), sem("q0_max")
        aug_w = [sem(f"aug_w{i}") for i in range(RING_W)]
        aug_f = [sem(f"aug_f{i}") for i in range(RING_F)]
        mrow_w = [sem(f"mrow_w{i}") for i in range(RING_W)]
        mrow_f = [sem(f"mrow_f{i}") for i in range(RING_F)]
        st_ready = sem("st_ready")
        exp_done = sem("exp_done")
        sm_ready, sm_read = sem("sm_ready"), sem("sm_read")
        nm_ready = sem("nm_ready")
        mt_ready = sem("mt_ready")
        split_act = sem("split_act")
        split_dve = sem("split_dve")
        pv_steps = sem("pv_steps")
        evac = sem("evac")
        g0 = sem("g0")
        g0v = sem("g0v")
        g0a = sem("g0a")
        at_mm, at_out, o_mm = sem("at_mm"), sem("at_out"), sem("o_mm")
        f_mm = sem("f_mm")
        r_pe, r_act, r_dve, r_pool = sem("r_pe"), sem("r_act"), sem("r_dve"), sem("r_pool")
        m_pe, m_act, m_dve, m_y = sem("m_pe"), sem("m_act"), sem("m_dve"), sem("m_y")
        stored = sem("stored")

        def w(name):
            return W[:, WI[name], :]

        def bcol(name):
            return bias[:, BI[name]:BI[name] + 1]

        def xch(t, c):
            return t[:, 512 * c:512 * c + 512]

        def xn(c):
            b, o = c // 2, HALF + 512 * (c % 2)
            return xp[:, b, o:o + 512]

        def xnt(t):
            b, o = t // KT, HALF + P * (t % KT)
            return xp[:, b, o:o + P]

        QCH = [(b, t, min(5, WT - t)) for b in range(B) for t in range(0, WT, 5)]
        KCH = [(b, t, min(4, WT - t)) for b in range(B) for t in range(0, WT, 4)]

        def qk_chunks(layer):
            if layer == 0:
                for b, t, n in QCH:
                    yield 0, xp[:, b, HALF + t * QT:HALF + (t + n) * QT], n * QT, b * QW + t * QT
                for b, t, n in KCH:
                    yield 1, xwin[:, b, t:t + n, :], n * P, b * KW + t * P
            else:
                for i in range(2):
                    for c in range(NC):
                        yield i, xn(c), 512, 512 * c

        QK_BASE = [0] + [len(QCH) + len(KCH) + 2 * NC * i for i in range(3)]
        VCH = [[(b * WT + t, min(4, WT - t)) for b in range(B) for t in range(0, WT, 4)],
               [(4 * c, 4) for c in range(NC)], [(4 * c, 4) for c in range(NC)]]
        V_BASE = [0, len(VCH[0]), len(VCH[0]) + NC, len(VCH[0]) + 2 * NC]
        AT_BASE = [0, len(QCH), len(QCH) + NC]
        ST_BASE = [0, UNITS, UNITS + UNITS * KT]
        SM_BASE = [0, UNITS, UNITS + UNITS * KT * 2]
        G_BASE = [0, H, H + UNITS]

        nst = min(stages, 8)
        LN_MEAN, LN_STD = (0, 1, 0, 1), (2, 0, 2, 1)
        R_U, R_G = [NC, 4 * NC], [2 * NC, 5 * NC]
        R_SQ = 7 * NC
        R_OUT = R_SQ + 4 * NC
        R_GELU2 = R_OUT + NC
        R_SCAN = 6 * NC + 2 * B
        R_HB = R_SCAN + 2
        M_PE, M_ACT, M_DVE = 3 + 2 * NC, 1 + NC, 17 + NC

        block = ctx.enter_context(nc.Block())

        @block.sync
        def _(sp):
            for c in range(NC):
                sp.dma_start(xch(x, c), xT[:, 512 * c:512 * c + 512]).then_inc(x_loaded, 16)
                sp.wait_ge(x_loaded, 16 * (c + 1))
            sp.dma_start(W[:, :, :], weights).then_inc(w_loaded, 16)
            sp.dma_start(bias[:, :], biases).then_inc(w_loaded, 16)
            sp.dma_start(wgs[:, :], wg).then_inc(w_loaded, 16)

            def store_parts(layer):
                for n, (i, _, cols, at) in enumerate(qk_chunks(layer), QK_BASE[layer]):
                    sp.wait_ge(part_dve, 2 * n + 2)
                    dst = (k_dram[:, :, at:at + cols].rearrange("a p c -> p a c") if i
                           else q_dram[:, :, at:at + cols])
                    sp.dma_start(dst, parts[:, n % 2, :, 0:cols]).then_inc(qk_out[n % 2], 16)

            def parts_stored(layer):
                n = QK_BASE[layer + 1]
                sp.wait_ge(qk_out[0], 16 * ((n + 1) // 2))
                sp.wait_ge(qk_out[1], 16 * (n // 2))

            def load_operands(q, k, h, qcols, kcols, loaded):
                w = q.shape[1]
                rows = q_dram[bass.ds(h * D, D), :, qcols:qcols + w].rearrange("d i t -> (d i) t")
                sp.dma_start(q[0:R, :], rows.unsqueeze(0).broadcast_to((3, 3 * D, w))).then_inc(loaded, 16)
                w = k.shape[1]
                for j in range(3):
                    rows = k_dram[j, bass.ds(h * D, D), kcols:kcols + w]
                    sp.dma_start(k[j * 24:j * 24 + 24, :],
                                 rows.unsqueeze(1).broadcast_to((D, 3, w))).then_inc(loaded, 16)

            def place_maximum(g, q, n, qt, slot, rows):
                sp.wait_ge(split_dve, 2 * g + 4)
                for i in range(3):
                    sp.dma_start(q[M0 + i:M0 + i + 1, slot, 0:n * qt], mp[0:n, slot, i, 0:qt]).then_inc(rows, 16)

            def windowed_attention():
                def load(h, slot):
                    load_operands(Qw[:, slot, :], Kw[:, slot, :], h, 0, 0, aug_w[slot])

                def place(h, slot):
                    place_maximum(h, Qw, B * WT, QT, slot, mrow_w[slot])

                for h in range(RING_W):
                    load(h, h)
                for h in range(2):
                    place(h, h)

                def head(i, j, last):
                    h = i * RING_W + j
                    if not last:
                        sp.wait_ge(st_ready, B * h + B)
                        load(i * RING_W + (RING_W + j), j)
                    if not last or j + 2 < RING_W:
                        place(h + 2, (j + 2) % RING_W)

                with sp.Fori(0, H // RING_W - 1) as i:
                    for j in range(RING_W):
                        head(i, j, False)
                for j in range(RING_W):
                    head(H // RING_W - 1, j, True)

            def full_attention(layer):
                def load(h, b, slot):
                    load_operands(Qf[:, slot, :], Kf[:, slot, :], h, b * S, b * S, aug_f[slot])

                def place(u, slot):
                    place_maximum(G_BASE[layer] + u, Qf, KT, P, slot, mrow_f[slot])

                for u in range(RING_F):
                    load(u // B, u % B, u)
                place(0, 0)

                def slot(i, j, last):
                    s = i * RING_F + j
                    if not last or j + 1 < RING_F:
                        place(s + 1, (j + 1) % RING_F)
                    if not last:
                        sp.wait_ge(st_ready, ST_BASE[layer] + (s + 1) * KT)
                        load(i * (RING_F // B) + (RING_F + j) // B, j % B, j)

                with sp.Fori(0, UNITS // RING_F - 1) as i:
                    for j in range(RING_F):
                        slot(i, j, False)
                for j in range(RING_F):
                    slot(UNITS // RING_F - 1, j, True)

            for stage in range(nst):
                if stage in (0, 4, 6):
                    layer = {0: 0, 4: 1, 6: 2}[stage]
                    store_parts(layer)
                    parts_stored(layer)
                    if layer == 0:
                        sp.wait_ge(win_const, 1)
                        windowed_attention()
                    else:
                        full_attention(layer)
            for c in range(NC):
                sp.wait_ge(x_new, NC * (nst - 1) + c + 1)
                sp.dma_start(out[:, 512 * c:512 * c + 512], xch(x, c)).then_inc(stored, 16)
            sp.wait_ge(stored, 16 * NC)

        @block.gpsimd
        def _(pool):
            n = [0]

            def step(ins):
                n[0] += 1
                ins.then_inc(c_steps, 1)
                pool.wait_ge(c_steps, n[0])

            def select(v, op, fill, base, pattern, cm):
                step(pool.affine_select(out=v, in_=v, compare_op=op, fill=fill, base=base, pattern=pattern,
                                        channel_multiplier=cm))

            step(pool.memset(meanw[:, :], 1.0 / P))
            step(pool.memset(epsc[:, :], LN_EPS))
            step(pool.memset(ones[:, :], 1.0))
            step(pool.memset(ident[:, :], 0.0))
            select(ident[:, :], ALU.not_equal, 1.0, 0, [[-1, P]], 1)
            step(pool.memset(xp[:, :, 0:HALF], 0.0))
            step(pool.memset(xp[:, :, HALF + S:PADW], 0.0))
            pool.drain().then_inc(ln_const, 1)
            step(pool.memset(V[:, :, :, D:D + 1], 1.0))
            step(pool.memset(Vb[:, :, :, 0, D:D + 1], 1.0))
            step(pool.memset(Vb[:, :, :, 1:3, D:D + 1], 0.0))
            step(pool.memset(hmask[:, :], 1.0))
            select(hmask[:, :], ALU.is_ge, 0.0, 0, [[-D, H]], 1)
            select(hmask[:, :], ALU.is_ge, 0.0, D - 1, [[D, H]], -1)
            step(pool.memset(hmaskT[:, :, :], 1.0))
            select(hmaskT[:, :, :], ALU.is_equal, 0.0, 0, [[-1, H], [0, D + 1]], 1)
            step(pool.memset(s0[:, :, :, :], 0.0))
            pool.drain().then_inc(q0_const, 1)
            step(pool.memset(Ks[:, :], 1.0))
            step(pool.memset(Qs[:, :], 0.0))
            step(pool.memset(identb[:, :], 0.0))
            select(identb[:, :], ALU.not_equal, 1.0, 0, [[-1, P]], 1)
            step(pool.memset(maskq[:, :, :], 0.0))
            select(maskq[:, :, 0:P - 1], ALU.is_ge, NEG, 0, [[0, WT], [1, P - 1]], -1)
            select(maskq[:, :, 0:P - 1], ALU.is_ge, NEG, 2 * HALF, [[0, WT], [-1, P - 1]], 1)
            select(maskq[:, :, 0:P - 1], ALU.is_gt, NEG, -HALF, [[QT, WT], [1, P - 1]], 0)
            select(maskq[:, :, 0:P - 1], ALU.is_gt, NEG, S + HALF, [[-QT, WT], [-1, P - 1]], 0)
            step(pool.memset(maskk[:, :, :], 0.0))
            select(maskk[:, :, :], ALU.is_ge, NEG, 0, [[0, WT], [-1, QT]], 1)
            select(maskk[:, :, :], ALU.is_ge, NEG, 2 * HALF, [[0, WT], [1, QT]], -1)
            select(maskk[:, :, :], ALU.is_gt, NEG, -HALF, [[QT, WT], [0, QT]], 1)
            select(maskk[:, :, :], ALU.is_gt, NEG, S + HALF, [[-QT, WT], [0, QT]], -1)
            select(maskk[:, :, :], ALU.is_gt, 0.0, P - 1, [[0, WT], [0, QT]], -1)
            pool.drain().then_inc(win_const, 1)
            step(pool.memset(tri[:, :], 1.0))
            select(tri[:, :], ALU.is_ge, 0.0, 0, [[1, P]], -1)
            step(pool.memset(keep[:, :, :], 1.0))
            step(pool.memset(keep[:, :, 0:1], 0.0))
            for e in range(E):
                step(pool.memset(rank[:, :, e:e + 1], float(E - e)))
            pool.drain().then_inc(moe_const, 1)

            def remainder(slot, n):
                pool.tensor_tensor(lo[:, slot, 0:n], pt[:, slot, 0:n], pth[:, slot, 0:n],
                                   ALU.subtract).then_inc(lo_pool, 1)

            if nst > 0:
                with pool.Fori(0, UNITS // BODY_W) as i:
                    for j in range(BODY_W):
                        pool.wait_ge(exp_done, i * BODY_W + j + 2)
                        remainder(j % 4, QW)
            for layer in (1, 2):
                if nst > 2 * layer + 2:
                    with pool.Fori(0, UNITS) as i:
                        for j in range(KT):
                            pool.wait_ge(exp_done, ST_BASE[layer] + i * KT + j + 2)
                            remainder(j % 4, LO_F)

        @block.tensor
        def _(pe):
            def mm(o, l, r, start=True, stop=True, **kw):
                return nc.tensor.matmul(o, l, r, start=start, stop=stop, **kw)

            def layernorm(k):
                def mean(c):
                    if k == 0:
                        pe.wait_ge(x_loaded, 16 * (c + 1))
                    else:
                        pe.wait_ge(x_new, NC * (k - 1) + c + 1)
                    if c >= 2:
                        pe.wait_ge(ln_cent, NC * k + c - 1)
                    mm(bk(LN_MEAN[c]), meanw[:, :], xch(x, c)).then_inc(ln_mean, 1)

                def variance(c):
                    pe.wait_ge(ln_sq, NC * k + c + 1)
                    if c:
                        pe.wait_ge(ln_std, NC * k + c)
                    for t in range(4 * c, 4 * c + 4):
                        ins = mm(bk(3)[:, t:t + 1], sq[:, P * t:P * t + P], meanw[:, 0:1])
                    ins.then_inc(ln_var, 1)

                def spread(c):
                    pe.wait_ge(ln_diag, NC * k + c + 1)
                    if c == 2:
                        pe.wait_ge(xn_ready, NC * k + 1)
                    mm(bk(LN_STD[c]), ones[:, :], res[:, c % 2, :]).then_inc(ln_b, 1)

                if k == 6:
                    pe.wait_ge(m_act, M_ACT)
                for step, c in ((mean, 0), (mean, 1), (variance, 0), (mean, 2), (variance, 1), (spread, 0),
                                (mean, 3), (variance, 2), (spread, 1), (variance, 3), (spread, 2), (spread, 3)):
                    step(c)

            def ternary():
                pe.wait_ge(tw, 1)
                mm(bk(6)[:, 0:1], ones[:, :], ts_[:, 0:1]).then_inc(tw_sum, 1)

            def project_qkv(layer):
                pe.wait_ge(xn_ready, NC * ({0: 0, 1: 4, 2: 6}[layer] + 1))
                if layer == 0:
                    pe.wait_ge(win_ready, 3)
                wn = ("wq%d" % layer, "wk%d" % layer)
                for n, (i, mov, cols, _) in enumerate(qk_chunks(layer), QK_BASE[layer]):
                    if n >= 2:
                        pe.wait_ge(part_dve, 2 * (n - 2) + 2)
                    mm(bk(n % 2)[:, 0:cols], w(wn[i]), mov).then_inc(qk_mm, 1)
                for g, (t0, k) in enumerate(VCH[layer], V_BASE[layer]):
                    if g >= 2:
                        pe.wait_ge(v_dve, 2 * g - 2)
                    for y in range(k):
                        t = t0 + y
                        lhs = xwin[:, t // WT, t % WT, :] if layer == 0 else xnt(t)
                        ins = mm(bk(2 + g % 2)[:, y * P:(y + 1) * P], lhs, w("wv%d" % layer))
                    ins.then_inc(v_mm, 1)

            def query_zero():
                pe.wait_ge(q0_const, 1)
                pe.wait_ge(g0v, 1)
                pe.wait_ge(v_dve, 2 * V_BASE[1])
                pe.wait_ge(part_dve, 2 * QK_BASE[1])
                for b in range(B):
                    for t in range(0, WT, 5):
                        k = min(5, WT - t)
                        cols = kf[:, b * KW + t * P:b * KW + (t + k) * P].rearrange("p (t k) -> p t k", k=P)
                        ins = mm(bk(3 * b + t // 5)[0:H, 0:k * QT].rearrange("p (t k) -> p t k", k=QT),
                                 q0m[:, b, :], cols[:, :, HALF:HALF + QT])
                    ins.then_inc(g0, 1)
                pe.wait_ge(g0a, 2)
                for b in range(B):
                    for t in range(WT):
                        ins = nc.tensor.transpose(bk(6)[:, (b * WT + t) * H:(b * WT + t + 1) * H],
                                                  s0[:, b, t, :], ident[0:H, 0:H])
                ins.then_inc(g0, 1)
                pe.wait_ge(g0v, 4)
                for b in range(B):
                    for t in range(WT):
                        ins = mm(bk(7)[0:H, 160 * b:160 * b + H * (D + 1)], s0t[:, b, t, :],
                                 V[:, b * WT + t, :, :].rearrange("p h d -> p (h d)"),
                                 start=(t == 0), stop=(t == WT - 1))
                ins.then_inc(g0, 1)
                pe.wait_ge(g0v, 14)
                for b in range(B):
                    ins = mm(bk(6)[:, 400 + b:401 + b], z0[:, b, :, :].rearrange("p h d -> p (h d)"),
                             ones[0:H, 0:1])
                ins.then_inc(g0, 1)

            def windowed_attention():
                pe.wait_ge(g0v, 15)
                pe.wait_ge(win_const, 1)
                pe.drain().then_inc(pv_steps, 4)

                def maxima(u, j):
                    pe.wait_ge(sm_read, u + 1)
                    k0, q0 = j % B * KW, j % B * QW
                    for t in range(0, WT, 4):
                        k = min(4, WT - t)
                        mm(bk(t // 4)[0:QT, 0:k * P], identb[0:QT, 0:QT],
                           maskq[0:QT, t:t + k, :].rearrange("p t k -> p (t k)"))
                        for y in range(t, t + k):
                            ins = mm(bk(t // 4)[0:QT, (y - t) * P:(y - t + 1) * P],
                                     Qw[0:M0, j // B, q0 + y * QT:q0 + (y + 1) * QT],
                                     Kw[0:M0, j // B, k0 + y * P:k0 + (y + 1) * P],
                                     start=False, stop=True, skip_group_check=True)
                    ins.then_inc(sm_ready, 1)

                def turn(h, slot):
                    pe.wait_ge(sm_read, B * h + B + 1)
                    pe.wait_ge(split_dve, 2 * h + 1)
                    nc.tensor.transpose(bk(7)[0:B * WT, 0:QT], nm[0:QT, slot, :],
                                        ident[0:QT, 0:QT]).then_inc(mt_ready, 1)

                def scores(u, j):
                    pe.wait_ge(exp_done, u + 1)
                    k0, q0 = j % B * KW, j % B * QW
                    for t in range(0, WT, 5):
                        k = min(5, WT - t)
                        mm(bk(3 + t // 5)[:, 0:k * QT], identb[:, :],
                           maskk[:, t:t + k, :].rearrange("p t k -> p (t k)"))
                        for y in range(t, t + k):
                            ins = mm(bk(3 + t // 5)[:, (y - t) * QT:(y - t + 1) * QT],
                                     Kw[:, j // B, k0 + y * P:k0 + (y + 1) * P],
                                     Qw[:, j // B, q0 + y * QT:q0 + (y + 1) * QT],
                                     start=False, stop=True, skip_group_check=True)
                    ins.then_inc(st_ready, 1)

                def values(u, j, h, b):
                    pe.wait_ge(lo_pool, u + 1)
                    pe.wait_ge(evac, 4 * u + 1)
                    for t in range(WT):
                        v = Vb[:, b * WT + t, bass.ds(h, 1), :, :].rearrange("p h n d -> p (h n d)")
                        o = bk(6)[0:QT, t * VC:(t + 1) * VC]
                        mm(o, pth[:, j % 4, t * QT:(t + 1) * QT], v, stop=False)
                        ins = mm(o, lo[:, j % 4, t * QT:(t + 1) * QT], v, start=False)
                    ins.then_inc(pv_steps, 1)

                for u in range(LEAD):
                    if u % B == 0:
                        pe.wait_ge(aug_w[u // B], 64)
                    maxima(u, u)
                for h in range(2):
                    turn(h, h)
                pe.wait_ge(mrow_w[0], 48)
                scores(0, 0)

                def unit(i, j, last):
                    u = i * BODY_W + j
                    left = BODY_W - j if last else UNITS
                    if left > 1:
                        n = j + 1
                        if n % B == 0:
                            pe.wait_ge(mrow_w[n // B % RING_W], 48 * (i + 1 + n // BODY_W))
                        scores(u + 1, n % BODY_W)
                    if j % B == 1 and left > 3:
                        turn(i * RING_W + (j // B + 2), (j // B + 2) % RING_W)
                    if left > LEAD:
                        n = j + LEAD
                        if n % B == 0:
                            pe.wait_ge(aug_w[n // B % RING_W], 64 * (i + 1 + n // BODY_W))
                        maxima(u + LEAD, n % BODY_W)
                    values(u, j, i * RING_W + j // B, j % B)

                with pe.Fori(0, UNITS // BODY_W - 1) as i:
                    for j in range(BODY_W):
                        unit(i, j, False)
                for j in range(BODY_W):
                    unit(UNITS // BODY_W - 1, j, True)

            def full_attention(layer):
                u0, st0, sm0 = layer * UNITS, ST_BASE[layer], SM_BASE[layer]
                use0 = (layer - 1) * (UNITS // RING_F)
                pe.wait_ge(v_dve, 2 * V_BASE[layer + 1])
                pe.wait_ge(part_dve, 2 * QK_BASE[layer + 1])

                def maxima(u, j, t):
                    for y in range(2):
                        pe.wait_ge(sm_read, sm0 + (u * KT + t) * 2 + y)
                        mm(bk(4 + y), Qf[0:M0, j, t * P:(t + 1) * P],
                           Kf[0:M0, j, 512 * y:512 * y + 512]).then_inc(sm_ready, 1)

                def turn(u, j):
                    pe.wait_ge(nm_ready, u0 - UNITS + u + 1)
                    pe.wait_ge(split_dve, 2 * (G_BASE[layer] + u) + 1)
                    nc.tensor.transpose(bk(7)[0:KT, 0:P], nm[:, j, 0:KT], ident[:, :]).then_inc(mt_ready, 1)

                def scores(u, j, t):
                    pe.wait_ge(exp_done, st0 + u * KT + t)
                    for y in range(2):
                        ins = mm(bk(2 * (t % 2) + y), Kf[:, j, t * P:(t + 1) * P],
                                 Qf[:, j, 512 * y:512 * y + 512])
                    ins.then_inc(st_ready, 1)

                def values(u, j, t, h, b):
                    n = st0 + u * KT + t
                    pe.wait_ge(lo_pool, n + 1)
                    pe.wait_ge(lo_dve, n - UNITS + 1)
                    if t == 0:
                        pe.wait_ge(evac, 4 * (u0 + u) + 1)
                    v = Vb[:, b * KT + t, bass.ds(h, 1), :, :].rearrange("p h n d -> p (h n d)")
                    for y in range(KT):
                        o = bk(6)[:, y * VC:(y + 1) * VC]
                        mm(o, pth[:, t % 4, y * P:(y + 1) * P], v, start=(t == 0 and y == 0), stop=False,
                           skip_group_check=True)
                        ins = mm(o, lo[:, t % 4, y * P:(y + 1) * P], v, start=False, stop=(t == KT - 1),
                                 skip_group_check=True)
                    ins.then_inc(pv_steps, 1)

                for u in range(2):
                    pe.wait_ge(aug_f[u], 64 * (use0 + 1))
                    for t in range(KT):
                        maxima(u, u, t)
                turn(0, 0)
                pe.wait_ge(mrow_f[0], 48 * (use0 + 1))
                scores(0, 0, 0)
                scores(0, 0, 1)

                def slot(i, j, last):
                    s = i * RING_F + j
                    nxt = not last or j + 1 < RING_F
                    smx = not last or j + 2 < RING_F
                    for t in range(KT):
                        if t < KT - 2:
                            scores(s, j, t + 2)
                        elif nxt:
                            if t == KT - 2:
                                pe.wait_ge(mrow_f[(j + 1) % RING_F], 48 * (use0 + i + 1 + (j + 1) // RING_F))
                            scores(s + 1, (j + 1) % RING_F, t + 2 - KT)
                        if smx:
                            if t == 0:
                                pe.wait_ge(aug_f[(j + 2) % RING_F], 64 * (use0 + i + 1 + (j + 2) // RING_F))
                            maxima(s + 2, (j + 2) % RING_F, t)
                        values(s, j, t, i * (RING_F // B) + j // B, j % B)
                        if t == 0 and nxt:
                            turn(s + 1, (j + 1) % RING_F)

                with pe.Fori(0, UNITS // RING_F - 1) as i:
                    for j in range(RING_F):
                        slot(i, j, False)
                for j in range(RING_F):
                    slot(UNITS // RING_F - 1, j, True)

            def project_out(layer):
                n0 = AT_BASE[layer]
                pe.wait_ge(evac, 4 * UNITS * (layer + 1) + 4)
                chunks = ([(b * WT + t, k, QT) for b, t, k in QCH] if layer == 0
                          else [(4 * c, 4, P) for c in range(NC)])
                for n, (t, k, q) in enumerate(chunks):
                    if n >= 2:
                        pe.wait_ge(at_out, n0 + n - 1)
                    for y in range(k):
                        ins = nc.tensor.transpose(bk(n % 2)[:, y * q:(y + 1) * q], A[0:q, t + y, :], ident[0:q, 0:q])
                    ins.then_inc(at_mm, 1)
                pe.wait_ge(at_out, n0 + len(chunks))
                if layer == 0:
                    pe.wait_ge(g0v, 16)
                for c in range(NC):
                    mm(bk(4 + c), w("wo%d" % layer), xch(aT, c)).then_inc(o_mm, 1)

            def ffn(k):
                pe.wait_ge(tw, 5)
                for c in range(NC):
                    pe.wait_ge(xn_ready, NC * (1 + 2 * k) + c + 1)
                    mm(bk(4 + c), tern[:, :], xn(c)).then_inc(f_mm, 1)

            def recurrent():
                pe.wait_ge(xn_ready, NC * 3)
                n = 0
                for d in range(2):
                    p = "fb"[d]
                    for c in range(NC):
                        if d == 0:
                            pe.wait_ge(r_act, c + 1)
                        else:
                            pe.wait_ge(r_act, R_U[0] + c + 1)
                        mm(bk(c), w(p + "_x"), rg[:, 0, 512 * c:512 * c + 512]).then_inc(r_pe, 1)
                    for c in range(NC):
                        pe.wait_ge(r_act, R_U[d] + c + 1)
                        if n >= 2:
                            pe.wait_ge(r_act, R_G[(n - 2) // NC] + 2 * ((n - 2) % NC) + 2)
                        u = rg[:, 1 + d, 512 * c:512 * c + 512]
                        mm(bk(4 + 2 * (n % 2)), w(p + "_gx"), u).then_inc(r_pe, 1)
                        mm(bk(5 + 2 * (n % 2)), w(p + "_ga"), u).then_inc(r_pe, 1)
                        n += 1
                pe.wait_ge(r_dve, R_SCAN)
                for c in range(NC):
                    mm(bk(c), w("f_o"), rg[:, 1, 512 * c:512 * c + 512], stop=False)
                    mm(bk(c), w("b_o"), rg[:, 2, 512 * c:512 * c + 512], start=False).then_inc(r_pe, 1)
                for c in range(NC):
                    pe.wait_ge(r_act, R_GELU2 + c + 1)
                    mm(bk(4 + c), w("ld"), rb[:, 0, 512 * c:512 * c + 512]).then_inc(r_pe, 1)

            def moe(k):
                pe.wait_ge(xn_ready, NC * (6 + 2 * k))
                for t in range(NT):
                    ins = mm(bk(0)[:, t * E:(t + 1) * E], xnt(t), wgs[:, :])
                ins.then_inc(m_pe, 1)
                for c in range(NC):
                    mm(bk(4 + c), w("we"), xn(c)).then_inc(m_pe, 1)
                pe.wait_ge(moe_const, 1)
                pe.wait_ge(m_dve, M_DVE * k + 10)
                mm(bk(1)[:, 0:P], tri[:, :], moh[:, :]).then_inc(m_pe, 1)
                mm(bk(2)[:, 0:P], ones[:, :], moh[:, :]).then_inc(m_pe, 1)
                for c in range(NC):
                    pe.wait_ge(m_dve, M_DVE * k + 17 + c + 1)
                    mm(bk(c), ones[:, :], res[:, c % 2, :]).then_inc(m_pe, 1)

            pe.wait_ge(ln_const, 1)
            for stage in range(nst):
                layernorm(stage)
                if stage == 0:
                    pe.wait_ge(w_loaded, 48)
                    project_qkv(0)
                    ternary()
                    query_zero()
                    windowed_attention()
                    project_out(0)
                if stage in (1, 3):
                    ffn(stage // 2)
                if stage == 2:
                    recurrent()
                if stage == 4 or stage == 6:
                    project_qkv(stage // 2 - 1)
                    full_attention(stage // 2 - 1)
                    project_out(stage // 2 - 1)
                if stage == 5 or stage == 7:
                    moe(stage // 2 - 2)

        @block.scalar
        def _(act):
            def fn(o, i, f, **kw):
                return nc.scalar.activation(o, i, f, **kw)

            def layernorm(k):
                def root(c):
                    act.wait_ge(ln_var, NC * k + c + 1)
                    fn(ln_s[:, 0, 4 * c:4 * c + 4], bk(3)[:, 4 * c:4 * c + 4], ACT.Sqrt,
                       bias=epsc[:, 0:1]).then_inc(ln_std, 1)

                for c in range(NC):
                    act.wait_ge(ln_cent, NC * k + c + 1)
                    fn(xch(sq, c), xch(xc, c), ACT.Square).then_inc(ln_sq, 1)
                    if c > 0:
                        root(c - 1)
                root(NC - 1)

            def project_qkv(layer):
                if layer == 0:
                    act.wait_ge(xn_ready, NC)
                    for b in range(B):
                        act.copy(xwin[:, b, :, P - 1:P],
                                 xp[:, b, HALF:HALF + 1].unsqueeze(1).broadcast_to((P, WT, 1))).then_inc(win_ready, 1)
                for n, (i, _, cols, at) in enumerate(qk_chunks(layer), QK_BASE[layer]):
                    act.wait_ge(qk_mm, n + 1)
                    if n >= 2:
                        act.wait_ge(qk_out[n % 2], 16 * (n // 2))
                    o = parts[:, n % 2, :, 0:cols]
                    if layer == 0 and i == 1:
                        fn(kf[:, at:at + cols], bk(n % 2)[:, 0:cols], ACT.Copy).then_inc(kf_done, 1)
                    elif layer == 0 and at % QW == 0:
                        fn(q0f[:, at // QW:at // QW + 1], bk(n % 2)[:, 0:1], ACT.Copy).then_inc(q0_copied, 1)
                    fn(o[:, 0, :], bk(n % 2)[:, 0:cols], ACT.Copy).then_inc(part_act, 1)
                    act.wait_ge(part_dve, 2 * n + 1)
                    fn(o[:, 1, :], res[:, n % 2, 0:cols], ACT.Copy).then_inc(part_act, 1)
                for g, (t0, k) in enumerate(VCH[layer], V_BASE[layer]):
                    act.wait_ge(v_mm, g + 1)
                    src = bk(2 + g % 2)[:, 0:k * P].rearrange("p (t h d) -> p t h d", t=k, h=H)
                    if layer == 0:
                        fn(V[:, t0:t0 + k, :, 0:D], src, ACT.Copy)
                    fn(Vb[:, t0:t0 + k, :, 0, 0:D], src, ACT.Copy).then_inc(v_out, 1)
                    act.wait_ge(v_dve, 2 * g + 1)
                    fn(Vb[:, t0:t0 + k, :, 1, 0:D],
                       res[:, g % 2, 0:k * P].rearrange("p (t h d) -> p t h d", t=k, h=H), ACT.Copy).then_inc(v_out, 1)

            def query_zero():
                act.wait_ge(g0v, 3)
                for b in range(B):
                    for t in range(0, WT, 5):
                        k = min(5, WT - t)
                        n = min(k * QT, S - t * QT)
                        src = bk(3 * b + t // 5)[0:H, 0:n]
                        dst = s0[:, b, t:t + k, HALF:HALF + QT] if n == k * QT else s0[:, b, t, HALF:HALF + n]
                        if n == k * QT:
                            src = src.rearrange("p (t k) -> p t k", k=QT)
                        ins = fn(dst, src, ACT.Exp, bias=s0s[:, b, 1:2], scale=SCALE)
                    ins.then_inc(g0a, 1)

            def split_part(g, rows, cols, j, step):
                o = mp[0:rows, j, step, 0:cols]
                if step == 0:
                    act.wait_ge(mt_ready, g + 1)
                    fn(o, bk(7)[0:rows, 0:cols], ACT.Copy).then_inc(split_act, 1)
                else:
                    act.wait_ge(split_dve, 2 * g + 3)
                    fn(o, mres[0:rows, j % 2, 0:cols], ACT.Copy).then_inc(split_act, 1)

            def windowed_attention():
                act.wait_ge(g0v, 15)
                act.drain().then_inc(exp_done, 1)
                for h in range(2):
                    for step in range(2):
                        split_part(h, B * WT, QT, h, step)

                def unit(i, j, last):
                    u = i * BODY_W + j
                    act.wait_ge(st_ready, u + 1)
                    act.wait_ge(pv_steps, u + 1)
                    fn(pt[:, j % 4, 0:5 * 2 * QT].rearrange("p (g c) -> p g c", g=2), wide[:, 3:5, 0:5 * QT],
                       ACT.Exp, scale=SCALE)
                    fn(pt[:, j % 4, 10 * QT:11 * QT], wide[:, 5, 0:QT], ACT.Exp, scale=SCALE).then_inc(exp_done, 1)
                    if j % B == 1 and not (last and BODY_W - j <= 3):
                        for step in range(2):
                            split_part(i * RING_W + (j // B + 2), B * WT, QT, (j // B + 2) % RING_W, step)

                with act.Fori(0, UNITS // BODY_W - 1) as i:
                    for j in range(BODY_W):
                        unit(i, j, False)
                for j in range(BODY_W):
                    unit(UNITS // BODY_W - 1, j, True)

            def full_attention(layer):
                st0, g0 = ST_BASE[layer], G_BASE[layer]
                for step in range(2):
                    split_part(g0, KT, P, 0, step)

                def unit(i, j, last):
                    s = i * RING_F + j
                    for t in range(KT):
                        n = st0 + s * KT + t
                        act.wait_ge(st_ready, n + 1)
                        act.wait_ge(pv_steps, n + 1)
                        fn(pt[:, t % 4, 0:S].rearrange("p (g c) -> p g c", g=2),
                           wide[:, 2 * (t % 2):2 * (t % 2) + 2, :], ACT.Exp, scale=SCALE).then_inc(exp_done, 1)
                        if t in (1, 3) and (not last or j + 1 < RING_F):
                            split_part(g0 + s + 1, KT, P, (j + 1) % RING_F, t // 2)

                with act.Fori(0, UNITS // RING_F - 1) as i:
                    for j in range(RING_F):
                        unit(i, j, False)
                for j in range(RING_F):
                    unit(UNITS // RING_F - 1, j, True)

            def project_out(layer):
                n0 = AT_BASE[layer]
                if layer == 0:
                    for n, (b, t, k) in enumerate(QCH):
                        act.wait_ge(at_mm, n0 + n + 1)
                        c = min(k * QT, S - t * QT)
                        fn(aT[:, b * S + t * QT:b * S + t * QT + c], bk(n % 2)[:, 0:c], ACT.Copy).then_inc(at_out, 1)
                else:
                    for c in range(NC):
                        act.wait_ge(at_mm, n0 + c + 1)
                        fn(xch(aT, c), bk(c % 2), ACT.Copy).then_inc(at_out, 1)

            def recurrent():
                def r(ins):
                    ins.then_inc(r_act, 1)

                for c in range(NC):
                    act.wait_ge(xn_ready, NC * 2 + c + 1)
                    r(fn(rg[:, 0, 512 * c:512 * c + 512], xn(c), ACT.Gelu_apprx_tanh))
                fn(eas[:, 0:1], bcol("f_a"), ACT.Sigmoid).then_inc(ea_ready, 1)
                fn(eas[:, 1:2], bcol("b_a"), ACT.Sigmoid).then_inc(ea_ready, 1)
                for d in range(2):
                    p = "fb"[d]
                    for c in range(NC):
                        act.wait_ge(r_pe, 3 * NC * d + c + 1)
                        r(fn(rg[:, 1 + d, 512 * c:512 * c + 512], bk(c), ACT.Identity, bias=bcol(p + "_bx")))
                    for c in range(NC):
                        k = 2 * ((NC * d + c) % 2)
                        act.wait_ge(r_pe, 3 * NC * d + NC + 2 * c + 2)
                        r(fn(rb[:, 0, 512 * (NC * d + c):512 * (NC * d + c) + 512], bk(4 + k), ACT.Sigmoid, bias=bcol(p + "_bgx")))
                        r(fn(rb[:, 1, 512 * (NC * d + c):512 * (NC * d + c) + 512], bk(5 + k), ACT.Sigmoid, bias=bcol(p + "_bga")))
                for d in range(2):
                    for c in range(NC):
                        at = 512 * (NC * d + c)
                        act.wait_ge(r_dve, 2 * (NC * d + c) + 1)
                        r(fn(rc[:, at:at + 512], rb[:, 1, at:at + 512], ACT.Square))
                        act.wait_ge(r_act, R_SQ + 2 * (NC * d + c) + 1)
                        r(fn(rc[:, at:at + 512], rc[:, at:at + 512], ACT.Sqrt, scale=-1.0, bias=ones[:, 0:1]))
                for c in range(NC):
                    act.wait_ge(r_pe, 6 * NC + c + 1)
                    act.wait_ge(r_dve, R_HB)
                    r(fn(rg[:, 0, 512 * c:512 * c + 512], bk(c), ACT.Identity, scale=0.5, bias=eas[:, 3:4]))
                for c in range(NC):
                    act.wait_ge(r_dve, R_HB + c + 1)
                    r(fn(rb[:, 0, 512 * c:512 * c + 512], rg[:, 0, 512 * c:512 * c + 512], ACT.Gelu_apprx_tanh))

            def moe(k):
                act.wait_ge(m_dve, M_DVE * k + 2)
                fn(me[:, :, :], me[:, :, :], ACT.Exp).then_inc(m_act, 1)
                for c in range(NC):
                    act.wait_ge(m_pe, M_PE * k + 7 + c + 1)
                    fn(xch(mgb, c), bk(c), ACT.Copy).then_inc(m_act, 1)

            act.wait_ge(ln_const, 1)
            for stage in range(nst):
                layernorm(stage)
                if stage == 0:
                    project_qkv(0)
                    query_zero()
                    windowed_attention()
                    project_out(0)
                if stage == 2:
                    recurrent()
                if stage == 4 or stage == 6:
                    project_qkv(stage // 2 - 1)
                    full_attention(stage // 2 - 1)
                    project_out(stage // 2 - 1)
                if stage == 5 or stage == 7:
                    moe(stage // 2 - 2)

        @block.vector
        def _(dve):
            def tt(o, a, b, op):
                return nc.vector.tensor_tensor(o, a, b, op)

            def spread(y, column):
                return tt(diag[:, y, :, :], ident[:, :].unsqueeze(1).broadcast_to((P, 4, P)),
                          column.unsqueeze(2).broadcast_to((P, 4, P)), ALU.mult)

            def layernorm(k):
                def centre(c):
                    dve.wait_ge(ln_mean, NC * k + c + 1)
                    tt(xch(xc, c), xch(x, c), bk(LN_MEAN[c]), ALU.subtract).then_inc(ln_cent, 1)

                def rstd(c):
                    dve.wait_ge(ln_std, NC * k + c + 1)
                    r = ln_s[:, 1, 4 * c:4 * c + 4]
                    nc.vector.reciprocal(r, ln_s[:, 0, 4 * c:4 * c + 4]).then_inc(ln_rstd, 1)
                    dve.wait_ge(ln_rstd, NC * k + c + 1)
                    if c >= 2:
                        dve.wait_ge(ln_b, NC * k + c - 1)
                    spread(c % 2, r).then_inc(ln_diag, 1)

                def normalise(c):
                    dve.wait_ge(ln_b, NC * k + c + 1)
                    tt(xn(c), xch(xc, c), bk(LN_STD[c]), ALU.mult).then_inc(xn_ready, 1)

                for step, c in ((centre, 0), (centre, 1), (centre, 2), (rstd, 0), (centre, 3), (rstd, 1),
                                (normalise, 0), (rstd, 2), (normalise, 1), (rstd, 3), (normalise, 2), (normalise, 3)):
                    step(c)

            def ternary():
                nc.vector.tensor_reduce(ts_[:, 0:1], w("tern"), AX.X, ALU.add,
                                        apply_absolute_value=True).then_inc(tw, 1)
                dve.wait_ge(tw_sum, 1)
                nc.vector.tensor_scalar(ts_[:, 1:2], bk(6)[:, 0:1], 1.0 / (P * P), 0.7,
                                        ALU.mult, ALU.mult).then_inc(tw, 1)
                dve.wait_ge(tw, 2)
                nc.vector.tensor_scalar(ts_[:, 2:3], ts_[:, 1:2], -1.0, None, ALU.mult).then_inc(tw, 1)
                dve.wait_ge(tw, 3)
                nc.vector.tensor_scalar(tg[:, 0, :], w("tern"), ts_[:, 1:2], bcol("alpha"), ALU.is_gt, ALU.mult)
                nc.vector.tensor_scalar(tg[:, 1, :], w("tern"), ts_[:, 2:3], bcol("alpha"), ALU.is_lt,
                                        ALU.mult).then_inc(tw, 1)
                dve.wait_ge(tw, 4)
                tt(tern[:, :], tg[:, 0, :], tg[:, 1, :], ALU.subtract).then_inc(tw, 1)

            def project_qkv(layer):
                if layer == 0:
                    for b in range(B):
                        dve.wait_ge(xn_ready, NC)
                        for t in range(WT):
                            ins = nc.vector.tensor_copy(xwin[:, b, t, 0:P - 1], xp[:, b, QT * t:QT * t + P - 1])
                    ins.then_inc(win_ready, 1)
                for n, (i, _, cols, _) in enumerate(qk_chunks(layer), QK_BASE[layer]):
                    src, o, r = bk(n % 2)[:, 0:cols], parts[:, n % 2, :, 0:cols], res[:, n % 2, 0:cols]
                    dve.wait_ge(part_act, 2 * n + 1)
                    tt(r, src, o[:, 0, :], ALU.subtract).then_inc(part_dve, 1)
                    dve.wait_ge(part_act, 2 * n + 2)
                    tt(o[:, 2, :], r, o[:, 1, :], ALU.subtract).then_inc(part_dve, 1)
                for g, (t0, k) in enumerate(VCH[layer], V_BASE[layer]):
                    v = [Vb[:, t0:t0 + k, :, i, 0:D] for i in range(3)]
                    src = bk(2 + g % 2)[:, 0:k * P].rearrange("p (t h d) -> p t h d", t=k, h=H)
                    r = res[:, g % 2, 0:k * P].rearrange("p (t h d) -> p t h d", t=k, h=H)
                    dve.wait_ge(v_out, 2 * g + 1)
                    tt(r, src, v[0], ALU.subtract).then_inc(v_dve, 1)
                    dve.wait_ge(v_out, 2 * g + 2)
                    tt(v[2], r, v[1], ALU.subtract).then_inc(v_dve, 1)

            def query_zero():
                dve.wait_ge(q0_copied, B)
                dve.wait_ge(q0_const, 1)
                for b in range(B):
                    ins = nc.vector.tensor_scalar(q0m[:, b, :], hmask[:, :], q0f[:, b:b + 1], None, ALU.mult)
                ins.then_inc(g0v, 1)
                for b in range(B):
                    dve.wait_ge(g0, b + 1)
                    for t in range(0, WT, 5):
                        c = min(5 * QT, S - t * QT)
                        ins = nc.vector.tensor_reduce(q0x[:, b, t // 5:t // 5 + 1],
                                                      bk(3 * b + t // 5)[0:H, 0:c], AX.X, ALU.max)
                    ins.then_inc(q0_max, 1)
                    dve.wait_ge(q0_max, 1 + 2 * b)
                    nc.vector.tensor_reduce(s0s[:, b, 0:1], q0x[:, b, :], AX.X, ALU.max).then_inc(q0_max, 1)
                    dve.wait_ge(q0_max, 2 + 2 * b)
                    nc.vector.tensor_scalar(s0s[:, b, 1:2], s0s[:, b, 0:1], -SCALE, None, ALU.mult).then_inc(g0v, 1)
                dve.wait_ge(g0, 3)
                nc.vector.tensor_copy(s0t[:, :, :, :].rearrange("p b t h -> p (b t h)"),
                                      bk(6)[:, 0:B * WT * H]).then_inc(g0v, 1)
                dve.wait_ge(g0, 4)
                k = 4
                for b in range(B):
                    tt(o0[:, b, :, :], bk(7)[0:H, 160 * b:160 * b + H * (D + 1)].rearrange("p (h d) -> p h d", h=H),
                       hmaskT[:, :, :], ALU.mult).then_inc(g0v, 1)
                    dve.wait_ge(g0v, k + 1)
                    nc.vector.tensor_reduce(o0s[:, b, :], o0[:, b, :, :].rearrange("p h d -> p d h"), AX.X,
                                            ALU.add).then_inc(g0v, 1)
                    dve.wait_ge(g0v, k + 2)
                    nc.vector.reciprocal(s0s[:, b, 2:3], o0s[:, b, D:D + 1]).then_inc(g0v, 1)
                    dve.wait_ge(g0v, k + 3)
                    nc.vector.tensor_scalar(o0s[:, b, 0:D], o0s[:, b, 0:D], s0s[:, b, 2:3], None,
                                            ALU.mult).then_inc(g0v, 1)
                    dve.wait_ge(g0v, k + 4)
                    tt(z0[:, b, :, :], hmaskT[:, :, 0:D], o0s[:, b, 0:D].unsqueeze(1).broadcast_to((H, H, D)),
                       ALU.mult).then_inc(g0v, 1)
                    k += 5
                dve.wait_ge(g0, 5)
                nc.vector.tensor_copy(q0o[:, :], bk(6)[:, 400:400 + B]).then_inc(g0v, 1)

            def split_maximum(g, rows, cols, j, step):
                src, o, r = bk(7)[0:rows, 0:cols], mp[0:rows, j, :, 0:cols], mres[0:rows, j % 2, 0:cols]
                if step == 0:
                    dve.wait_ge(split_act, 2 * g + 1)
                    tt(r, src, o[:, 0, :], ALU.subtract).then_inc(split_dve, 1)
                else:
                    dve.wait_ge(split_act, 2 * g + 2)
                    tt(o[:, 2, :], r, o[:, 1, :], ALU.subtract).then_inc(split_dve, 1)

            def remainder(slot, a, b):
                tt(lo[:, slot, a:b], pt[:, slot, a:b], pth[:, slot, a:b], ALU.subtract).then_inc(lo_dve, 1)

            def divide(g, q, tiles, t0, h, eps, y, step):
                n, d = num[0:q, y, 0:tiles, :], den[0:q, y, 0:tiles]
                src = bk(6)[0:q, 0:tiles * VC].rearrange("p (t n d) -> p t d n", t=tiles, d=D + 1)
                if step == 0:
                    nc.vector.tensor_reduce(n, src, AX.X, ALU.add).then_inc(evac, 1)
                elif step == 1:
                    dve.wait_ge(evac, 4 * g + 5)
                    nc.vector.tensor_scalar(d, n[:, :, D], eps, None, ALU.add).then_inc(evac, 1)
                elif step == 2:
                    dve.wait_ge(evac, 4 * g + 6)
                    nc.vector.reciprocal(rden[0:q, y, 0:tiles], d).then_inc(evac, 1)
                else:
                    dve.wait_ge(evac, 4 * g + 7)
                    tt(A[0:q, t0:t0 + tiles, bass.ds(h * D, D)], n[:, :, 0:D],
                       rden[0:q, y, 0:tiles].unsqueeze(2).broadcast_to((q, tiles, D)), ALU.mult).then_inc(evac, 1)

            def windowed_attention():
                dve.wait_ge(g0v, 15)
                dve.drain().then_inc(sm_read, 1)
                dve.drain().then_inc(split_dve, 2)
                dve.drain().then_inc(evac, 4)

                def maxima(u, j):
                    dve.wait_ge(sm_ready, u + 1)
                    b = j % B
                    nc.vector.tensor_reduce(nm[0:QT, j // B, b * WT:(b + 1) * WT],
                                            wide[0:QT, 0:3, :].rearrange("p g (t k) -> p (g t) k", k=P)[:, 0:WT, :],
                                            AX.X, ALU.max, negate=True).then_inc(sm_read, 1)

                for u in range(LEAD):
                    maxima(u, u)
                for h in range(2):
                    for step in range(2):
                        split_maximum(h, B * WT, QT, h, step)

                def unit(i, j, last):
                    u = i * BODY_W + j
                    left = BODY_W - j if last else UNITS

                    def quotients(d, step):
                        k = j - d
                        if step == 0:
                            dve.wait_ge(pv_steps, u - d + 5)
                        divide(u - d, QT, WT, k % B * WT, i * RING_W + k // B, 0.0, k % 2, step)

                    if j > 0:
                        quotients(1, 0)
                    if j % B == 1 and left > 3:
                        split_maximum(i * RING_W + (j // B + 2), B * WT, QT, (j // B + 2) % RING_W, 0)
                    if j > 0:
                        quotients(1, 1)
                    if j % B == 1 and left > 3:
                        split_maximum(i * RING_W + (j // B + 2), B * WT, QT, (j // B + 2) % RING_W, 1)
                    if left > LEAD:
                        maxima(u + LEAD, (j + LEAD) % BODY_W)
                    if j > 0:
                        quotients(1, 2)
                        quotients(1, 3)
                    if j == BODY_W - 1:
                        for step in range(4):
                            quotients(0, step)

                with dve.Fori(0, UNITS // BODY_W - 1) as i:
                    for j in range(BODY_W):
                        unit(i, j, False)
                for j in range(BODY_W):
                    unit(UNITS // BODY_W - 1, j, True)

            def full_attention(layer):
                u0, st0, sm0 = layer * UNITS, ST_BASE[layer], SM_BASE[layer]
                use0 = (layer - 1) * (UNITS // RING_F)
                eps = DEN_EPS if layer == 1 else 0.0

                def maximum(u, j, t, y):
                    dve.wait_ge(sm_ready, sm0 + (u * KT + t) * 2 + y + 1)
                    nc.vector.tensor_reduce(mx[:, j % 2, t, y:y + 1], bk(4 + y), AX.X, ALU.max).then_inc(sm_read, 1)

                def collect(u, j):
                    dve.wait_ge(sm_read, sm0 + (u + 1) * KT * 2 + 1)
                    nc.vector.tensor_reduce(nm[:, j, 0:KT], mx[:, j % 2, :, :], AX.X, ALU.max,
                                            negate=True).then_inc(nm_ready, 1)

                for u in range(2):
                    for t in range(KT):
                        for y in range(2):
                            maximum(u, u, t, y)
                collect(0, 0)
                for step in range(2):
                    split_maximum(G_BASE[layer], KT, P, 0, step)

                def slot(i, j, last):
                    s = i * RING_F + j
                    nxt = not last or j + 1 < RING_F
                    smx = not last or j + 2 < RING_F

                    def quotients(d, step):
                        k = j - d
                        if step == 0:
                            dve.wait_ge(pv_steps, st0 + (s - d + 1) * KT + 4)
                        divide(u0 + s - d, P, KT, (k % B) * KT, i * (RING_F // B) + k // B, eps, k % 2, step)

                    def divide_before(step):
                        if j > 0:
                            quotients(1, step)

                    def split_next(step):
                        if nxt:
                            split_maximum(G_BASE[layer] + s + 1, KT, P, (j + 1) % RING_F, step)

                    def collect_next():
                        if nxt:
                            collect(s + 1, (j + 1) % RING_F)

                    between = {(0, 0): (collect_next, lambda: divide_before(0)), (0, 1): (lambda: divide_before(1),),
                               (1, 0): (lambda: divide_before(2),), (1, 1): (lambda: divide_before(3),),
                               (1, 2): (lambda: split_next(0),), (3, 0): (lambda: split_next(1),)}
                    for t in range(KT):
                        dve.wait_ge(exp_done, st0 + s * KT + t + 2)
                        remainder(t % 4, LO_F, S)
                        for k in range(3):
                            if k and smx:
                                maximum(s + 2, j, t, k - 1)
                            for step in between.get((t, k), ()):
                                step()
                    if j == RING_F - 1:
                        for step in range(4):
                            quotients(0, step)

                with dve.Fori(0, UNITS // RING_F - 1) as i:
                    for j in range(RING_F):
                        slot(i, j, False)
                for j in range(RING_F):
                    slot(UNITS // RING_F - 1, j, True)

            def add_projection(layer, stage):
                if layer == 0:
                    dve.wait_ge(at_out, AT_BASE[1])
                    nc.vector.tensor_copy(aT[:, 0:N].rearrange("p (b s) -> p b s", b=B)[:, :, 0:1],
                                          q0o[:, :].unsqueeze(2)).then_inc(g0v, 1)
                for c in range(NC):
                    dve.wait_ge(o_mm, NC * layer + c + 1)
                    if layer == 1:
                        nc.vector.scalar_tensor_tensor(xch(x, c), bk(4 + c), bcol("bo"), xch(x, c), ALU.add,
                                                       ALU.add).then_inc(x_new, 1)
                    else:
                        tt(xch(x, c), bk(4 + c), xch(x, c), ALU.add).then_inc(x_new, 1)

            def ffn(k):
                for c in range(NC):
                    dve.wait_ge(f_mm, NC * k + c + 1)
                    nc.vector.scalar_tensor_tensor(xch(x, c), bk(4 + c), bcol("ffn_b"), xch(x, c), ALU.add,
                                                   ALU.add).then_inc(x_new, 1)

            def recurrent():
                n = [0]

                def r(ins):
                    n[0] += 1
                    ins.then_inc(r_dve, 1)

                dve.wait_ge(ea_ready, 2)
                for d in range(2):
                    for c in range(NC):
                        at = 512 * (NC * d + c)
                        dve.wait_ge(r_act, R_G[d] + 2 * c + 2)
                        a = rb[:, 1, at:at + 512]
                        r(nc.vector.tensor_scalar(a, a, eas[:, d:d + 1], None, ALU.mult))
                        g = rb[:, 0, at:at + 512]
                        r(tt(g, g, rg[:, 1 + d, 512 * c:512 * c + 512], ALU.mult))
                for d in range(2):
                    for c in range(NC):
                        at = 512 * (NC * d + c)
                        dve.wait_ge(r_act, R_SQ + 2 * (NC * d + c) + 2)
                        dve.wait_ge(r_dve, 2 * (NC * d + c) + 2)
                        g = rb[:, 0, at:at + 512]
                        r(tt(g, g, rc[:, at:at + 512], ALU.mult))
                for d in range(2):
                    for b in range(B):
                        at = N * d + S * b
                        dve.wait_ge(r_dve, 2 * 2 * NC + 2 * NC)
                        a, g, h = rb[:, 1, at:at + S], rb[:, 0, at:at + S], rg[:, 1 + d, S * b:S * b + S]
                        if d:
                            a, g, h = a[:, ::-1], g[:, ::-1], h[:, ::-1]
                        r(nc.vector.tensor_tensor_scan(h, a, g, 0.0, ALU.mult, ALU.add))
                assert n[0] == R_SCAN, n[0]
                r(tt(eas[:, 2:3], bcol("f_bo"), bcol("b_bo"), ALU.add))
                dve.wait_ge(r_dve, n[0])
                r(nc.vector.tensor_scalar(eas[:, 3:4], eas[:, 2:3], 0.5, None, ALU.mult))
                assert n[0] == R_HB
                for c in range(NC):
                    dve.wait_ge(r_act, R_OUT + c + 1)
                    y = rg[:, 0, 512 * c:512 * c + 512]
                    r(tt(y, y, xn(c), ALU.add))
                for c in range(NC):
                    dve.wait_ge(r_pe, 7 * NC + c + 1)
                    y = rb[:, 1, 512 * c:512 * c + 512]
                    r(nc.vector.scalar_tensor_tensor(y, bk(4 + c), bcol("ld_b"), xn(c), ALU.add, ALU.add))
                    dve.wait_ge(r_dve, n[0])
                    tt(xch(x, c), y, xch(x, c), ALU.add).then_inc(x_new, 1)

            def moe(k):
                n = [0]

                def m(ins):
                    n[0] += 1
                    ins.then_inc(m_dve, 1)
                    dve.wait_ge(m_dve, M_DVE * k + n[0])

                logits = bk(0)[:, 0:NT * E].rearrange("p (t e) -> p t e", e=E)

                def wide8(t):
                    return t.unsqueeze(2).broadcast_to((P, NT, E))

                dve.wait_ge(moe_const, 1)
                dve.wait_ge(m_pe, M_PE * k + 1)
                m(nc.vector.tensor_reduce(mst[:, 0, :], logits, AX.X, ALU.max))
                m(tt(me[:, :, :], logits, wide8(mst[:, 0, :]), ALU.subtract))
                dve.wait_ge(m_act, M_ACT * k + 1)
                m(nc.vector.tensor_reduce(mst[:, 1, :], me[:, :, :], AX.X, ALU.add))
                m(nc.vector.reciprocal(mst[:, 2, :], mst[:, 1, :]))
                m(tt(me[:, :, :], me[:, :, :], wide8(mst[:, 2, :]), ALU.mult))
                m(nc.vector.tensor_reduce(mst[:, 3, :], me[:, :, :], AX.X, ALU.max))
                m(tt(mw[:, :, :], me[:, :, :], wide8(mst[:, 3, :]), ALU.is_equal))
                m(tt(mw[:, :, :], mw[:, :, :], rank[:, :, :], ALU.mult))
                m(nc.vector.tensor_reduce(mst[:, 4, :], mw[:, :, :], AX.X, ALU.max))
                onehot = moh[:, :].rearrange("p (t e) -> p t e", e=E)
                m(tt(onehot, mw[:, :, :], wide8(mst[:, 4, :]), ALU.is_equal))
                dve.wait_ge(m_pe, M_PE * k + 7)
                m(nc.vector.tensor_copy(mt1[:, :, :], bk(2)[:, 0:P].rearrange("p (t e) -> p e t", e=E)))
                m(nc.vector.tensor_tensor_scan(mt2[:, :, :].rearrange("p e t -> p (e t)"),
                                               keep[:, :, :].rearrange("p e t -> p (e t)"),
                                               mt1[:, :, :].rearrange("p e t -> p (e t)"), 0.0, ALU.mult, ALU.add))
                m(tt(mt2[:, :, :], mt2[:, :, :], mt1[:, :, :], ALU.subtract))
                m(tt(mloc[:, :, :], bk(1)[:, 0:P].rearrange("p (t e) -> p t e", e=E),
                     mt2[:, :, :].rearrange("p e t -> p t e"), ALU.add))
                m(nc.vector.scalar_tensor_tensor(mloc[:, :, :], mloc[:, :, :], float(CAP), onehot, ALU.is_le, ALU.mult))
                m(nc.vector.tensor_reduce(mst[:, 5, :], mloc[:, :, :], AX.X, ALU.add))
                m(tt(mgate[:, :], mst[:, 5, :], mst[:, 3, :], ALU.mult))
                for c in range(NC):
                    if c >= 2:
                        dve.wait_ge(m_pe, M_PE * k + 7 + c - 1)
                    m(spread(c % 2, mgate[:, 4 * c:4 * c + 4]))
                assert n[0] == M_DVE, n[0]
                for c in range(NC):
                    dve.wait_ge(m_act, M_ACT * k + 2 + c)
                    y = xch(xc, c)
                    nc.vector.scalar_tensor_tensor(y, bk(4 + c), bcol("be"), xch(mgb, c), ALU.add,
                                                   ALU.mult).then_inc(m_y, 1)
                    dve.wait_ge(m_y, NC * k + c + 1)
                    tt(xch(x, c), y, xch(x, c), ALU.add).then_inc(x_new, 1)

            dve.wait_ge(ln_const, 1)
            for stage in range(nst):
                layernorm(stage)
                if stage == 0:
                    dve.wait_ge(w_loaded, 48)
                    project_qkv(0)
                    ternary()
                    query_zero()
                    windowed_attention()
                    add_projection(0, 0)
                if stage in (1, 3):
                    ffn(stage // 2)
                if stage == 2:
                    recurrent()
                if stage == 4 or stage == 6:
                    full = stage // 2 - 1
                    project_qkv(full)
                    full_attention(full)
                    add_projection(full, stage)
                if stage == 5 or stage == 7:
                    moe(stage // 2 - 2)


def kernel(**inputs):
    import concourse.bacc as bacc
    from concourse.bass_utils import run_bass_kernel_spmd

    a = {k: np.asarray(v) for k, v in inputs.items()}

    def rows(name):
        return a[name].transpose(1, 0, 2).reshape(P, P)

    rec = {f"{p}_{n}": a[f"L0_attn_b_{q}_W{m}"] for p, q in (("f", "fwd"), ("b", "bwd"))
           for n, m in (("x", "x"), ("gx", "gx"), ("ga", "ga"), ("o", "o"))}
    ws = {"wq0": a["L0_attn_a_Wq"].T, "wk0": a["L0_attn_a_Wk"].T, "wv0": a["L0_attn_a_Wv"].T,
          "wo0": a["L0_attn_a_Wo"].T, "ld": a["L0_attn_b_ld_W"], "tern": a["L0_ffn_weight"].T,
          "wq1": a["L1_attn_a_Wq"].T, "wk1": a["L1_attn_a_Wk"].T, "wv1": a["L1_attn_a_Wv"].T,
          "wo1": a["L1_attn_a_Wo"].T, "wq2": rows("L1_attn_b_W_query"), "wk2": rows("L1_attn_b_W_key"),
          "wv2": rows("L1_attn_b_W_val"), "wo2": a["L1_attn_b_W_out"].reshape(P, P), "we": a["L1_ffn_We"], **rec}
    bs = {f"{p}_{n}": a[f"L0_attn_b_{q}_{m}"] for p, q in (("f", "fwd"), ("b", "bwd"))
          for n, m in (("a", "a_logit"), ("bx", "bx"), ("bgx", "bgx"), ("bga", "bga"), ("bo", "bo"))}
    bs.update(ld_b=a["L0_attn_b_ld_b"], ffn_b=a["L0_ffn_bias"], bo=a["L1_attn_a_bo"], be=a["L1_ffn_be"],
              alpha=np.repeat(a["L0_ffn_alpha"], P))
    arrays = {
        "xT": np.ascontiguousarray(a["L0_attn_a_x"].reshape(N, P).T),
        "weights": np.ascontiguousarray(np.stack([ws[n] for n in W_NAMES], 1)),
        "biases": np.ascontiguousarray(np.stack([bs[n] for n in B_NAMES], 1)),
        "wg": np.ascontiguousarray(a["L1_ffn_Wg"]),
    }
    nc = bacc.Bacc("TRN2", target_bir_lowering=False, num_devices=1)
    aps = [nc.dram_tensor(n, v.shape, F32, kind="ExternalInput").ap() for n, v in arrays.items()]
    out = nc.dram_tensor("outT", (P, N), F32, kind="ExternalOutput").ap()
    build(nc, *aps, out)
    r = run_bass_kernel_spmd(nc, [arrays], core_ids=[0])
    return np.ascontiguousarray(r.results[0]["outT"].T).reshape(B, S, P)
```

```python
from contextlib import ExitStack

import numpy as np

import concourse.bass as bass
from concourse import mybir

ALU = mybir.AluOpType
ACT = mybir.ActivationFunctionType
AX = mybir.AxisListType
F32 = mybir.dt.float32
BF16 = mybir.dt.bfloat16
F16 = mybir.dt.float16

P = 128
B, S = 2, 1024
N = B * S
NC = N // 512
NT = N // P
H, D = 16, 8
NP = 9
R = NP * D
M0 = P - 3
SCALE = float(D) ** -0.5
LN_EPS = 1e-5
DEN_EPS = 1e-8
HALF = 16
QT = P - 1 - 2 * HALF
WT = -(-S // QT)
QW = WT * QT
KW = WT * P
PADW = HALF + QW + HALF + 3
E = 8
CAP = N // E
NEG = -1.0e30
UNITS = B * H
KT = S // P
VC = 3 * (D + 1)
LO_F = 25 * P // 4
DIRECT = 1
RING_W, RING_F = 4, 4
LEAD = 6
BODY_W = B * RING_W

W_NAMES = ["wq0", "wk0", "wv0", "wo0", "f_x", "f_gx", "f_ga", "f_o", "b_x", "b_gx", "b_ga", "b_o", "ld",
           "tern", "wq1", "wk1", "wv1", "wo1", "wq2", "wk2", "wv2", "wo2", "we"]
B_NAMES = ["f_a", "f_bx", "f_bgx", "f_bga", "f_bo", "b_a", "b_bx", "b_bgx", "b_bga", "b_bo", "ld_b",
           "ffn_b", "bo", "be", "alpha"]
WI = {n: i for i, n in enumerate(W_NAMES)}
BI = {n: i for i, n in enumerate(B_NAMES)}


def build(nc, xT, weights, biases, wg, out, stages=8):
    with ExitStack() as ctx:
        def sb(name, shape, dt=F32):
            return ctx.enter_context(nc.sbuf_tensor(name, shape, dt))

        def sem(name):
            return ctx.enter_context(nc.semaphore(name))

        q_dram = nc.dram_tensor("q_dram", (P, 3, B * QW), BF16).ap()
        k_dram = nc.dram_tensor("k_dram", (3, P, B * KW), BF16).ap()

        bank = [ctx.enter_context(nc.psum_tensor(f"bank{i}", [P, 512], F32)) for i in range(2)]
        wide = ctx.enter_context(nc.psum_tensor("wide", [P, 6, 512], F32))

        def bk(i):
            return wide[:, i, :] if i < 6 else bank[i - 6][:, :]

        x = sb("x", [P, N])
        xcsq = sb("xcsq", [P, 2 * N])
        xc, sq = xcsq[:, 0:N], xcsq[:, N:2 * N]
        xp = sb("xp", [P, B, PADW])
        W = sb("W", [P, len(W_NAMES), P])
        bias = sb("bias", [P, len(B_NAMES)])
        wgs = sb("wgs", [P, E])
        ident = sb("ident", [P, P])
        identb = sb("identb", [P, P], BF16)
        ones = sb("ones", [P, P])
        meanw = sb("meanw", [P, P])
        tri = sb("tri", [P, P])
        epsc = sb("epsc", [P, 1])
        keep = sb("keep", [P, E, NT])
        rank = sb("rank", [P, NT, E])
        maskq = sb("maskq", [P, WT, P], BF16)
        maskk = sb("maskk", [P, WT, QT], BF16)
        hmask = sb("hmask", [P, H])
        hmaskT = sb("hmaskT", [H, H, D + 1])
        ln_s = sb("ln_s", [P, 2, NT])
        tern = sb("tern", [P, P])
        tg = sb("tg", [P, 2, P])
        ts_ = sb("ts_", [P, 4])
        eas = sb("eas", [P, 4])

        big = sb("big", [P, 7 * N])
        xwin = big[:, 0:B * KW].rearrange("p (b t k) -> p b t k", b=B, t=WT)
        kf = big[:, B * KW:2 * B * KW]
        V = sb("V", [P, B * WT, H, D + 1])
        o = 2 * B * KW
        A = big[:, o:o + B * WT * P].rearrange("p (t f) -> p t f", f=P)
        o += B * WT * P
        pt = big[:, o:o + 4 * 1056].rearrange("p (n c) -> p n c", n=4)
        aT = sq
        pth = big[:, o:o + 4 * 1056].bitcast(BF16).rearrange("p (n c two) -> p n c two", n=4, two=2)[:, :, :, 1]
        lo = kf.bitcast(F16)[:, 0:4 * 1056].rearrange("p (n c) -> p n c", n=4)
        Vb = sb("Vb", [P, B * WT, H, 3, D + 1], BF16)
        res = sb("res", [P, 3, 512])
        diag = res[:, 0:2, :].rearrange("p n (t c) -> p n t c", c=P)
        parts = sb("parts", [P, 3, 3, 512], BF16)
        Ks = sb("Ks", [P, RING_W * B * KW], BF16)
        Qs = sb("Qs", [P, RING_W * B * QW], BF16)
        Kw, Qw = (a[:, :].rearrange("p (n c) -> p n c", n=RING_W) for a in (Ks, Qs))
        Kf, Qf = (a[:, 0:RING_F * S].rearrange("p (n c) -> p n c", n=RING_F) for a in (Ks, Qs))
        mx = sb("mx", [P, 2, KT, 2])
        nm = sb("nm", [P, RING_W, B * WT])
        mres = sb("mres", [B * WT, 2, P])
        mp = big[0:B * WT, o + 4 * 1056:o + 4 * 1056 + RING_W * 3 * P // 2].bitcast(BF16).rearrange(
            "p (u n c) -> p u n c", u=RING_W, n=3)
        num = sb("num", [P, 2, WT, D + 1])
        den = sb("den", [P, 2, WT])
        rden = sb("rden", [P, 2, WT])
        q0f = sb("q0f", [P, B])
        q0m = sb("q0m", [P, B, H])
        s0 = big[0:H, o:o + B * WT * P].rearrange("p (b t k) -> p b t k", b=B, t=WT)
        s0s = sb("s0s", [H, B, 4])
        s0t = sb("s0t", [P, B, WT, H])
        o0 = sb("o0", [H, B, H, D + 1])
        o0s = sb("o0s", [H, B, D + 1])
        z0 = sb("z0", [H, B, H, D])
        q0x = sb("q0x", [H, B, 3])
        q0o = sb("q0o", [P, B])
        rg = big[:, 0:3 * N].rearrange("p (n t) -> p n t", n=3)
        rb = big[:, 3 * N:7 * N].rearrange("p (n t) -> p n t", n=2)
        rc = xcsq
        mgb = big[:, 0:N]
        me = sb("me", [P, NT, E])
        mw = sb("mw", [P, NT, E])
        moh = sb("moh", [P, NT * E])
        mloc = sb("mloc", [P, NT, E])
        mt1 = sb("mt1", [P, E, NT])
        mt2 = sb("mt2", [P, E, NT])
        mst = sb("mst", [P, 6, NT])
        mgate = sb("mgate", [P, NT])

        x_loaded, w_loaded = sem("x_loaded"), sem("w_loaded")
        c_steps = sem("c_steps")
        ln_const, win_const, moe_const = sem("ln_const"), sem("win_const"), sem("moe_const")
        q0_const = sem("q0_const")
        tw = sem("tw")
        tw_sum = sem("tw_sum")
        ea_ready = sem("ea_ready")
        x_new = sem("x_new")
        ln_mean, ln_cent, ln_sq, ln_var = sem("ln_mean"), sem("ln_cent"), sem("ln_sq"), sem("ln_var")
        ln_std, ln_rstd, ln_diag = sem("ln_std"), sem("ln_rstd"), sem("ln_diag")
        ln_b, xn_ready = sem("ln_b"), sem("xn_ready")
        win_ready = sem("win_ready")
        proj_mm = sem("proj_mm")
        part1, residue = sem("part1"), sem("residue")
        part2, part3 = sem("part2"), sem("part3")
        qk_out = [sem(f"qk_out{i}") for i in range(3)]
        lo_pool, lo_dve = sem("lo_pool"), sem("lo_dve")
        q0_max = sem("q0_max")
        aug_w = [sem(f"aug_w{i}") for i in range(RING_W)]
        aug_f = [sem(f"aug_f{i}") for i in range(RING_F)]
        mrow_w = [sem(f"mrow_w{i}") for i in range(RING_W)]
        mrow_f = [sem(f"mrow_f{i}") for i in range(RING_F)]
        st_ready = sem("st_ready")
        exp_done = sem("exp_done")
        sm_ready, sm_read = sem("sm_ready"), sem("sm_read")
        nm_ready = sem("nm_ready")
        mt_ready = sem("mt_ready")
        split_act = sem("split_act")
        split_dve = sem("split_dve")
        pv_steps = sem("pv_steps")
        evac = sem("evac")
        g0 = sem("g0")
        g0v = sem("g0v")
        g0a = sem("g0a")
        at_mm, at_out, o_mm = sem("at_mm"), sem("at_out"), sem("o_mm")
        f_mm = sem("f_mm")
        r_pe, r_act, r_dve, r_pool = sem("r_pe"), sem("r_act"), sem("r_dve"), sem("r_pool")
        m_pe, m_act, m_dve, m_y = sem("m_pe"), sem("m_act"), sem("m_dve"), sem("m_y")
        stored = sem("stored")

        def w(name):
            return W[:, WI[name], :]

        def bcol(name):
            return bias[:, BI[name]:BI[name] + 1]

        def xch(t, c):
            return t[:, 512 * c:512 * c + 512]

        def xn(c):
            b, o = c // 2, HALF + 512 * (c % 2)
            return xp[:, b, o:o + 512]

        def xnt(t):
            b, o = t // KT, HALF + P * (t % KT)
            return xp[:, b, o:o + P]

        QCH = [(b, t, min(5, WT - t)) for b in range(B) for t in range(0, WT, 5)]
        KCH = [(b, t, min(4, WT - t)) for b in range(B) for t in range(0, WT, 4)]

        VCH = [(b, t, min(4, WT - t)) for b in range(B) for t in range(0, WT, 4)]

        def chunks(layer):
            if layer == 0:
                for b, t, n in QCH:
                    yield "q", xp[:, b, HALF + t * QT:HALF + (t + n) * QT], n * QT, b * QW + t * QT
                for b, t, n in KCH:
                    yield "k", xwin[:, b, t:t + n, :], n * P, b * KW + t * P
                for b, t, n in VCH:
                    yield "v", None, n * P, b * WT + t
            else:
                for i in "qk":
                    for c in range(NC):
                        yield i, xn(c), 512, 512 * c
                for c in range(NC):
                    yield "v", None, 512, 4 * c

        CH_BASE = [0] + [len(QCH) + len(KCH) + len(VCH) + 3 * NC * i for i in range(3)]
        QK_BASE = [0] + [len(QCH) + len(KCH) + 2 * NC * i for i in range(3)]
        CBUF = 3

        def chunk_buffers(layer, n, kind, cols, at):
            src, r = bk(n % CBUF)[:, 0:cols], res[:, n % CBUF, 0:cols]
            if kind == "v":
                def by_head(a):
                    return a.rearrange("p (t h d) -> p t h d", h=H, d=D)

                return by_head(src), by_head(r), [Vb[:, at:at + cols // P, :, i, 0:D] for i in range(3)]
            m = n - CH_BASE[layer] + QK_BASE[layer]
            return src, r, [parts[:, m % CBUF, i, 0:cols] for i in range(3)]

        AT_BASE = [0, len(QCH), len(QCH) + NC]
        ST_BASE = [0, UNITS, UNITS + UNITS * KT]
        SM_BASE = [0, UNITS, UNITS + UNITS * KT * 2]
        G_BASE = [0, H, H + UNITS]

        nst = min(stages, 8)
        LN_MEAN, LN_STD = (0, 1, 0, 1), (2, 0, 2, 1)
        R_U, R_G = [NC, 4 * NC], [2 * NC, 5 * NC]
        R_SQ = 7 * NC
        R_OUT = R_SQ + 4 * NC
        R_GELU2 = R_OUT + NC
        R_SCAN = 6 * NC + 2 * B
        R_HB = R_SCAN + 2
        M_PE, M_ACT, M_DVE = 3 + 2 * NC, 1 + NC, 17 + NC

        block = ctx.enter_context(nc.Block())

        @block.sync
        def _(sp):
            for c in range(NC):
                sp.dma_start(xch(x, c), xT[:, 512 * c:512 * c + 512]).then_inc(x_loaded, 16)
                sp.wait_ge(x_loaded, 16 * (c + 1))
            sp.dma_start(W[:, :, :], weights).then_inc(w_loaded, 16)
            sp.dma_start(bias[:, :], biases).then_inc(w_loaded, 16)
            sp.dma_start(wgs[:, :], wg).then_inc(w_loaded, 16)

            def store_parts(layer):
                m = QK_BASE[layer]
                for n, (kind, _, cols, at) in enumerate(chunks(layer), CH_BASE[layer]):
                    if kind == "v":
                        continue
                    sp.wait_ge(part3, n + 1)
                    dst = q_dram[:, :, at:at + cols] if kind == "q" else k_dram[:, :, at:at + cols].rearrange("a p c -> p a c")
                    sp.dma_start(dst, parts[:, m % CBUF, :, 0:cols]).then_inc(qk_out[m % CBUF], 16)
                    m += 1

            def parts_stored(layer):
                n = QK_BASE[layer + 1]
                for i in range(CBUF):
                    sp.wait_ge(qk_out[i], 16 * ((n + CBUF - 1 - i) // CBUF))

            def load_operands(q, k, h, qcols, kcols, loaded):
                w = q.shape[1]
                rows = q_dram[bass.ds(h * D, D), :, qcols:qcols + w].rearrange("d i t -> (d i) t")
                sp.dma_start(q[0:R, :], rows.unsqueeze(0).broadcast_to((3, 3 * D, w))).then_inc(loaded, 16)
                w = k.shape[1]
                for j in range(3):
                    rows = k_dram[j, bass.ds(h * D, D), kcols:kcols + w]
                    sp.dma_start(k[j * 24:j * 24 + 24, :],
                                 rows.unsqueeze(1).broadcast_to((D, 3, w))).then_inc(loaded, 16)

            def place_maximum(g, q, n, qt, slot, rows):
                sp.wait_ge(split_dve, 2 * g + 4)
                for i in range(3):
                    sp.dma_start(q[M0 + i:M0 + i + 1, slot, 0:n * qt], mp[0:n, slot, i, 0:qt]).then_inc(rows, 16)

            def windowed_attention():
                def load(h, slot):
                    load_operands(Qw[:, slot, :], Kw[:, slot, :], h, 0, 0, aug_w[slot])

                def place(h, slot):
                    place_maximum(h, Qw, B * WT, QT, slot, mrow_w[slot])

                for h in range(RING_W):
                    load(h, h)
                for h in range(2):
                    place(h, h)

                def head(i, j, last):
                    h = i * RING_W + j
                    if not last:
                        sp.wait_ge(st_ready, B * h + B)
                        load(i * RING_W + (RING_W + j), j)
                    if not last or j + 2 < RING_W:
                        place(h + 2, (j + 2) % RING_W)

                with sp.Fori(0, H // RING_W - 1) as i:
                    for j in range(RING_W):
                        head(i, j, False)
                for j in range(RING_W):
                    head(H // RING_W - 1, j, True)

            def full_attention(layer):
                def load(h, b, slot):
                    load_operands(Qf[:, slot, :], Kf[:, slot, :], h, b * S, b * S, aug_f[slot])

                def place(u, slot):
                    place_maximum(G_BASE[layer] + u, Qf, KT, P, slot, mrow_f[slot])

                for u in range(RING_F):
                    load(u // B, u % B, u)
                place(0, 0)

                def slot(i, j, last):
                    s = i * RING_F + j
                    if not last or j + 1 < RING_F:
                        place(s + 1, (j + 1) % RING_F)
                    if not last:
                        sp.wait_ge(st_ready, ST_BASE[layer] + (s + 1) * KT)
                        load(i * (RING_F // B) + (RING_F + j) // B, j % B, j)

                with sp.Fori(0, UNITS // RING_F - 1) as i:
                    for j in range(RING_F):
                        slot(i, j, False)
                for j in range(RING_F):
                    slot(UNITS // RING_F - 1, j, True)

            for stage in range(nst):
                if stage in (0, 4, 6):
                    layer = {0: 0, 4: 1, 6: 2}[stage]
                    store_parts(layer)
                    parts_stored(layer)
                    if layer == 0:
                        sp.wait_ge(win_const, 1)
                        windowed_attention()
                    else:
                        full_attention(layer)
            for c in range(NC):
                sp.wait_ge(x_new, NC * (nst - 1) + c + 1)
                sp.dma_start(out[:, 512 * c:512 * c + 512], xch(x, c)).then_inc(stored, 16)
            sp.wait_ge(stored, 16 * NC)

        @block.gpsimd
        def _(pool):
            n = [0]

            def step(ins):
                n[0] += 1
                ins.then_inc(c_steps, 1)
                pool.wait_ge(c_steps, n[0])

            def select(v, op, fill, base, pattern, cm):
                step(pool.affine_select(out=v, in_=v, compare_op=op, fill=fill, base=base, pattern=pattern,
                                        channel_multiplier=cm))

            step(pool.memset(meanw[:, :], 1.0 / P))
            step(pool.memset(epsc[:, :], LN_EPS))
            step(pool.memset(ones[:, :], 1.0))
            step(pool.memset(ident[:, :], 0.0))
            select(ident[:, :], ALU.not_equal, 1.0, 0, [[-1, P]], 1)
            step(pool.memset(xp[:, :, 0:HALF], 0.0))
            step(pool.memset(xp[:, :, HALF + S:PADW], 0.0))
            pool.drain().then_inc(ln_const, 1)
            step(pool.memset(V[:, :, :, D:D + 1], 1.0))
            step(pool.memset(Vb[:, :, :, 0, D:D + 1], 1.0))
            step(pool.memset(Vb[:, :, :, 1:3, D:D + 1], 0.0))
            step(pool.memset(hmask[:, :], 1.0))
            select(hmask[:, :], ALU.is_ge, 0.0, 0, [[-D, H]], 1)
            select(hmask[:, :], ALU.is_ge, 0.0, D - 1, [[D, H]], -1)
            step(pool.memset(hmaskT[:, :, :], 1.0))
            select(hmaskT[:, :, :], ALU.is_equal, 0.0, 0, [[-1, H], [0, D + 1]], 1)
            step(pool.memset(s0[:, :, :, :], 0.0))
            pool.drain().then_inc(q0_const, 1)
            step(pool.memset(Ks[:, :], 1.0))
            step(pool.memset(Qs[:, :], 0.0))
            step(pool.memset(identb[:, :], 0.0))
            select(identb[:, :], ALU.not_equal, 1.0, 0, [[-1, P]], 1)
            step(pool.memset(maskq[:, :, :], 0.0))
            select(maskq[:, :, 0:P - 1], ALU.is_ge, NEG, 0, [[0, WT], [1, P - 1]], -1)
            select(maskq[:, :, 0:P - 1], ALU.is_ge, NEG, 2 * HALF, [[0, WT], [-1, P - 1]], 1)
            select(maskq[:, :, 0:P - 1], ALU.is_gt, NEG, -HALF, [[QT, WT], [1, P - 1]], 0)
            select(maskq[:, :, 0:P - 1], ALU.is_gt, NEG, S + HALF, [[-QT, WT], [-1, P - 1]], 0)
            step(pool.memset(maskk[:, :, :], 0.0))
            select(maskk[:, :, :], ALU.is_ge, NEG, 0, [[0, WT], [-1, QT]], 1)
            select(maskk[:, :, :], ALU.is_ge, NEG, 2 * HALF, [[0, WT], [1, QT]], -1)
            select(maskk[:, :, :], ALU.is_gt, NEG, -HALF, [[QT, WT], [0, QT]], 1)
            select(maskk[:, :, :], ALU.is_gt, NEG, S + HALF, [[-QT, WT], [0, QT]], -1)
            select(maskk[:, :, :], ALU.is_gt, 0.0, P - 1, [[0, WT], [0, QT]], -1)
            pool.drain().then_inc(win_const, 1)
            step(pool.memset(tri[:, :], 1.0))
            select(tri[:, :], ALU.is_ge, 0.0, 0, [[1, P]], -1)
            step(pool.memset(keep[:, :, :], 1.0))
            step(pool.memset(keep[:, :, 0:1], 0.0))
            for e in range(E):
                step(pool.memset(rank[:, :, e:e + 1], float(E - e)))
            pool.drain().then_inc(moe_const, 1)

            def remainder(slot, a, b):
                pool.tensor_tensor(lo[:, slot, a:b], pt[:, slot, a:b], pth[:, slot, a:b],
                                   ALU.subtract).then_inc(lo_pool, 1)

            if nst > 0:
                with pool.Fori(0, UNITS // BODY_W) as i:
                    for j in range(BODY_W):
                        pool.wait_ge(exp_done, i * BODY_W + j + 2)
                        remainder(j % 4, 0, QW)
            for layer in (1, 2):
                if nst > 2 * layer + 2:
                    with pool.Fori(0, UNITS) as i:
                        for j in range(KT):
                            pool.wait_ge(exp_done, ST_BASE[layer] + i * KT + j + 2)
                            remainder(j % 4, DIRECT * P, LO_F)

        @block.tensor
        def _(pe):
            def mm(o, l, r, start=True, stop=True, **kw):
                return nc.tensor.matmul(o, l, r, start=start, stop=stop, **kw)

            def layernorm(k):
                def mean(c):
                    if k == 0:
                        pe.wait_ge(x_loaded, 16 * (c + 1))
                    else:
                        pe.wait_ge(x_new, NC * (k - 1) + c + 1)
                    if c >= 2:
                        pe.wait_ge(ln_cent, NC * k + c - 1)
                    mm(bk(LN_MEAN[c]), meanw[:, :], xch(x, c)).then_inc(ln_mean, 1)

                def variance(c):
                    pe.wait_ge(ln_sq, NC * k + c + 1)
                    if c:
                        pe.wait_ge(ln_std, NC * k + c)
                    for t in range(4 * c, 4 * c + 4):
                        ins = mm(bk(3)[:, t:t + 1], sq[:, P * t:P * t + P], meanw[:, 0:1])
                    ins.then_inc(ln_var, 1)

                def spread(c):
                    pe.wait_ge(ln_diag, NC * k + c + 1)
                    if c == 2:
                        pe.wait_ge(xn_ready, NC * k + 1)
                    mm(bk(LN_STD[c]), ones[:, :], res[:, c % 2, :]).then_inc(ln_b, 1)

                if k == 6:
                    pe.wait_ge(m_act, M_ACT)
                for step, c in ((mean, 0), (mean, 1), (variance, 0), (mean, 2), (variance, 1), (spread, 0),
                                (mean, 3), (variance, 2), (spread, 1), (variance, 3), (spread, 2), (spread, 3)):
                    step(c)

            def ternary():
                pe.wait_ge(tw, 1)
                mm(bk(6)[:, 0:1], ones[:, :], ts_[:, 0:1]).then_inc(tw_sum, 1)

            def project_qkv(layer):
                pe.wait_ge(xn_ready, NC * ({0: 0, 1: 4, 2: 6}[layer] + 1))
                if layer == 0:
                    pe.wait_ge(win_ready, 3)
                for n, (kind, mov, cols, at) in enumerate(chunks(layer), CH_BASE[layer]):
                    if n >= CBUF:
                        pe.wait_ge(residue, n - CBUF + 1)
                    wn = w("w%s%d" % (kind, layer))
                    if kind == "v":
                        for t in range(at, at + cols // P):
                            lhs = xwin[:, t // WT, t % WT, :] if layer == 0 else xnt(t)
                            ins = mm(bk(n % CBUF)[:, (t - at) * P:(t - at + 1) * P], lhs, wn)
                    else:
                        ins = mm(bk(n % CBUF)[:, 0:cols], wn, mov)
                    ins.then_inc(proj_mm, 1)

            def query_zero():
                pe.wait_ge(q0_const, 1)
                pe.wait_ge(g0v, 1)
                pe.wait_ge(part3, CH_BASE[1])
                for b in range(B):
                    for t in range(0, WT, 5):
                        k = min(5, WT - t)
                        cols = kf[:, b * KW + t * P:b * KW + (t + k) * P].rearrange("p (t k) -> p t k", k=P)
                        ins = mm(bk(3 * b + t // 5)[0:H, 0:k * QT].rearrange("p (t k) -> p t k", k=QT),
                                 q0m[:, b, :], cols[:, :, HALF:HALF + QT])
                    ins.then_inc(g0, 1)
                pe.wait_ge(g0a, 2)
                for b in range(B):
                    for t in range(WT):
                        ins = nc.tensor.transpose(bk(6)[:, (b * WT + t) * H:(b * WT + t + 1) * H],
                                                  s0[:, b, t, :], ident[0:H, 0:H])
                ins.then_inc(g0, 1)
                pe.wait_ge(g0v, 4)
                for b in range(B):
                    for t in range(WT):
                        ins = mm(bk(7)[0:H, 160 * b:160 * b + H * (D + 1)], s0t[:, b, t, :],
                                 V[:, b * WT + t, :, :].rearrange("p h d -> p (h d)"),
                                 start=(t == 0), stop=(t == WT - 1))
                ins.then_inc(g0, 1)
                pe.wait_ge(g0v, 14)
                for b in range(B):
                    ins = mm(bk(6)[:, 400 + b:401 + b], z0[:, b, :, :].rearrange("p h d -> p (h d)"),
                             ones[0:H, 0:1])
                ins.then_inc(g0, 1)

            def windowed_attention():
                pe.wait_ge(g0v, 15)
                pe.wait_ge(win_const, 1)
                pe.drain().then_inc(pv_steps, 4)

                def maxima(u, j, bank=0):
                    k0, q0 = j % B * KW, j % B * QW
                    for t in range(0, WT, 4):
                        k = min(4, WT - t)
                        mm(bk(bank + t // 4)[0:QT, 0:k * P], identb[0:QT, 0:QT],
                           maskq[0:QT, t:t + k, :].rearrange("p t k -> p (t k)"))
                        for y in range(t, t + k):
                            ins = mm(bk(bank + t // 4)[0:QT, (y - t) * P:(y - t + 1) * P],
                                     Qw[0:M0, j // B, q0 + y * QT:q0 + (y + 1) * QT],
                                     Kw[0:M0, j // B, k0 + y * P:k0 + (y + 1) * P],
                                     start=False, stop=True, skip_group_check=True)
                    ins.then_inc(sm_ready, 1)

                def turn(h, slot):
                    pe.wait_ge(sm_read, B * h + B + 1)
                    pe.wait_ge(split_dve, 2 * h + 1)
                    nc.tensor.transpose(bk(7)[0:B * WT, 0:QT], nm[0:QT, slot, :],
                                        ident[0:QT, 0:QT]).then_inc(mt_ready, 1)

                def scores(u, j):
                    pe.wait_ge(exp_done, u + 1)
                    k0, q0 = j % B * KW, j % B * QW
                    for t in range(0, WT, 5):
                        k = min(5, WT - t)
                        mm(bk(3 + t // 5)[:, 0:k * QT], identb[:, :],
                           maskk[:, t:t + k, :].rearrange("p t k -> p (t k)"))
                        for y in range(t, t + k):
                            ins = mm(bk(3 + t // 5)[:, (y - t) * QT:(y - t + 1) * QT],
                                     Kw[:, j // B, k0 + y * P:k0 + (y + 1) * P],
                                     Qw[:, j // B, q0 + y * QT:q0 + (y + 1) * QT],
                                     start=False, stop=True, skip_group_check=True)
                    ins.then_inc(st_ready, 1)

                def values(u, j, h, b):
                    pe.wait_ge(lo_pool, u + 1)
                    pe.wait_ge(evac, 4 * u + 1)
                    for t in range(WT):
                        v = Vb[:, b * WT + t, bass.ds(h, 1), :, :].rearrange("p h n d -> p (h n d)")
                        o = bk(6)[0:QT, t * VC:(t + 1) * VC]
                        mm(o, pth[:, j % 4, t * QT:(t + 1) * QT], v, stop=False)
                        ins = mm(o, lo[:, j % 4, t * QT:(t + 1) * QT], v, start=False)
                    ins.then_inc(pv_steps, 1)

                for u in range(LEAD):
                    if u % B == 0:
                        pe.wait_ge(aug_w[u // B], 64)
                    pe.wait_ge(sm_read, max(u, 1))
                    maxima(u, u, 3 * (u % 2))
                    if u in (2, 4):
                        turn(u // 2 - 1, u // 2 - 1)
                pe.wait_ge(mrow_w[0], 48)
                pe.wait_ge(sm_read, LEAD + 1)
                scores(0, 0)

                def unit(i, j, last):
                    u = i * BODY_W + j
                    left = BODY_W - j if last else UNITS
                    if left > 1:
                        n = j + 1
                        if n % B == 0:
                            pe.wait_ge(mrow_w[n // B % RING_W], 48 * (i + 1 + n // BODY_W))
                        scores(u + 1, n % BODY_W)
                    if j % B == 0 and left > 4:
                        turn(i * RING_W + (j // B + 2), (j // B + 2) % RING_W)
                    if left > LEAD:
                        n = j + LEAD
                        if n % B == 0:
                            pe.wait_ge(aug_w[n // B % RING_W], 64 * (i + 1 + n // BODY_W))
                        pe.wait_ge(sm_read, u + LEAD + 1)
                        maxima(u + LEAD, n % BODY_W)
                    values(u, j, i * RING_W + j // B, j % B)

                with pe.Fori(0, UNITS // BODY_W - 1) as i:
                    for j in range(BODY_W):
                        unit(i, j, False)
                for j in range(BODY_W):
                    unit(UNITS // BODY_W - 1, j, True)

            def full_attention(layer):
                u0, st0, sm0 = layer * UNITS, ST_BASE[layer], SM_BASE[layer]
                use0 = (layer - 1) * (UNITS // RING_F)
                pe.wait_ge(part3, CH_BASE[layer + 1])

                def maxima(u, j, t):
                    for y in range(2):
                        pe.wait_ge(sm_read, sm0 + (u * KT + t) * 2 + y)
                        mm(bk(4 + y), Qf[0:M0, j, t * P:(t + 1) * P],
                           Kf[0:M0, j, 512 * y:512 * y + 512]).then_inc(sm_ready, 1)

                def turn(u, j):
                    pe.wait_ge(nm_ready, u0 - UNITS + u + 1)
                    pe.wait_ge(split_dve, 2 * (G_BASE[layer] + u) + 1)
                    nc.tensor.transpose(bk(7)[0:KT, 0:P], nm[:, j, 0:KT], ident[:, :]).then_inc(mt_ready, 1)

                def scores(u, j, t):
                    pe.wait_ge(exp_done, st0 + u * KT + t)
                    for y in range(2):
                        ins = mm(bk(2 * (t % 2) + y), Kf[:, j, t * P:(t + 1) * P],
                                 Qf[:, j, 512 * y:512 * y + 512])
                    ins.then_inc(st_ready, 1)

                def values(u, j, t, h, b):
                    n = st0 + u * KT + t
                    pe.wait_ge(lo_pool, n + 1)
                    pe.wait_ge(lo_dve, n - UNITS + 1)
                    if t == 0:
                        pe.wait_ge(evac, 4 * (u0 + u) + 1)
                    v = V[:, b * KT + t, bass.ds(h, 1), :].rearrange("p h d -> p (h d)")
                    for y in range(DIRECT):
                        ins = mm(bk(6)[:, y * VC:y * VC + D + 1], pt[:, t % 4, y * P:(y + 1) * P], v,
                                 start=(t == 0 and y == 0), stop=(t == KT - 1), skip_group_check=True)
                    v = Vb[:, b * KT + t, bass.ds(h, 1), :, :].rearrange("p h n d -> p (h n d)")
                    for y in range(DIRECT, KT):
                        o = bk(6)[:, y * VC:(y + 1) * VC]
                        mm(o, pth[:, t % 4, y * P:(y + 1) * P], v, start=(t == 0 and y == 0), stop=False,
                           skip_group_check=True)
                        ins = mm(o, lo[:, t % 4, y * P:(y + 1) * P], v, start=False, stop=(t == KT - 1),
                                 skip_group_check=True)
                    ins.then_inc(pv_steps, 1)

                for u in range(2):
                    pe.wait_ge(aug_f[u], 64 * (use0 + 1))
                    for t in range(KT):
                        maxima(u, u, t)
                        if u == 1 and t == KT // 2 - 1:
                            turn(0, 0)
                pe.wait_ge(mrow_f[0], 48 * (use0 + 1))
                scores(0, 0, 0)
                scores(0, 0, 1)

                def slot(i, j, last):
                    s = i * RING_F + j
                    nxt = not last or j + 1 < RING_F
                    smx = not last or j + 2 < RING_F
                    for t in range(KT):
                        if t < KT - 2:
                            scores(s, j, t + 2)
                        elif nxt:
                            if t == KT - 2:
                                pe.wait_ge(mrow_f[(j + 1) % RING_F], 48 * (use0 + i + 1 + (j + 1) // RING_F))
                            scores(s + 1, (j + 1) % RING_F, t + 2 - KT)
                        if smx:
                            if t == 0:
                                pe.wait_ge(aug_f[(j + 2) % RING_F], 64 * (use0 + i + 1 + (j + 2) // RING_F))
                            maxima(s + 2, (j + 2) % RING_F, t)
                        if t == 0 and nxt:
                            turn(s + 1, (j + 1) % RING_F)
                        values(s, j, t, i * (RING_F // B) + j // B, j % B)

                with pe.Fori(0, UNITS // RING_F - 1) as i:
                    for j in range(RING_F):
                        slot(i, j, False)
                for j in range(RING_F):
                    slot(UNITS // RING_F - 1, j, True)

            def project_out(layer):
                n0 = AT_BASE[layer]
                pe.wait_ge(evac, 4 * UNITS * (layer + 1) + 4)
                chunks = ([(b * WT + t, k, QT) for b, t, k in QCH] if layer == 0
                          else [(4 * c, 4, P) for c in range(NC)])
                for n, (t, k, q) in enumerate(chunks):
                    if n >= 2:
                        pe.wait_ge(at_out, n0 + n - 1)
                    for y in range(k):
                        ins = nc.tensor.transpose(bk(n % 2)[:, y * q:(y + 1) * q], A[0:q, t + y, :], ident[0:q, 0:q])
                    ins.then_inc(at_mm, 1)
                pe.wait_ge(at_out, n0 + len(chunks))
                if layer == 0:
                    pe.wait_ge(g0v, 16)
                for c in range(NC):
                    mm(bk(4 + c), w("wo%d" % layer), xch(aT, c)).then_inc(o_mm, 1)

            def ffn(k):
                pe.wait_ge(tw, 5)
                for c in range(NC):
                    pe.wait_ge(xn_ready, NC * (1 + 2 * k) + c + 1)
                    mm(bk(4 + c), tern[:, :], xn(c)).then_inc(f_mm, 1)

            def recurrent():
                pe.wait_ge(xn_ready, NC * 3)
                n = 0
                for d in range(2):
                    p = "fb"[d]
                    for c in range(NC):
                        if d == 0:
                            pe.wait_ge(r_act, c + 1)
                        else:
                            pe.wait_ge(r_act, R_U[0] + c + 1)
                        mm(bk(c), w(p + "_x"), rg[:, 0, 512 * c:512 * c + 512]).then_inc(r_pe, 1)
                    for c in range(NC):
                        pe.wait_ge(r_act, R_U[d] + c + 1)
                        if n >= 2:
                            pe.wait_ge(r_act, R_G[(n - 2) // NC] + 2 * ((n - 2) % NC) + 2)
                        u = rg[:, 1 + d, 512 * c:512 * c + 512]
                        mm(bk(4 + 2 * (n % 2)), w(p + "_gx"), u).then_inc(r_pe, 1)
                        mm(bk(5 + 2 * (n % 2)), w(p + "_ga"), u).then_inc(r_pe, 1)
                        n += 1
                pe.wait_ge(r_dve, R_SCAN)
                for c in range(NC):
                    mm(bk(c), w("f_o"), rg[:, 1, 512 * c:512 * c + 512], stop=False)
                    mm(bk(c), w("b_o"), rg[:, 2, 512 * c:512 * c + 512], start=False).then_inc(r_pe, 1)
                for c in range(NC):
                    pe.wait_ge(r_act, R_GELU2 + c + 1)
                    mm(bk(4 + c), w("ld"), rb[:, 0, 512 * c:512 * c + 512]).then_inc(r_pe, 1)

            def moe(k):
                pe.wait_ge(xn_ready, NC * (6 + 2 * k))
                for t in range(NT):
                    ins = mm(bk(0)[:, t * E:(t + 1) * E], xnt(t), wgs[:, :])
                ins.then_inc(m_pe, 1)
                for c in range(NC):
                    mm(bk(4 + c), w("we"), xn(c)).then_inc(m_pe, 1)
                pe.wait_ge(moe_const, 1)
                pe.wait_ge(m_dve, M_DVE * k + 10)
                mm(bk(1)[:, 0:P], tri[:, :], moh[:, :]).then_inc(m_pe, 1)
                mm(bk(2)[:, 0:P], ones[:, :], moh[:, :]).then_inc(m_pe, 1)
                for c in range(NC):
                    pe.wait_ge(m_dve, M_DVE * k + 17 + c + 1)
                    mm(bk(c), ones[:, :], res[:, c % 2, :]).then_inc(m_pe, 1)

            pe.wait_ge(ln_const, 1)
            for stage in range(nst):
                layernorm(stage)
                if stage == 0:
                    pe.wait_ge(w_loaded, 48)
                    project_qkv(0)
                    ternary()
                    query_zero()
                    windowed_attention()
                    project_out(0)
                if stage in (1, 3):
                    ffn(stage // 2)
                if stage == 2:
                    recurrent()
                if stage == 4 or stage == 6:
                    project_qkv(stage // 2 - 1)
                    full_attention(stage // 2 - 1)
                    project_out(stage // 2 - 1)
                if stage == 5 or stage == 7:
                    moe(stage // 2 - 2)

        @block.scalar
        def _(act):
            def fn(o, i, f, **kw):
                return nc.scalar.activation(o, i, f, **kw)

            def layernorm(k):
                def root(c):
                    act.wait_ge(ln_var, NC * k + c + 1)
                    fn(ln_s[:, 0, 4 * c:4 * c + 4], bk(3)[:, 4 * c:4 * c + 4], ACT.Sqrt,
                       bias=epsc[:, 0:1]).then_inc(ln_std, 1)

                for c in range(NC):
                    act.wait_ge(ln_cent, NC * k + c + 1)
                    fn(xch(sq, c), xch(xc, c), ACT.Square).then_inc(ln_sq, 1)
                    if c > 0:
                        root(c - 1)
                root(NC - 1)

            def project_qkv(layer):
                if layer == 0:
                    act.wait_ge(xn_ready, NC)
                    for b in range(B):
                        act.copy(xwin[:, b, :, P - 1:P],
                                 xp[:, b, HALF:HALF + 1].unsqueeze(1).broadcast_to((P, WT, 1))).then_inc(win_ready, 1)
                def second(n, r, o):
                    act.wait_ge(residue, n + 1)
                    fn(o, r, ACT.Copy).then_inc(part2, 1)

                before = None
                for n, (kind, _, cols, at) in enumerate(chunks(layer), CH_BASE[layer]):
                    src, r, o = chunk_buffers(layer, n, kind, cols, at)
                    act.wait_ge(proj_mm, n + 1)
                    if kind != "v":
                        m = n - CH_BASE[layer] + QK_BASE[layer]
                        if m >= CBUF:
                            act.wait_ge(qk_out[m % CBUF], 16 * (m // CBUF))
                    if layer == 0 and kind == "k":
                        fn(kf[:, at:at + cols], src, ACT.Copy)
                    elif kind == "v":
                        fn(V[:, at:at + cols // P, :, 0:D], src, ACT.Copy)
                    elif layer == 0 and at % QW == 0:
                        fn(q0f[:, at // QW:at // QW + 1], src[:, 0:1], ACT.Copy)
                    fn(o[0], src, ACT.Copy).then_inc(part1, 1)
                    if before:
                        second(*before)
                    before = n, r, o[1]
                second(*before)

            def query_zero():
                act.wait_ge(g0v, 3)
                for b in range(B):
                    for t in range(0, WT, 5):
                        k = min(5, WT - t)
                        n = min(k * QT, S - t * QT)
                        src = bk(3 * b + t // 5)[0:H, 0:n]
                        dst = s0[:, b, t:t + k, HALF:HALF + QT] if n == k * QT else s0[:, b, t, HALF:HALF + n]
                        if n == k * QT:
                            src = src.rearrange("p (t k) -> p t k", k=QT)
                        ins = fn(dst, src, ACT.Exp, bias=s0s[:, b, 1:2], scale=SCALE)
                    ins.then_inc(g0a, 1)

            def split_part(g, rows, cols, j, step):
                o = mp[0:rows, j, step, 0:cols]
                if step == 0:
                    act.wait_ge(mt_ready, g + 1)
                    fn(o, bk(7)[0:rows, 0:cols], ACT.Copy).then_inc(split_act, 1)
                else:
                    act.wait_ge(split_dve, 2 * g + 3)
                    fn(o, mres[0:rows, j % 2, 0:cols], ACT.Copy).then_inc(split_act, 1)

            def windowed_attention():
                act.wait_ge(g0v, 15)
                act.drain().then_inc(exp_done, 1)
                for h in range(2):
                    for step in range(2):
                        split_part(h, B * WT, QT, h, step)

                def unit(i, j, last):
                    u = i * BODY_W + j
                    act.wait_ge(st_ready, u + 1)
                    act.wait_ge(pv_steps, u + 1)
                    fn(pt[:, j % 4, 0:5 * 2 * QT].rearrange("p (g c) -> p g c", g=2), wide[:, 3:5, 0:5 * QT],
                       ACT.Exp, scale=SCALE)
                    fn(pt[:, j % 4, 10 * QT:11 * QT], wide[:, 5, 0:QT], ACT.Exp, scale=SCALE).then_inc(exp_done, 1)
                    if not last or BODY_W - j > 4 - j % B:
                        split_part(i * RING_W + (j // B + 2), B * WT, QT, (j // B + 2) % RING_W, j % B)

                with act.Fori(0, UNITS // BODY_W - 1) as i:
                    for j in range(BODY_W):
                        unit(i, j, False)
                for j in range(BODY_W):
                    unit(UNITS // BODY_W - 1, j, True)

            def full_attention(layer):
                st0, g0 = ST_BASE[layer], G_BASE[layer]
                for step in range(2):
                    split_part(g0, KT, P, 0, step)

                def unit(i, j, last):
                    s = i * RING_F + j
                    for t in range(KT):
                        n = st0 + s * KT + t
                        act.wait_ge(st_ready, n + 1)
                        act.wait_ge(pv_steps, n + 1)
                        fn(pt[:, t % 4, 0:S].rearrange("p (g c) -> p g c", g=2),
                           wide[:, 2 * (t % 2):2 * (t % 2) + 2, :], ACT.Exp, scale=SCALE).then_inc(exp_done, 1)
                        if t in (1, 3) and (not last or j + 1 < RING_F):
                            split_part(g0 + s + 1, KT, P, (j + 1) % RING_F, t // 2)

                with act.Fori(0, UNITS // RING_F - 1) as i:
                    for j in range(RING_F):
                        unit(i, j, False)
                for j in range(RING_F):
                    unit(UNITS // RING_F - 1, j, True)

            def project_out(layer):
                n0 = AT_BASE[layer]
                if layer == 0:
                    for n, (b, t, k) in enumerate(QCH):
                        act.wait_ge(at_mm, n0 + n + 1)
                        c = min(k * QT, S - t * QT)
                        fn(aT[:, b * S + t * QT:b * S + t * QT + c], bk(n % 2)[:, 0:c], ACT.Copy).then_inc(at_out, 1)
                else:
                    for c in range(NC):
                        act.wait_ge(at_mm, n0 + c + 1)
                        fn(xch(aT, c), bk(c % 2), ACT.Copy).then_inc(at_out, 1)

            def recurrent():
                def r(ins):
                    ins.then_inc(r_act, 1)

                for c in range(NC):
                    act.wait_ge(xn_ready, NC * 2 + c + 1)
                    r(fn(rg[:, 0, 512 * c:512 * c + 512], xn(c), ACT.Gelu_apprx_tanh))
                fn(eas[:, 0:1], bcol("f_a"), ACT.Sigmoid).then_inc(ea_ready, 1)
                fn(eas[:, 1:2], bcol("b_a"), ACT.Sigmoid).then_inc(ea_ready, 1)
                for d in range(2):
                    p = "fb"[d]
                    for c in range(NC):
                        act.wait_ge(r_pe, 3 * NC * d + c + 1)
                        r(fn(rg[:, 1 + d, 512 * c:512 * c + 512], bk(c), ACT.Identity, bias=bcol(p + "_bx")))
                    for c in range(NC):
                        k = 2 * ((NC * d + c) % 2)
                        act.wait_ge(r_pe, 3 * NC * d + NC + 2 * c + 2)
                        r(fn(rb[:, 0, 512 * (NC * d + c):512 * (NC * d + c) + 512], bk(4 + k), ACT.Sigmoid, bias=bcol(p + "_bgx")))
                        r(fn(rb[:, 1, 512 * (NC * d + c):512 * (NC * d + c) + 512], bk(5 + k), ACT.Sigmoid, bias=bcol(p + "_bga")))
                for d in range(2):
                    for c in range(NC):
                        at = 512 * (NC * d + c)
                        act.wait_ge(r_dve, 2 * (NC * d + c) + 1)
                        r(fn(rc[:, at:at + 512], rb[:, 1, at:at + 512], ACT.Square))
                        act.wait_ge(r_act, R_SQ + 2 * (NC * d + c) + 1)
                        r(fn(rc[:, at:at + 512], rc[:, at:at + 512], ACT.Sqrt, scale=-1.0, bias=ones[:, 0:1]))
                for c in range(NC):
                    act.wait_ge(r_pe, 6 * NC + c + 1)
                    act.wait_ge(r_dve, R_HB)
                    r(fn(rg[:, 0, 512 * c:512 * c + 512], bk(c), ACT.Identity, scale=0.5, bias=eas[:, 3:4]))
                for c in range(NC):
                    act.wait_ge(r_dve, R_HB + c + 1)
                    r(fn(rb[:, 0, 512 * c:512 * c + 512], rg[:, 0, 512 * c:512 * c + 512], ACT.Gelu_apprx_tanh))

            def moe(k):
                act.wait_ge(m_dve, M_DVE * k + 2)
                fn(me[:, :, :], me[:, :, :], ACT.Exp).then_inc(m_act, 1)
                for c in range(NC):
                    act.wait_ge(m_pe, M_PE * k + 7 + c + 1)
                    fn(xch(mgb, c), bk(c), ACT.Copy).then_inc(m_act, 1)

            act.wait_ge(ln_const, 1)
            for stage in range(nst):
                layernorm(stage)
                if stage == 0:
                    project_qkv(0)
                    query_zero()
                    windowed_attention()
                    project_out(0)
                if stage == 2:
                    recurrent()
                if stage == 4 or stage == 6:
                    project_qkv(stage // 2 - 1)
                    full_attention(stage // 2 - 1)
                    project_out(stage // 2 - 1)
                if stage == 5 or stage == 7:
                    moe(stage // 2 - 2)

        @block.vector
        def _(dve):
            def tt(o, a, b, op):
                return nc.vector.tensor_tensor(o, a, b, op)

            def spread(y, column):
                return tt(diag[:, y, :, :], ident[:, :].unsqueeze(1).broadcast_to((P, 4, P)),
                          column.unsqueeze(2).broadcast_to((P, 4, P)), ALU.mult)

            def layernorm(k):
                def centre(c):
                    dve.wait_ge(ln_mean, NC * k + c + 1)
                    tt(xch(xc, c), xch(x, c), bk(LN_MEAN[c]), ALU.subtract).then_inc(ln_cent, 1)

                def rstd(c):
                    dve.wait_ge(ln_std, NC * k + c + 1)
                    r = ln_s[:, 1, 4 * c:4 * c + 4]
                    nc.vector.reciprocal(r, ln_s[:, 0, 4 * c:4 * c + 4]).then_inc(ln_rstd, 1)
                    dve.wait_ge(ln_rstd, NC * k + c + 1)
                    if c >= 2:
                        dve.wait_ge(ln_b, NC * k + c - 1)
                    spread(c % 2, r).then_inc(ln_diag, 1)

                def normalise(c):
                    dve.wait_ge(ln_b, NC * k + c + 1)
                    tt(xn(c), xch(xc, c), bk(LN_STD[c]), ALU.mult).then_inc(xn_ready, 1)

                for step, c in ((centre, 0), (centre, 1), (centre, 2), (rstd, 0), (centre, 3), (rstd, 1),
                                (normalise, 0), (rstd, 2), (normalise, 1), (rstd, 3), (normalise, 2), (normalise, 3)):
                    step(c)

            def ternary():
                nc.vector.tensor_reduce(ts_[:, 0:1], w("tern"), AX.X, ALU.add,
                                        apply_absolute_value=True).then_inc(tw, 1)
                dve.wait_ge(tw_sum, 1)
                nc.vector.tensor_scalar(ts_[:, 1:2], bk(6)[:, 0:1], 1.0 / (P * P), 0.7,
                                        ALU.mult, ALU.mult).then_inc(tw, 1)
                dve.wait_ge(tw, 2)
                nc.vector.tensor_scalar(ts_[:, 2:3], ts_[:, 1:2], -1.0, None, ALU.mult).then_inc(tw, 1)
                dve.wait_ge(tw, 3)
                nc.vector.tensor_scalar(tg[:, 0, :], w("tern"), ts_[:, 1:2], bcol("alpha"), ALU.is_gt, ALU.mult)
                nc.vector.tensor_scalar(tg[:, 1, :], w("tern"), ts_[:, 2:3], bcol("alpha"), ALU.is_lt,
                                        ALU.mult).then_inc(tw, 1)
                dve.wait_ge(tw, 4)
                tt(tern[:, :], tg[:, 0, :], tg[:, 1, :], ALU.subtract).then_inc(tw, 1)

            def project_qkv(layer):
                if layer == 0:
                    for b in range(B):
                        dve.wait_ge(xn_ready, NC)
                        for t in range(WT):
                            ins = nc.vector.tensor_copy(xwin[:, b, t, 0:P - 1], xp[:, b, QT * t:QT * t + P - 1])
                    ins.then_inc(win_ready, 1)
                def third(n, r, o):
                    dve.wait_ge(part2, n + 1)
                    tt(o[2], r, o[1], ALU.subtract).then_inc(part3, 1)

                before = None
                for n, (kind, _, cols, at) in enumerate(chunks(layer), CH_BASE[layer]):
                    src, r, o = chunk_buffers(layer, n, kind, cols, at)
                    dve.wait_ge(part1, n + 1)
                    if n >= CBUF:
                        dve.wait_ge(part3, n - CBUF + 1)
                    tt(r, src, o[0], ALU.subtract).then_inc(residue, 1)
                    if before:
                        third(*before)
                    before = n, r, o
                third(*before)

            def query_zero():
                dve.wait_ge(part1, CH_BASE[1])
                dve.wait_ge(q0_const, 1)
                for b in range(B):
                    ins = nc.vector.tensor_scalar(q0m[:, b, :], hmask[:, :], q0f[:, b:b + 1], None, ALU.mult)
                ins.then_inc(g0v, 1)
                for b in range(B):
                    dve.wait_ge(g0, b + 1)
                    for t in range(0, WT, 5):
                        c = min(5 * QT, S - t * QT)
                        ins = nc.vector.tensor_reduce(q0x[:, b, t // 5:t // 5 + 1],
                                                      bk(3 * b + t // 5)[0:H, 0:c], AX.X, ALU.max)
                    ins.then_inc(q0_max, 1)
                    dve.wait_ge(q0_max, 1 + 2 * b)
                    nc.vector.tensor_reduce(s0s[:, b, 0:1], q0x[:, b, :], AX.X, ALU.max).then_inc(q0_max, 1)
                    dve.wait_ge(q0_max, 2 + 2 * b)
                    nc.vector.tensor_scalar(s0s[:, b, 1:2], s0s[:, b, 0:1], -SCALE, None, ALU.mult).then_inc(g0v, 1)
                dve.wait_ge(g0, 3)
                nc.vector.tensor_copy(s0t[:, :, :, :].rearrange("p b t h -> p (b t h)"),
                                      bk(6)[:, 0:B * WT * H]).then_inc(g0v, 1)
                dve.wait_ge(g0, 4)
                k = 4
                for b in range(B):
                    tt(o0[:, b, :, :], bk(7)[0:H, 160 * b:160 * b + H * (D + 1)].rearrange("p (h d) -> p h d", h=H),
                       hmaskT[:, :, :], ALU.mult).then_inc(g0v, 1)
                    dve.wait_ge(g0v, k + 1)
                    nc.vector.tensor_reduce(o0s[:, b, :], o0[:, b, :, :].rearrange("p h d -> p d h"), AX.X,
                                            ALU.add).then_inc(g0v, 1)
                    dve.wait_ge(g0v, k + 2)
                    nc.vector.reciprocal(s0s[:, b, 2:3], o0s[:, b, D:D + 1]).then_inc(g0v, 1)
                    dve.wait_ge(g0v, k + 3)
                    nc.vector.tensor_scalar(o0s[:, b, 0:D], o0s[:, b, 0:D], s0s[:, b, 2:3], None,
                                            ALU.mult).then_inc(g0v, 1)
                    dve.wait_ge(g0v, k + 4)
                    tt(z0[:, b, :, :], hmaskT[:, :, 0:D], o0s[:, b, 0:D].unsqueeze(1).broadcast_to((H, H, D)),
                       ALU.mult).then_inc(g0v, 1)
                    k += 5
                dve.wait_ge(g0, 5)
                nc.vector.tensor_copy(q0o[:, :], bk(6)[:, 400:400 + B]).then_inc(g0v, 1)

            def split_maximum(g, rows, cols, j, step):
                src, o, r = bk(7)[0:rows, 0:cols], mp[0:rows, j, :, 0:cols], mres[0:rows, j % 2, 0:cols]
                if step == 0:
                    dve.wait_ge(split_act, 2 * g + 1)
                    tt(r, src, o[:, 0, :], ALU.subtract).then_inc(split_dve, 1)
                else:
                    dve.wait_ge(split_act, 2 * g + 2)
                    tt(o[:, 2, :], r, o[:, 1, :], ALU.subtract).then_inc(split_dve, 1)

            def remainder(slot, a, b):
                tt(lo[:, slot, a:b], pt[:, slot, a:b], pth[:, slot, a:b], ALU.subtract).then_inc(lo_dve, 1)

            def divide(g, q, tiles, direct, t0, h, eps, y, step):
                n, d = num[0:q, y, 0:tiles, :], den[0:q, y, 0:tiles]
                src = bk(6)[0:q, 0:tiles * VC].rearrange("p (t n d) -> p t d n", t=tiles, d=D + 1)
                if step == 0:
                    if direct:
                        nc.vector.tensor_copy(n[:, 0:direct, :], src[:, 0:direct, :, 0])
                    nc.vector.tensor_reduce(n[:, direct:tiles, :], src[:, direct:tiles, :, :], AX.X,
                                            ALU.add).then_inc(evac, 1)
                elif step == 1:
                    dve.wait_ge(evac, 4 * g + 5)
                    nc.vector.tensor_scalar(d, n[:, :, D], eps, None, ALU.add).then_inc(evac, 1)
                elif step == 2:
                    dve.wait_ge(evac, 4 * g + 6)
                    nc.vector.reciprocal(rden[0:q, y, 0:tiles], d).then_inc(evac, 1)
                else:
                    dve.wait_ge(evac, 4 * g + 7)
                    tt(A[0:q, t0:t0 + tiles, bass.ds(h * D, D)], n[:, :, 0:D],
                       rden[0:q, y, 0:tiles].unsqueeze(2).broadcast_to((q, tiles, D)), ALU.mult).then_inc(evac, 1)

            def windowed_attention():
                dve.wait_ge(g0v, 15)
                dve.drain().then_inc(sm_read, 1)
                dve.drain().then_inc(split_dve, 2)
                dve.drain().then_inc(evac, 4)

                def maxima(u, j, bank=0):
                    dve.wait_ge(sm_ready, u + 1)
                    b = j % B
                    nc.vector.tensor_reduce(nm[0:QT, j // B, b * WT:(b + 1) * WT],
                                            wide[0:QT, bank:bank + 3, :].rearrange("p g (t k) -> p (g t) k", k=P)[:, 0:WT, :],
                                            AX.X, ALU.max, negate=True).then_inc(sm_read, 1)

                for u in range(LEAD):
                    maxima(u, u, 3 * (u % 2))
                    if u == 2:
                        for step in range(2):
                            split_maximum(0, B * WT, QT, 0, step)
                for step in range(2):
                    split_maximum(1, B * WT, QT, 1, step)

                def unit(i, j, last=False):
                    u = i * BODY_W + j
                    left = BODY_W - j if last else UNITS

                    def quotients(d, step):
                        k = j - d
                        if step == 0:
                            dve.wait_ge(pv_steps, u - d + 5)
                        divide(u - d, QT, WT, 0, k % B * WT, i * RING_W + k // B, 0.0, k % 2, step)

                    if j > 0:
                        quotients(1, 0)
                    if left > 4 - j % B:
                        split_maximum(i * RING_W + (j // B + 2), B * WT, QT, (j // B + 2) % RING_W, j % B)
                    if j > 0:
                        quotients(1, 1)
                    if left > LEAD:
                        maxima(u + LEAD, (j + LEAD) % BODY_W)
                    if j > 0:
                        quotients(1, 2)
                        quotients(1, 3)
                    if last and left == 1:
                        for step in range(4):
                            quotients(0, step)

                unit(0, 0)
                with dve.Fori(0, UNITS // BODY_W - 1) as i:
                    for j in range(1, BODY_W + 1):
                        unit(i, j)
                for j in range(1, BODY_W):
                    unit(UNITS // BODY_W - 1, j, True)

            def full_attention(layer):
                u0, st0, sm0 = layer * UNITS, ST_BASE[layer], SM_BASE[layer]
                use0 = (layer - 1) * (UNITS // RING_F)
                eps = DEN_EPS if layer == 1 else 0.0

                def maximum(u, j, t, y):
                    dve.wait_ge(sm_ready, sm0 + (u * KT + t) * 2 + y + 1)
                    nc.vector.tensor_reduce(mx[:, j % 2, t, y:y + 1], bk(4 + y), AX.X, ALU.max).then_inc(sm_read, 1)

                def collect(u, j):
                    dve.wait_ge(sm_read, sm0 + (u + 1) * KT * 2 + 1)
                    nc.vector.tensor_reduce(nm[:, j, 0:KT], mx[:, j % 2, :, :], AX.X, ALU.max,
                                            negate=True).then_inc(nm_ready, 1)

                for u in range(2):
                    for t in range(KT):
                        for y in range(2):
                            maximum(u, u, t, y)
                        if u == 1 and t >= KT // 2 and t < KT // 2 + 2:
                            split_maximum(G_BASE[layer], KT, P, 0, t - KT // 2)
                    if u == 0:
                        collect(0, 0)

                def slot(i, j, last=False):
                    s = i * RING_F + j
                    nxt = not last or j + 1 < RING_F
                    smx = not last or j + 2 < RING_F

                    def quotients(d, step):
                        k = j - d
                        if step == 0:
                            dve.wait_ge(pv_steps, st0 + (s - d + 1) * KT + 4)
                        divide(u0 + s - d, P, KT, DIRECT, (k % B) * KT, i * (RING_F // B) + k // B, eps, k % 2, step)

                    def divide_before(step):
                        if j > 0:
                            quotients(1, step)

                    def split_next(step):
                        if nxt:
                            split_maximum(G_BASE[layer] + s + 1, KT, P, (j + 1) % RING_F, step)

                    def collect_next():
                        if nxt:
                            collect(s + 1, (j + 1) % RING_F)

                    between = {(0, 0): (collect_next, lambda: divide_before(0)), (0, 1): (lambda: divide_before(1),),
                               (1, 0): (lambda: divide_before(2),), (1, 1): (lambda: divide_before(3),),
                               (1, 2): (lambda: split_next(0),), (3, 0): (lambda: split_next(1),)}
                    for t in range(KT):
                        dve.wait_ge(exp_done, st0 + s * KT + t + 2)
                        remainder(t % 4, LO_F, S)
                        for k in range(3):
                            if k and smx:
                                maximum(s + 2, j % RING_F, t, k - 1)
                            for step in between.get((t, k), ()):
                                step()
                    if last and not nxt:
                        for step in range(4):
                            quotients(0, step)

                slot(0, 0)
                with dve.Fori(0, UNITS // RING_F - 1) as i:
                    for j in range(1, RING_F + 1):
                        slot(i, j)
                for j in range(1, RING_F):
                    slot(UNITS // RING_F - 1, j, True)

            def add_projection(layer, stage):
                if layer == 0:
                    dve.wait_ge(at_out, AT_BASE[1])
                    nc.vector.tensor_copy(aT[:, 0:N].rearrange("p (b s) -> p b s", b=B)[:, :, 0:1],
                                          q0o[:, :].unsqueeze(2)).then_inc(g0v, 1)
                for c in range(NC):
                    dve.wait_ge(o_mm, NC * layer + c + 1)
                    if layer == 1:
                        nc.vector.scalar_tensor_tensor(xch(x, c), bk(4 + c), bcol("bo"), xch(x, c), ALU.add,
                                                       ALU.add).then_inc(x_new, 1)
                    else:
                        tt(xch(x, c), bk(4 + c), xch(x, c), ALU.add).then_inc(x_new, 1)

            def ffn(k):
                for c in range(NC):
                    dve.wait_ge(f_mm, NC * k + c + 1)
                    nc.vector.scalar_tensor_tensor(xch(x, c), bk(4 + c), bcol("ffn_b"), xch(x, c), ALU.add,
                                                   ALU.add).then_inc(x_new, 1)

            def recurrent():
                n = [0]

                def r(ins):
                    n[0] += 1
                    ins.then_inc(r_dve, 1)

                dve.wait_ge(ea_ready, 2)
                for d in range(2):
                    for c in range(NC):
                        at = 512 * (NC * d + c)
                        dve.wait_ge(r_act, R_G[d] + 2 * c + 2)
                        a = rb[:, 1, at:at + 512]
                        r(nc.vector.tensor_scalar(a, a, eas[:, d:d + 1], None, ALU.mult))
                        g = rb[:, 0, at:at + 512]
                        r(tt(g, g, rg[:, 1 + d, 512 * c:512 * c + 512], ALU.mult))
                for d in range(2):
                    for c in range(NC):
                        at = 512 * (NC * d + c)
                        dve.wait_ge(r_act, R_SQ + 2 * (NC * d + c) + 2)
                        dve.wait_ge(r_dve, 2 * (NC * d + c) + 2)
                        g = rb[:, 0, at:at + 512]
                        r(tt(g, g, rc[:, at:at + 512], ALU.mult))
                for d in range(2):
                    for b in range(B):
                        at = N * d + S * b
                        dve.wait_ge(r_dve, 2 * 2 * NC + 2 * NC)
                        a, g, h = rb[:, 1, at:at + S], rb[:, 0, at:at + S], rg[:, 1 + d, S * b:S * b + S]
                        if d:
                            a, g, h = a[:, ::-1], g[:, ::-1], h[:, ::-1]
                        r(nc.vector.tensor_tensor_scan(h, a, g, 0.0, ALU.mult, ALU.add))
                assert n[0] == R_SCAN, n[0]
                r(tt(eas[:, 2:3], bcol("f_bo"), bcol("b_bo"), ALU.add))
                dve.wait_ge(r_dve, n[0])
                r(nc.vector.tensor_scalar(eas[:, 3:4], eas[:, 2:3], 0.5, None, ALU.mult))
                assert n[0] == R_HB
                for c in range(NC):
                    dve.wait_ge(r_act, R_OUT + c + 1)
                    y = rg[:, 0, 512 * c:512 * c + 512]
                    r(tt(y, y, xn(c), ALU.add))
                for c in range(NC):
                    dve.wait_ge(r_pe, 7 * NC + c + 1)
                    y = rb[:, 1, 512 * c:512 * c + 512]
                    r(nc.vector.scalar_tensor_tensor(y, bk(4 + c), bcol("ld_b"), xn(c), ALU.add, ALU.add))
                    dve.wait_ge(r_dve, n[0])
                    tt(xch(x, c), y, xch(x, c), ALU.add).then_inc(x_new, 1)

            def moe(k):
                n = [0]

                def m(ins):
                    n[0] += 1
                    ins.then_inc(m_dve, 1)
                    dve.wait_ge(m_dve, M_DVE * k + n[0])

                logits = bk(0)[:, 0:NT * E].rearrange("p (t e) -> p t e", e=E)

                def wide8(t):
                    return t.unsqueeze(2).broadcast_to((P, NT, E))

                dve.wait_ge(moe_const, 1)
                dve.wait_ge(m_pe, M_PE * k + 1)
                m(nc.vector.tensor_reduce(mst[:, 0, :], logits, AX.X, ALU.max))
                m(tt(me[:, :, :], logits, wide8(mst[:, 0, :]), ALU.subtract))
                dve.wait_ge(m_act, M_ACT * k + 1)
                m(nc.vector.tensor_reduce(mst[:, 1, :], me[:, :, :], AX.X, ALU.add))
                m(nc.vector.reciprocal(mst[:, 2, :], mst[:, 1, :]))
                m(tt(me[:, :, :], me[:, :, :], wide8(mst[:, 2, :]), ALU.mult))
                m(nc.vector.tensor_reduce(mst[:, 3, :], me[:, :, :], AX.X, ALU.max))
                m(tt(mw[:, :, :], me[:, :, :], wide8(mst[:, 3, :]), ALU.is_equal))
                m(tt(mw[:, :, :], mw[:, :, :], rank[:, :, :], ALU.mult))
                m(nc.vector.tensor_reduce(mst[:, 4, :], mw[:, :, :], AX.X, ALU.max))
                onehot = moh[:, :].rearrange("p (t e) -> p t e", e=E)
                m(tt(onehot, mw[:, :, :], wide8(mst[:, 4, :]), ALU.is_equal))
                dve.wait_ge(m_pe, M_PE * k + 7)
                m(nc.vector.tensor_copy(mt1[:, :, :], bk(2)[:, 0:P].rearrange("p (t e) -> p e t", e=E)))
                m(nc.vector.tensor_tensor_scan(mt2[:, :, :].rearrange("p e t -> p (e t)"),
                                               keep[:, :, :].rearrange("p e t -> p (e t)"),
                                               mt1[:, :, :].rearrange("p e t -> p (e t)"), 0.0, ALU.mult, ALU.add))
                m(tt(mt2[:, :, :], mt2[:, :, :], mt1[:, :, :], ALU.subtract))
                m(tt(mloc[:, :, :], bk(1)[:, 0:P].rearrange("p (t e) -> p t e", e=E),
                     mt2[:, :, :].rearrange("p e t -> p t e"), ALU.add))
                m(nc.vector.scalar_tensor_tensor(mloc[:, :, :], mloc[:, :, :], float(CAP), onehot, ALU.is_le, ALU.mult))
                m(nc.vector.tensor_reduce(mst[:, 5, :], mloc[:, :, :], AX.X, ALU.add))
                m(tt(mgate[:, :], mst[:, 5, :], mst[:, 3, :], ALU.mult))
                for c in range(NC):
                    if c >= 2:
                        dve.wait_ge(m_pe, M_PE * k + 7 + c - 1)
                    m(spread(c % 2, mgate[:, 4 * c:4 * c + 4]))
                assert n[0] == M_DVE, n[0]
                for c in range(NC):
                    dve.wait_ge(m_act, M_ACT * k + 2 + c)
                    y = xch(xc, c)
                    nc.vector.scalar_tensor_tensor(y, bk(4 + c), bcol("be"), xch(mgb, c), ALU.add,
                                                   ALU.mult).then_inc(m_y, 1)
                    dve.wait_ge(m_y, NC * k + c + 1)
                    tt(xch(x, c), y, xch(x, c), ALU.add).then_inc(x_new, 1)

            dve.wait_ge(ln_const, 1)
            for stage in range(nst):
                layernorm(stage)
                if stage == 0:
                    dve.wait_ge(w_loaded, 48)
                    project_qkv(0)
                    ternary()
                    query_zero()
                    windowed_attention()
                    add_projection(0, 0)
                if stage in (1, 3):
                    ffn(stage // 2)
                if stage == 2:
                    recurrent()
                if stage == 4 or stage == 6:
                    full = stage // 2 - 1
                    project_qkv(full)
                    full_attention(full)
                    add_projection(full, stage)
                if stage == 5 or stage == 7:
                    moe(stage // 2 - 2)


def kernel(**inputs):
    import concourse.bacc as bacc
    from concourse.bass_utils import run_bass_kernel_spmd

    a = {k: np.asarray(v) for k, v in inputs.items()}

    def rows(name):
        return a[name].transpose(1, 0, 2).reshape(P, P)

    rec = {f"{p}_{n}": a[f"L0_attn_b_{q}_W{m}"] for p, q in (("f", "fwd"), ("b", "bwd"))
           for n, m in (("x", "x"), ("gx", "gx"), ("ga", "ga"), ("o", "o"))}
    ws = {"wq0": a["L0_attn_a_Wq"].T, "wk0": a["L0_attn_a_Wk"].T, "wv0": a["L0_attn_a_Wv"].T,
          "wo0": a["L0_attn_a_Wo"].T, "ld": a["L0_attn_b_ld_W"], "tern": a["L0_ffn_weight"].T,
          "wq1": a["L1_attn_a_Wq"].T, "wk1": a["L1_attn_a_Wk"].T, "wv1": a["L1_attn_a_Wv"].T,
          "wo1": a["L1_attn_a_Wo"].T, "wq2": rows("L1_attn_b_W_query"), "wk2": rows("L1_attn_b_W_key"),
          "wv2": rows("L1_attn_b_W_val"), "wo2": a["L1_attn_b_W_out"].reshape(P, P), "we": a["L1_ffn_We"], **rec}
    bs = {f"{p}_{n}": a[f"L0_attn_b_{q}_{m}"] for p, q in (("f", "fwd"), ("b", "bwd"))
          for n, m in (("a", "a_logit"), ("bx", "bx"), ("bgx", "bgx"), ("bga", "bga"), ("bo", "bo"))}
    bs.update(ld_b=a["L0_attn_b_ld_b"], ffn_b=a["L0_ffn_bias"], bo=a["L1_attn_a_bo"], be=a["L1_ffn_be"],
              alpha=np.repeat(a["L0_ffn_alpha"], P))
    arrays = {
        "xT": np.ascontiguousarray(a["L0_attn_a_x"].reshape(N, P).T),
        "weights": np.ascontiguousarray(np.stack([ws[n] for n in W_NAMES], 1)),
        "biases": np.ascontiguousarray(np.stack([bs[n] for n in B_NAMES], 1)),
        "wg": np.ascontiguousarray(a["L1_ffn_Wg"]),
    }
    nc = bacc.Bacc("TRN2", target_bir_lowering=False, num_devices=1)
    aps = [nc.dram_tensor(n, v.shape, F32, kind="ExternalInput").ap() for n, v in arrays.items()]
    out = nc.dram_tensor("outT", (P, N), F32, kind="ExternalOutput").ap()
    build(nc, *aps, out)
    r = run_bass_kernel_spmd(nc, [arrays], core_ids=[0])
    return np.ascontiguousarray(r.results[0]["outT"].T).reshape(B, S, P)
```
